# Optimizing a Trainium2 kernel written in Bass

```python
import numpy as np
import jax
import jax.numpy as jnp

def _softmax(x, axis=-1):
    return jax.nn.softmax(x, axis=axis)

def _gelu(x):
    return jax.nn.gelu(x, approximate=True)

def _silu(x):
    return jax.nn.silu(x)

def _sigmoid(x):
    return jax.nn.sigmoid(x)

def _layernorm(x, axis=-1, eps=1e-05):
    m = jnp.mean(x, axis=axis, keepdims=True)
    v = jnp.var(x, axis=axis, keepdims=True)
    return (x - m) / jnp.sqrt(v + eps)

def _scatter_add(tgt, idx, src, axis=0):
    return tgt.at[idx].add(src)

def _segment_sum(src, seg, n):
    return jax.ops.segment_sum(src, seg, n)
kernel_name = 'mk_decoder_postln_d1_seqx_r8_2e690f'

def setup_inputs(seed: int=0):
    np.random.seed(seed)
    _w = jnp.asarray

    def _rec_inputs():
        import jax
        import jax.numpy as jnp
        _rk = jax.random.key(seed)
        x = -0.0005207 + 1.001 * jax.random.normal(jax.random.fold_in(_rk, 1), (16, 64, 512), jnp.float32)
        _lenS = 64 - jax.random.randint(jax.random.fold_in(_rk, 7), (16,), 0, max(1, 64 // 4) + 1, jnp.int32)
        _lenS2 = 64 - jax.random.randint(jax.random.fold_in(_rk, 8), (16,), 0, max(1, 64 // 4) + 1, jnp.int32)
        _ctx_4096P = jax.random.normal(jax.random.fold_in(_rk, 11), (16, 16, 512), jnp.float32)
        _ctx_4096c = jax.random.dirichlet(jax.random.fold_in(_rk, 511), 0.3 * jnp.ones((16,), jnp.float32), (16, 64))
        _ctx_4096t = jnp.einsum('bsk,bkd->bsd', _ctx_4096c, _ctx_4096P)
        _ctx_4096t = _ctx_4096t * jax.lax.rsqrt(jnp.mean(jnp.square(_ctx_4096t)) + 1e-12) * 0.953939
        ctx_4096 = -0.00010331 + 0.999899 * (_ctx_4096t + 0.3 * jax.random.normal(jax.random.fold_in(_rk, 611), (16, 64, 512), jnp.float32))
        return (x, ctx_4096)
    x, ctx_4096 = _rec_inputs()

    def _L0_attn_setup():
        import jax, jax.numpy as jnp
        import numpy as np
        import math
        FACTOR = 1
        key = jax.random.key(seed)
        x = jax.random.normal(key, (8, 64, 512), dtype=jnp.float32)
        return {'x': x}
    _L0_attn_all = _L0_attn_setup()
    _L0_attn_in = {k: v for k, v in _L0_attn_all.items() if k in ()}
    del _L0_attn_all

    def _L0_xattn_setup():
        import jax, jax.numpy as jnp
        import numpy as np
        B, Q, D = (8, 64, 512)
        CTX = 512
        H, KV, HD = (16, 4, 96)
        G = H // KV
        key = jax.random.key(seed)
        ks = jax.random.split(key, 6)
        s = 0.02
        return {'latents': jax.random.normal(ks[0], (B, Q, D), jnp.float32), 'context': jax.random.normal(ks[1], (B, CTX, D), jnp.float32), 'Wq': jax.random.normal(ks[2], (H * HD, D), jnp.float32) * s, 'Wk': jax.random.normal(ks[3], (KV * HD, D), jnp.float32) * s, 'Wv': jax.random.normal(ks[4], (KV * HD, D), jnp.float32) * s, 'Wo': jax.random.normal(ks[5], (D, H * HD), jnp.float32) * s}
    _L0_xattn_all = _L0_xattn_setup()
    _L0_xattn_in = {k: v for k, v in _L0_xattn_all.items() if k in ('Wq', 'Wk', 'Wv', 'Wo')}
    del _L0_xattn_all

    def _L0_ffn_setup():
        import jax, jax.numpy as jnp
        import numpy as np
        LORA_SCALING = 1.0 / 2.0

        def _qlora_linear(x, wq, A, B):
            w = jnp.tile(wq, (1, 4))
            base = x @ w.T
            lora = x @ A.T @ B.T
            return base + lora * LORA_SCALING
        key = jax.random.key(seed)
        ks = jax.random.split(key, 10)
        d, h, r = (512, 1376, 2)
        return {'x': jax.random.normal(ks[0], (16, 1, d), dtype=jnp.float32), 'w1q': jax.random.normal(ks[1], (h, d // 4), dtype=jnp.float32) * 0.02, 'a1': jax.random.normal(ks[2], (r, d), dtype=jnp.float32) * 0.02, 'b1': jax.random.normal(ks[3], (h, r), dtype=jnp.float32) * 0.02, 'w3q': jax.random.normal(ks[4], (h, d // 4), dtype=jnp.float32) * 0.02, 'a3': jax.random.normal(ks[5], (r, d), dtype=jnp.float32) * 0.02, 'b3': jax.random.normal(ks[6], (h, r), dtype=jnp.float32) * 0.02, 'w2q': jax.random.normal(ks[7], (d, h // 4), dtype=jnp.float32) * 0.02, 'a2': jax.random.normal(ks[8], (r, h), dtype=jnp.float32) * 0.02, 'b2': jax.random.normal(ks[9], (d, r), dtype=jnp.float32) * 0.02}
    _L0_ffn_all = _L0_ffn_setup()
    _L0_ffn_in = {k: v for k, v in _L0_ffn_all.items() if k in ('w1q', 'a1', 'b1', 'w3q', 'a3', 'b3', 'w2q', 'a2', 'b2')}
    del _L0_ffn_all
    return {'x': x, 'ctx_4096': ctx_4096, 'L0_xattn_Wq': _L0_xattn_in['Wq'], 'L0_xattn_Wk': _L0_xattn_in['Wk'], 'L0_xattn_Wv': _L0_xattn_in['Wv'], 'L0_xattn_Wo': _L0_xattn_in['Wo'], 'L0_ffn_w1q': _L0_ffn_in['w1q'], 'L0_ffn_a1': _L0_ffn_in['a1'], 'L0_ffn_b1': _L0_ffn_in['b1'], 'L0_ffn_w3q': _L0_ffn_in['w3q'], 'L0_ffn_a3': _L0_ffn_in['a3'], 'L0_ffn_b3': _L0_ffn_in['b3'], 'L0_ffn_w2q': _L0_ffn_in['w2q'], 'L0_ffn_a2': _L0_ffn_in['a2'], 'L0_ffn_b2': _L0_ffn_in['b2']}

def reference(x, ctx_4096, L0_xattn_Wq, L0_xattn_Wk, L0_xattn_Wv, L0_xattn_Wo, L0_ffn_w1q, L0_ffn_a1, L0_ffn_b1, L0_ffn_w3q, L0_ffn_a3, L0_ffn_b3, L0_ffn_w2q, L0_ffn_a2, L0_ffn_b2):
    import jax
    import jax.numpy as jnp

    def _L0_attn_ref(x):
        import jax, jax.numpy as jnp
        import numpy as np
        import math
        FACTOR = 1
        B, C, L = x.shape
        xh = x[:, None]
        f = jnp.fft.rfft(xh, axis=-1)
        corr = jnp.fft.irfft(f * jnp.conj(f), n=L, axis=-1)
        top_k = int(FACTOR * math.log(L))
        weights, delay = jax.lax.top_k(corr, top_k)
        tmp_corr = jax.nn.softmax(weights, axis=-1)
        init_index = jnp.arange(L)
        idx = (init_index[None, None, None, None, :] + delay[..., None]) % L
        pattern = jnp.take_along_axis(xh[:, :, :, None, :], idx, axis=-1)
        delays_agg = jnp.sum(pattern * tmp_corr[..., None], axis=-2)
        return delays_agg[:, 0]

    def _L0_xattn_ref(latents, context, Wq, Wk, Wv, Wo):
        import jax, jax.numpy as jnp
        import numpy as np
        B, Q, D = (8, 64, 512)
        CTX = 512
        H, KV, HD = (16, 4, 96)
        G = H // KV
        b, q_len, _ = latents.shape
        hidden = jnp.concatenate([context, latents], axis=1)
        s_len = hidden.shape[1]
        q = (latents @ Wq.T).reshape(b, q_len, H, HD)
        k = (hidden @ Wk.T).reshape(b, s_len, KV, HD)
        v = (hidden @ Wv.T).reshape(b, s_len, KV, HD)
        q = q.transpose(0, 2, 1, 3).reshape(b, KV, G, q_len, HD)
        k = k.transpose(0, 2, 1, 3)
        v = v.transpose(0, 2, 1, 3)
        scale = 1.0 / jnp.sqrt(jnp.asarray(HD, q.dtype))
        scores = jnp.einsum('bkgqd,bksd->bkgqs', q, k) * scale
        attn = jax.nn.softmax(scores.astype(jnp.float32), axis=-1).astype(q.dtype)
        out = jnp.einsum('bkgqs,bksd->bkgqd', attn, v)
        out = out.reshape(b, H, q_len, HD).transpose(0, 2, 1, 3).reshape(b, q_len, H * HD)
        return out @ Wo.T

    def _L0_ffn_ref(x, w1q, a1, b1, w3q, a3, b3, w2q, a2, b2):
        import jax, jax.numpy as jnp
        import numpy as np
        LORA_SCALING = 1.0 / 2.0

        def _qlora_linear(x, wq, A, B):
            w = jnp.tile(wq, (1, 4))
            base = x @ w.T
            lora = x @ A.T @ B.T
            return base + lora * LORA_SCALING
        gate = jax.nn.silu(_qlora_linear(x, w1q, a1, b1))
        up = _qlora_linear(x, w3q, a3, b3)
        return _qlora_linear(gate * up, w2q, a2, b2)
    x = _layernorm(x + _L0_attn_ref(x), axis=-1)
    x = _layernorm(x + _L0_xattn_ref(x, ctx_4096, L0_xattn_Wq, L0_xattn_Wk, L0_xattn_Wv, L0_xattn_Wo), axis=-1)
    x = _layernorm(x + _L0_ffn_ref(x, L0_ffn_w1q, L0_ffn_a1, L0_ffn_b1, L0_ffn_w3q, L0_ffn_a3, L0_ffn_b3, L0_ffn_w2q, L0_ffn_a2, L0_ffn_b2), axis=-1)
    return x

_drawn_inputs = setup_inputs


def setup_inputs(seed=0):
    import zlib

    import numpy as np

    out = dict(_drawn_inputs(seed))
    spreads = {}
    factors = {'L0_xattn_Wq': 5.47,
     'L0_xattn_Wk': 5.46,
     'L0_ffn_a1': 8.0,
     'L0_ffn_b1': 8.0,
     'L0_ffn_a3': 8.0,
     'L0_ffn_b3': 8.0,
     'L0_ffn_a2': 8.0,
     'L0_ffn_b2': 8.0}
    for name, (base, spread) in spreads.items():
        noise = np.random.default_rng([zlib.crc32(name.encode()), seed]).standard_normal(out[name].shape)
        drawn = base * np.exp(spread * noise) if base else spread * noise
        out[name] = jnp.asarray(drawn.astype(out[name].dtype))
    for name, factor in factors.items():
        out[name] = (out[name] * factor).astype(out[name].dtype)
    return out
```

```python
from contextlib import ExitStack

import numpy as np

import concourse.bass as bass
from concourse import mybir

F32 = mybir.dt.float32
F32R = mybir.dt.float32r
ALU = mybir.AluOpType
ACT = mybir.ActivationFunctionType
AX = mybir.AxisListType

P = 128
B, S, D = 16, 64, 512
ROWS = B * S
NT = ROWS // P
HR = ROWS // 2
TH = NT // 2
KD = D // P
H, KV, HD = 16, 4, 96
G = H // KV
CH = G * HD // P
F = 1376
FQ = F // 4
FC = 3
FW = [128, 128, 96]
FQP = sum(FW)
NF = 4 * FC
SCALE = float(np.float32(1.0) / np.sqrt(np.float32(HD)))
EPS = 1e-5
TOPK = 6
LOW = -3.0e38
LAGS = D // 4 + 1
W = 512


def dft_tables():
    g = np.arange(P)
    j = np.arange(D // 2)
    even = 2 * np.pi * np.outer(j, 2 * g) / D
    odd = 2 * np.pi * np.outer(j, 2 * g + 1) / D
    ere, eim, ore, oim = np.cos(even), -np.sin(even), np.cos(odd), -np.sin(odd)
    eim[:, 0] = (-1.0) ** j
    fwd = np.stack([np.concatenate([ere, eim], 1)[:P], np.concatenate([ere, eim], 1)[P:],
                    np.concatenate([ore, oim], 1)[:P], np.concatenate([ore, oim], 1)[P:]], 1)
    weight = np.full((P, 1), 2.0)
    weight[0] = 1.0
    inv = np.stack([ere.T * weight, eim.T * weight, ore.T * 2.0, oim.T * 2.0], 1) / D
    n = np.arange(LAGS)
    ce = np.cos(2 * np.pi * np.outer(2 * g, n) / D) * weight
    ci = np.cos(2 * np.pi * np.outer(2 * g, n) / D) * weight
    ci[0] = (-1.0) ** n
    co = np.cos(2 * np.pi * np.outer(2 * g + 1, n) / D) * 2.0
    co[:, LAGS - 1] = 0.0
    corr = np.stack([ce, ci, co], 1) / D
    return fwd.astype(np.float32), inv.astype(np.float32), corr.astype(np.float32)


def decoder_layer(nc, xT, xN, ctxT, wqT, wkT, wvT, woT, w1T, w3T, w2T, a13, a2, bb, b2, fwd, inv, ctab, consts, out):
    ctx = ExitStack()
    with ctx:
        arena = ctx.enter_context(nc.sbuf_tensor("arena", [P, 212800 // 4], F32))
        base = nc.sbuf_base - 212800

        def at(name, offset, shape, dt=F32):
            return nc.alloc_sbuf_tensor_at(name, [P] + shape, dt, offset=base + offset)

        oROW, oSTG, oKC, oVB, oS, oU = 0, 16384, 24576, 57344, 81920, 114688
        rows = at("rows", oROW, [NT, D])
        stg = at("stg", oSTG, [4, W])
        KC = at("KC", oKC, [2, KV, ROWS])
        VB = at("VB", oVB, [B, KV * HD])
        Shi = at("Shi", oS, [2, KD, HR], F32R)
        Slo = at("Slo", oS + 16384, [2, KD, HR], F32R)
        X = at("X", oU, [KD, 2, HR])
        SQ = at("SQ", oU + 16384, [KD, HR])
        DThi = at("DThi", oU + 24576, [KD, 256], F32R)
        DTlo = at("DTlo", oU + 28672, [KD, 256], F32R)
        IThi = at("IThi", oU + 32768, [KD, 256], F32R)
        ITlo = at("ITlo", oU + 36864, [KD, 256], F32R)
        CT = at("CT", oU + 40960, [3, LAGS])
        CXhi = at("CXhi", oU + 42560, [KD, HR], F32R)
        CXlo = at("CXlo", oU + 50752, [KD, HR], F32R)
        WKhi = at("WKhi", oU + 58944, [KD, KV * HD], F32R)
        WKlo = at("WKlo", oU + 65088, [KD, KV * HD], F32R)
        WVhi = at("WVhi", oU + 71232, [KD, KV * HD], F32R)
        WVlo = at("WVlo", oU + 77376, [KD, KV * HD], F32R)
        FOLD = at("FOLD", oU + 83520, [KD, HR])
        WF = at("WF", oU + 83520, [4, D])
        CORR = at("CORR", oKC, [2, D + 8])
        REP = at("REP", oKC + 4160, [2, D + 8])
        E1 = at("E1", oKC + 8320, [2, D])
        E2 = at("E2", oKC + 12416, [D])
        TE = at("TE", oKC + 14464, [2, LAGS + 7])
        QC = at("QC", oU, [2, 8, G, S])
        WQhi = at("WQhi", oU + 16384, [KD, G * HD], F32R)
        WQlo = at("WQlo", oU + 22528, [KD, G * HD], F32R)
        WOhi = at("WOhi", oU + 28672, [CH, D], F32R)
        WOlo = at("WOlo", oU + 34816, [CH, D], F32R)
        OTF = at("OTF", oU + 40960, [2, G, HR])
        OThi = at("OThi", oU + 57344, [2, CH, HR], F32R)
        OTlo = at("OTlo", oU + 69632, [2, CH, HR], F32R)
        PX = at("PX", oU + 81920, [2, 4, P])
        PT = at("PT", oU + 86016, [2, W])
        W1hi = at("W1hi", oS, [2 * 4 * FQP], F32R)
        W1lo = at("W1lo", oS + 11264, [2 * 4 * FQP], F32R)
        A2S = at("A2S", oS + 22528, [NF, 96], F32R)
        A13S = at("A13S", oS + 27136, [KD, 96], F32R)
        B2S = at("B2S", oS + 28672, [D], F32R)
        BS = at("BS", oU + 16384, [2 * 4 * FQP], F32R)
        W2hi = at("W2hi", oU + 28672, [FC, D], F32R)
        W2lo = at("W2lo", oU + 34816, [FC, D], F32R)
        X2hi = at("X2hi", oKC, [KD, HR], F32R)
        X2lo = at("X2lo", oKC + 8192, [KD, HR], F32R)
        XFhi = at("XFhi", oKC + 16384, [HR], F32R)
        XFlo = at("XFlo", oKC + 18432, [HR], F32R)
        TS = at("TS", oKC + 20480, [HR], F32R)
        T2S = at("T2S", oKC + 22528, [HR], F32R)
        SG = at("SG", oKC + 24576, [2, HR])
        HF = at("HF", oKC + 28672, [2, HR])
        Hb = at("Hb", oVB, [4, HR])
        HShi = at("HShi", oVB + 8192, [2, HR], F32R)
        HSlo = at("HSlo", oVB + 12288, [2, HR], F32R)
        XFt = at("XFt", oVB + 16384, [2, P])
        HFhi = at("HFhi", oU, [FC, HR], F32R)
        HFlo = at("HFlo", oU + 6144, [FC, HR], F32R)
        oC = oU + 91712
        cst = at("cst", oC, [P + 1])
        T8 = at("T8", oC + 544, [2, 8])
        ngm = at("ngm", oC + 608, [2, 1])
        es6 = at("es6", oC + 640, [2, TOPK])
        ssum = at("ssum", oC + 704, [NT])
        rsum = at("rsum", oC + 736, [NT])
        nrs = at("nrs", oC + 768, [NT])
        st6 = at("st6", oC + 800, [NT, 6])
        mv = at("mv", oC + 992, [NT, 2])
        ve = at("ve", oC + 1056, [TH])
        y0 = at("y0", oC + 1088, [TH])
        y1 = at("y1", oC + 1120, [TH])
        y2 = at("y2", oC + 1152, [TH])
        lnv = at("lnv", oC + 1184, [TH])
        mx = at("mx", oC + 1216, [2, 4])
        nb = at("nb", oC + 1248, [2, 4])
        sm = at("sm", oC + 1280, [2, 4])
        rc = at("rc", oC + 1312, [2, 4])
        ident = cst[:, 0:P]
        mask = cst[:, P:P + 1]

        def bank(name):
            return ctx.enter_context(nc.psum_tensor(name, [P, W], F32))

        acc = [bank("acc0"), bank("acc1")]
        sc = [bank("sc0"), bank("sc1")]
        pt = [bank("pt0"), bank("pt1")]
        pv = [bank("pv0"), bank("pv1")]
        dftb = [sc[0], sc[1], pt[0], pt[1]]

        def sem(name):
            return ctx.enter_context(nc.semaphore(name))

        stage_in = [sem(f"stage_in{i}") for i in range(4)]
        hi_done, lo_done = sem("hi_done"), sem("lo_done")
        x_in = [sem("x_in0"), sem("x_in1")]
        rows_in, const_in, ctab_in = sem("rows_in"), sem("const_in"), sem("ctab_in")
        folded, xhi_done, xlo_done = sem("folded"), sem("xhi_done"), sem("xlo_done")
        dft_ps, x_copied, squared, odd_sum = sem("dft_ps"), sem("x_copied"), sem("squared"), sem("odd_sum")
        corr_ps, even_copied, corr_built, topped = sem("corr_ps"), sem("even_copied"), sem("corr_built"), sem("topped")
        lag_exps, lag_diff, wf_done = sem("lag_exps"), sem("lag_diff"), sem("wf_done")
        wt_ps, wthi_done, wtlo_done = sem("wt_ps"), sem("wthi_done"), sem("wtlo_done")
        wdft_ps, prods, ysum, yhi_done, ylo_done = sem("wdft_ps"), sem("prods"), sem("ysum"), sem("yhi_done"), sem("ylo_done")
        inv_ps, combined, normed_rows = sem("inv_ps"), sem("combined"), sem("normed_rows")
        var_ready, ln_log, ln_exp = sem("var_ready"), sem("ln_log"), sem("ln_exp")
        x1_ps, x1hi_done, x1lo_done = sem("x1_ps"), sem("x1hi_done"), sem("x1lo_done")
        acc_full, acc_act, acc_dve = sem("acc_full"), sem("acc_act"), sem("acc_dve")
        k_moved = sem("k_moved")
        q_moved = [sem("q_moved0"), sem("q_moved1")]
        o_moved = [sem("o_moved0"), sem("o_moved1")]
        scored, max_ready, exped, recips, p_normed = (
            sem("scored"), sem("max_ready"), sem("exped"), sem("recips"), sem("p_normed"))
        pt_ps, pt_read, pv_ps, ot_read = sem("pt_ps"), sem("pt_read"), sem("pv_ps"), sem("ot_read")
        othi_done, otlo_done = sem("othi_done"), sem("otlo_done")
        x2_ps, x2hi_done, x2lo_done, xft_done, xfhi_done, xflo_done = (
            sem("x2_ps"), sem("x2hi_done"), sem("x2lo_done"), sem("xft_done"), sem("xfhi_done"), sem("xflo_done"))
        ta_ps, tahi_done, talo_done = sem("ta_ps"), sem("tahi_done"), sem("talo_done")
        gu_ps, silu_done, h_done, hhi_done, hlo_done = (
            sem("gu_ps"), sem("silu_done"), sem("h_done"), sem("hhi_done"), sem("hlo_done"))
        fold_done, hfhi_done, hflo_done, a2_ps = sem("fold_done"), sem("hfhi_done"), sem("hflo_done"), sem("a2_ps")
        t2_ps, t2hi_done, t2lo_done = sem("t2_ps"), sem("t2hi_done"), sem("t2lo_done")
        w2_ps, w2_read, stored = sem("w2_ps"), sem("w2_read"), sem("stored")
        dch, pch = sem("dve_chain"), sem("pool_chain")

        def flat(t):
            return t.rearrange("p a b -> p (a b)")

        items = []
        index = {}

        def add(kind, n, src, hi, lo):
            index[(kind, n)] = len(items)
            items.append((kind, src, hi, lo))

        def add_flat(kind, dram, hi, lo, width, step=W):
            for n in range((width + step - 1) // step):
                a, b = n * step, min(width, (n + 1) * step)
                add(kind, n, dram[:, a:b], hi[:, a:b], lo[:, a:b])

        add_flat("fwd", flat(fwd), flat(DThi[:]), flat(DTlo[:]), KD * 256)
        add_flat("wk", flat(wkT), flat(WKhi[:]), flat(WKlo[:]), KD * KV * HD)
        for c in range(KD):
            add("cx0", c, ctxT[:, c, 0:HR], CXhi[:, c, :], CXlo[:, c, :])
        add_flat("wv", flat(wvT), flat(WVhi[:]), flat(WVlo[:]), KD * KV * HD)
        add_flat("inv", flat(inv), flat(IThi[:]), flat(ITlo[:]), KD * 256)
        for c in range(KD):
            add("cx1", c, ctxT[:, c, HR:ROWS], CXhi[:, c, :], CXlo[:, c, :])
        add_flat("wq0", flat(wqT[0]), flat(WQhi[:]), flat(WQlo[:]), KD * G * HD)
        add_flat("wo0", flat(woT[0]), flat(WOhi[:]), flat(WOlo[:]), CH * D)
        for v in range(1, KV + 1):
            if v < KV:
                add_flat(f"wq{v}", flat(wqT[v]), flat(WQhi[:]), flat(WQlo[:]), KD * G * HD)
            if v >= 2:
                add_flat(f"wo{v - 1}", flat(woT[v - 1]), flat(WOhi[:]), flat(WOlo[:]), CH * D)
        NW1 = 4 * FQP
        for w, dram in ((0, w1T), (1, w3T)):
            for n in range(3):
                a, b = n * W, min(NW1, (n + 1) * W)
                add(f"w1{w}", n, dram[:, a:b], W1hi[:, w * NW1 + a:w * NW1 + b], W1lo[:, w * NW1 + a:w * NW1 + b])
        add("a13", 0, flat(a13), flat(A13S[:]), None)
        for n in range(3):
            add("a2", n, flat(a2[:, 4 * n:4 * n + 4]), flat(A2S[:, 4 * n:4 * n + 4]), None)
        add("b2", 0, b2, B2S[0:96], None)
        for n in range(6):
            a, b = n * W, min(2 * NW1, (n + 1) * W)
            add("bb", n, bb[:, a:b], BS[0:96, a:b], None)
        add_flat("w2", flat(w2T), flat(W2hi[:]), flat(W2lo[:]), FC * D)
        count = {}
        for kind, n in index:
            count[kind] = count.get(kind, 0) + 1

        def last_item(kind):
            return index[(kind, count[kind] - 1)] + 1

        groups = []
        groups += [("kc", 0, m) for m in range(CH)] + [("vc", 0, t) for t in range(TH)]
        groups += [("kc", 1, m) for m in range(CH)] + [("vc", 1, t) for t in range(TH)]
        groups += [("kx", 0, m) for m in range(CH)] + [("vx", 0, t) for t in range(TH)]
        groups += [("q", 0, m) for m in range(CH)]
        groups += [("kx", 1, m) for m in range(CH)] + [("vx", 1, t) for t in range(TH)]
        NS = 2 * KV
        NQ = NS * 4
        WOLAG = 6
        for it in range(NQ + WOLAG):
            s, i = divmod(it, 4)
            if i >= 1 and s + 1 < NS:
                groups.append(("q", s + 1, i - 1))
            if it >= WOLAG:
                groups.append(("wo",) + divmod(it - WOLAG, 4))
        gidx = {g: n for n, g in enumerate(groups)}
        by_act = {"kc", "kx", "q"}

        def evac_count(g):
            act = g[0] in by_act
            return sum((x[0] in by_act) == act for x in groups[:gidx[g] + 1])

        def acc_bank(g):
            return acc[gidx[g] % 2]

        tuses = [("corr", t) for t in range(NT)] + [("wt", t) for t in range(TH)] + [("inv", t) for t in range(TH)]
        tuses += [("wt", t) for t in range(TH, NT)] + [("inv", t) for t in range(TH, NT)]
        tuses += [("x1", t) for t in range(NT)]
        tidx = {u: n for n, u in enumerate(tuses)}

        def tbank(u):
            return pv[tidx[u] % 2]

        read_by = {"corr": corr_built, "wt": wtlo_done, "inv": combined, "x1": x1lo_done}

        def prods_count(h, part):
            return 9 * h + (5 if part == 0 else 9)

        block = ctx.enter_context(nc.Block())

        @block.sync
        def _(sp):
            def load(kind):
                for n in range(count[kind]):
                    i = index[(kind, n)]
                    if i >= 4:
                        sp.wait_ge(lo_done, i - 3)
                    src = items[i][1]
                    sp.dma_start(stg[0:src.shape[0], i % 4, 0:src.shape[1]], src).then_inc(stage_in[i % 4], 16)

            sp.dma_start(X[:, :, 0, :], xT[:, :, 0:HR]).then_inc(x_in[0], 16)
            load("fwd")
            sp.dma_start(X[:, :, 1, :], xT[:, :, HR:ROWS]).then_inc(x_in[1], 16)
            sp.dma_start(cst[:], consts).then_inc(const_in, 16)
            sp.dma_start(CT[:], ctab).then_inc(ctab_in, 16)
            load("wk")
            load("cx0")
            load("wv")
            sp.dma_start(rows[:], xN).then_inc(rows_in, 16)
            load("inv")
            load("cx1")

            def move_k(part, h):
                for m in range(CH):
                    kind = ("kx", "kc")[part]
                    sp.wait_ge(acc_act, evac_count((kind, h, m)))
                    sp.dma_start(KC[32 * m:32 * m + 32, part, 3, h * HR:(h + 1) * HR],
                                 KC[96:128, part, m, h * HR:(h + 1) * HR]).then_inc(k_moved, 16)

            def move_q(s, m):
                sp.wait_ge(acc_act, evac_count(("q", s, m)))
                sp.dma_start(QC[32 * m:32 * m + 32, s % 2, :, 3, :],
                             QC[96:128, s % 2, :, m, :]).then_inc(q_moved[s % 2], 16)

            move_k(1, 0)
            move_k(1, 1)
            load("wq0")
            move_k(0, 0)
            for m in range(CH):
                move_q(0, m)
            load("wo0")
            move_k(0, 1)
            for it in range(NQ + WOLAG):
                s, i = divmod(it, 4)
                if i == 2 and s % 2 == 0 and s // 2 + 1 < KV:
                    load(f"wq{s // 2 + 1}")
                if i == 1 and s % 2 == 1 and 1 <= s // 2 < KV:
                    load(f"wo{s // 2}")
                if i >= 1 and s + 1 < NS:
                    move_q(s + 1, i - 1)
                if i == 1 and 1 <= s <= NS:
                    sp.wait_ge(ot_read, 4 * s)
                    for c in range(CH):
                        sp.dma_start(OTF[96:128, (s - 1) % 2, c, :],
                                     OTF[32 * c:32 * c + 32, (s - 1) % 2, 3, :]).then_inc(o_moved[(s - 1) % 2], 16)
                if it == 31:
                    load("w10")
                if it == 32:
                    load("w11")
                if it == 33:
                    load("a13")
                    load("a2")
                    load("b2")
                if it == 34:
                    load("bb")
            load("w2")
            for t in range(NT):
                sp.wait_ge(normed_rows, 2 * NT + t + 1)
                sp.dma_start(out[t * P:(t + 1) * P, :], rows[:, t, :]).then_inc(stored, 16)
            sp.wait_ge(stored, 16 * NT)

        @block.tensor
        def _(_pe):
            pe = nc.tensor

            def mm3(o, lhs, rhs, first, last):
                pe.matmul(o, lhs[0], rhs[0], start=first, stop=False)
                pe.matmul(o, lhs[0], rhs[1], start=False, stop=False)
                return pe.matmul(o, lhs[1], rhs[0], start=False, stop=last)

            def spectrum(h, done):
                for m in range(4):
                    part, im = divmod(m, 2)
                    for k in range(2):
                        kk = 2 * part + k
                        ins = mm3(dftb[m][:], (DThi[:, kk, im * P:(im + 1) * P], DTlo[:, kk, im * P:(im + 1) * P]),
                                  (Shi[:, h, kk, :], Slo[:, h, kk, :]), k == 0, k == 1)
                    ins.then_inc(done, 1)

            def begin_tbank(u):
                n = tidx[u]
                if n >= 2:
                    kind, t = tuses[n - 2]
                    pe.wait_ge(read_by[kind], t + 1)
                return pv[n % 2]

            def correlate(t):
                h = t // TH
                ps = begin_tbank(("corr", t))
                pe.wait_ge(odd_sum, h + 1)
                cols = slice((t % TH) * P, (t % TH + 1) * P)
                pe.matmul(ps[:, 0:LAGS], SQ[:, 0, cols], CT[:, 0, :], start=True, stop=False)
                pe.matmul(ps[:, 0:LAGS], SQ[:, 1, cols], CT[:, 1, :], start=False, stop=True)
                pe.matmul(ps[:, 256:256 + LAGS], SQ[:, 2, cols], CT[:, 2, :], start=True, stop=True).then_inc(corr_ps, 1)

            def turn_weights(t):
                ps = begin_tbank(("wt", t))
                pe.wait_ge(wf_done, t + 1)
                for k in range(KD):
                    ins = pe.transpose(ps[:, k * P:(k + 1) * P], WF[:, t % 4, k * P:(k + 1) * P], ident)
                ins.then_inc(wt_ps, 1)

            def weight_spectrum(h):
                pe.wait_ge(wtlo_done, TH * (h + 1))
                pe.wait_ge(squared, 8)
                pe.wait_ge(x_copied, 8)
                if h == 1:
                    pe.wait_ge(prods, prods_count(0, 1))
                spectrum(h, wdft_ps)

            def invert(t):
                h = t // TH
                ps = begin_tbank(("inv", t))
                pe.wait_ge(ylo_done, 4 * (h + 1))
                pe.wait_ge(lo_done, last_item("inv"))
                cols = slice((t % TH) * P, (t % TH + 1) * P)
                for part in range(2):
                    for k in range(2):
                        kk = 2 * part + k
                        ins = mm3(ps[:, part * 256:(part + 1) * 256], (Shi[:, h, kk, cols], Slo[:, h, kk, cols]),
                                  (IThi[:, kk, :], ITlo[:, kk, :]), k == 0, k == 1)
                ins.then_inc(inv_ps, 1)

            def turn_rows(t):
                ps = begin_tbank(("x1", t))
                pe.wait_ge(normed_rows, t + 1)
                for k in range(KD):
                    ins = pe.transpose(ps[:, k * P:(k + 1) * P], rows[:, t, k * P:(k + 1) * P], ident)
                ins.then_inc(x1_ps, 1)

            def begin_acc(g):
                n = gidx[g]
                if n >= 2:
                    prev = groups[n - 2]
                    pe.wait_ge(acc_act if prev[0] in by_act else acc_dve, evac_count(prev))
                return acc[n % 2]

            def keys(kind, h, m):
                ps = begin_acc((kind, h, m))
                ops = (CXhi, CXlo) if kind == "kc" else (Shi[:, h], Slo[:, h])
                for k in range(KD):
                    ins = mm3(ps[:], (WKhi[:, k, m * P:(m + 1) * P], WKlo[:, k, m * P:(m + 1) * P]),
                              (ops[0][:, k, :], ops[1][:, k, :]), k == 0, k == KD - 1)
                ins.then_inc(acc_full, 1)

            def values(kind, h, t):
                ps = begin_acc((kind, h, t))
                ops = (CXhi, CXlo) if kind == "vc" else (Shi[:, h], Slo[:, h])
                for k in range(KD):
                    ins = mm3(ps[:, 0:KV * HD], (ops[0][:, k, t * P:(t + 1) * P], ops[1][:, k, t * P:(t + 1) * P]),
                              (WVhi[:, k, :], WVlo[:, k, :]), k == 0, k == KD - 1)
                ins.then_inc(acc_full, 1)

            def queries(s, m):
                v, h = divmod(s, 2)
                ps = begin_acc(("q", s, m))
                pe.wait_ge(lo_done, last_item(f"wq{v}"))
                for k in range(KD):
                    ins = mm3(ps[:], (WQhi[:, k, m * P:(m + 1) * P], WQlo[:, k, m * P:(m + 1) * P]),
                              (Shi[:, h, k, :], Slo[:, h, k, :]), k == 0, k == KD - 1)
                ins.then_inc(acc_full, 1)

            def project_out(s, t):
                v = s // 2
                ps = begin_acc(("wo", s, t))
                pe.wait_ge(lo_done, last_item(f"wo{v}"))
                pe.wait_ge(otlo_done, s + 1)
                for c in range(CH):
                    ins = mm3(ps[:], (OThi[:, s % 2, c, t * P:(t + 1) * P], OTlo[:, s % 2, c, t * P:(t + 1) * P]),
                              (WOhi[:, c, :], WOlo[:, c, :]), c == 0, c == CH - 1)
                ins.then_inc(acc_full, 1)

            pe.wait_ge(lo_done, last_item("fwd"))
            pe.wait_ge(xlo_done, 4)
            spectrum(0, dft_ps)
            pe.wait_ge(xlo_done, 8)
            pe.wait_ge(squared, 4)
            pe.wait_ge(x_copied, 4)
            spectrum(1, dft_ps)
            pe.wait_ge(ctab_in, 16)
            pe.wait_ge(const_in, 16)
            for t in range(TH):
                correlate(t)
            pe.wait_ge(lo_done, last_item("cx0"))
            for m in range(CH):
                keys("kc", 0, m)
            for t in range(TH, NT):
                correlate(t)
            pe.wait_ge(lo_done, last_item("wv"))
            for t in range(TH):
                values("vc", 0, t)
            for t in range(TH):
                turn_weights(t)
            weight_spectrum(0)
            pe.wait_ge(lo_done, last_item("cx1"))
            for m in range(CH):
                keys("kc", 1, m)
            for t in range(TH):
                invert(t)
            for t in range(TH, NT):
                turn_weights(t)
            weight_spectrum(1)
            for t in range(TH):
                values("vc", 1, t)
            for t in range(TH, NT):
                invert(t)
            for h in range(2):
                for t in range(TH):
                    turn_rows(h * TH + t)
                pe.wait_ge(x1lo_done, TH * (h + 1))
                for m in range(CH):
                    keys("kx", h, m)
                for t in range(TH):
                    values("vx", h, t)
                if h == 0:
                    for m in range(CH):
                        queries(0, m)

            def score(n):
                s, i = divmod(n, 4)
                v, h = divmod(s, 2)
                if i == 0:
                    pe.wait_ge(q_moved[s % 2], 48 * (s // 2 + 1))
                if n == 0:
                    pe.wait_ge(k_moved, 16 * 4 * CH)
                    pe.wait_ge(prods, prods_count(1, 1))
                if n >= 2:
                    pe.wait_ge(exped, n - 1)
                for u in range(4):
                    bl = 2 * i + u // 2
                    b = 8 * h + bl
                    q = QC[0:HD, s % 2, bl, 2 * (u % 2):2 * (u % 2) + 2, :].rearrange("p a b -> p (a b)")
                    ins = pe.matmul(sc[n % 2][:, u * P:(u + 1) * P], q, KC[0:HD, :, v, b * S:(b + 1) * S],
                                    start=True, stop=True)
                ins.then_inc(scored, 1)

            def turn_probs(n):
                pe.wait_ge(p_normed, n + 1)
                if n >= 2:
                    pe.wait_ge(pt_read, n - 1)
                for u in range(4):
                    ins = pe.transpose(pt[n % 2][:, u * P:(u + 1) * P], PX[:, n % 2, u, :], ident)
                ins.then_inc(pt_ps, 1)

            def attend(n):
                s, i = divmod(n, 4)
                v, h = divmod(s, 2)
                pe.wait_ge(pt_read, n + 1)
                if n == 0:
                    pe.wait_ge(x1lo_done, NT)
                    pe.wait_ge(acc_dve, evac_count(("vx", 1, TH - 1)))
                if n >= 2:
                    pe.wait_ge(ot_read, n - 1)
                for j in range(2):
                    b = 8 * h + 2 * i + j
                    ins = pe.matmul(pv[n % 2][0:HD, j * 256:(j + 1) * 256], VB[:, b, v * HD:(v + 1) * HD],
                                    PT[:, n % 2, j * 256:(j + 1) * 256], start=True, stop=True)
                ins.then_inc(pv_ps, 1)

            for it in range(NQ + WOLAG):
                s, i = divmod(it, 4)
                if it < NQ:
                    score(it)
                if 1 <= it <= NQ:
                    turn_probs(it - 1)
                if i >= 1 and s + 1 < NS:
                    queries(s + 1, i - 1)
                if 1 <= it <= NQ:
                    attend(it - 1)
                if it >= WOLAG:
                    project_out(*divmod(it - WOLAG, 4))

            def turn_rows2(t):
                n = t
                if n >= 2:
                    pe.wait_ge(x2lo_done, n - 1)
                    pe.wait_ge(xft_done, n - 1)
                else:
                    pe.wait_ge(acc_dve, evac_count(groups[-1]))
                if t == TH:
                    pe.wait_ge(w2_read, 0) if False else None
                pe.wait_ge(normed_rows, NT + t + 1)
                for k in range(KD):
                    ins = pe.transpose(pv[t % 2][:, k * P:(k + 1) * P], rows[:, t, k * P:(k + 1) * P], ident)
                ins.then_inc(x2_ps, 1)

            def lora_down(h):
                pe.wait_ge(x2lo_done, TH * (h + 1))
                for k in range(KD):
                    pe.matmul(acc[0][0:96, :], A13S[:, k, :], X2hi[:, k, :], start=k == 0, stop=False)
                    ins = pe.matmul(acc[0][0:96, :], A13S[:, k, :], X2lo[:, k, :], start=False, stop=k == KD - 1)
                ins.then_inc(ta_ps, 1)

            def gate_up(h, n):
                c, q = divmod(n, 4)
                g = h * NF + n
                m = FW[c]
                if g >= 2:
                    pe.wait_ge(h_done, g - 1)
                for w, ps in ((0, sc[g % 2]), (1, pt[g % 2])):
                    o = w * NW1 + q * FQP + c * P
                    mm3(ps[0:m, :], (W1hi[:, o:o + m], W1lo[:, o:o + m]), (XFhi[:], XFlo[:]), True, False)
                    ins = pe.matmul(ps[0:m, :], BS[0:96, o:o + m], TS[0:96, :], start=False, stop=True)
                ins.then_inc(gu_ps, 1)

            def lora2_down(h, n):
                m = FW[n // 4]
                g = h * NF + n
                pe.wait_ge(hlo_done, g + 1)
                pe.matmul(acc[1][0:96, :], A2S[0:m, n, :], HShi[0:m, g % 2, :], start=n == 0, stop=False)
                ins = pe.matmul(acc[1][0:96, :], A2S[0:m, n, :], HSlo[0:m, g % 2, :], start=False, stop=n == NF - 1)
                ins.then_inc(a2_ps, 1)

            def down(t):
                h = t // TH
                if t % TH == 0:
                    pe.wait_ge(lo_done, last_item("w2"))
                    pe.wait_ge(hflo_done, FC * (h + 1))
                    pe.wait_ge(t2lo_done, h + 1)
                if t % TH < 2:
                    pe.wait_ge(x2lo_done, min(NT, TH * (h + 2)))
                    pe.wait_ge(xft_done, min(NT, TH * (h + 2)))
                if t >= 2:
                    pe.wait_ge(w2_read, t - 1)
                ps = pv[t % 2]
                cols = slice((t % TH) * P, (t % TH + 1) * P)
                for c in range(FC):
                    m = FW[c]
                    mm3(ps[:], (HFhi[0:m, c, cols], HFlo[0:m, c, cols]), (W2hi[0:m, c, :], W2lo[0:m, c, :]), c == 0, False)
                pe.matmul(ps[:], T2S[0:96, cols], B2S[0:96, :], start=False, stop=True).then_inc(w2_ps, 1)

            pe.wait_ge(lo_done, last_item("bb"))
            pe.wait_ge(ot_read, NQ)
            for t in range(TH):
                turn_rows2(t)
            for h in range(2):
                lora_down(h)
                pe.wait_ge(talo_done, h + 1)
                pe.wait_ge(xflo_done, TH * (h + 1))
                for n in range(NF + 2):
                    if n < NF:
                        gate_up(h, n)
                    if n >= 2:
                        if h == 1 and n == 2:
                            pe.wait_ge(t2lo_done, 1)
                        lora2_down(h, n - 2)
                if h == 0:
                    for t in range(TH, NT):
                        turn_rows2(t)
                for t in range(TH):
                    down(h * TH + t)

        @block.scalar
        def _(_act):
            act = nc.scalar

            def hi(kind, wait=None):
                for n in range(count[kind]):
                    i = index[(kind, n)]
                    _, src, dst, _ = items[i]
                    act.wait_ge(stage_in[i % 4], 16 * (i // 4 + 1))
                    act.activation(dst, stg[0:src.shape[0], i % 4, 0:src.shape[1]], ACT.Copy).then_inc(hi_done, 1)

            def x_hi(h):
                for k in range(4):
                    act.wait_ge(folded, 4 * h + k + 1)
                    act.activation(Shi[:, h, k, :], FOLD[:, k, :], ACT.Copy).then_inc(xhi_done, 1)

            def spectrum_out(h):
                act.wait_ge(folded, 4 * (h + 1))
                for m in range(4):
                    act.wait_ge(dft_ps, 4 * h + m + 1)
                    act.activation(X[:, m, h, :], dftb[m][:], ACT.Copy).then_inc(x_copied, 1)
                    if h == 1:
                        act.wait_ge(corr_ps, TH)
                    act.activation(SQ[:, m, :], dftb[m][:], ACT.Square).then_inc(squared, 1)

            def even_copy(t):
                act.wait_ge(corr_ps, t + 1)
                if t >= 2:
                    act.wait_ge(corr_built, t - 1)
                act.activation(TE[:, t % 2, 0:LAGS], tbank(("corr", t))[:, 0:LAGS], ACT.Copy).then_inc(even_copied, 1)

            def lag_exp(t):
                act.wait_ge(topped, t + 1)
                if t >= 1:
                    act.wait_ge(lag_diff, t)
                if t >= 2:
                    act.wait_ge(wf_done, t - 1)
                act.activation(E1[:, t % 2, :], CORR[:, t % 2, 0:D], ACT.Exp, bias=ngm[:, t % 2, :]).then_inc(lag_exps, 1)
                act.activation(E2[:], REP[:, t % 2, 0:D], ACT.Exp, bias=ngm[:, t % 2, :]).then_inc(lag_exps, 1)
                act.activation(es6[:, t % 2, :], T8[:, t % 2, 0:TOPK], ACT.Exp, bias=ngm[:, t % 2, :],
                               accum_out=ssum[:, t:t + 1]).then_inc(lag_exps, 1)

            def weights_hi(t):
                h = t // TH
                act.wait_ge(wt_ps, t + 1)
                act.activation(Shi[:, h, :, (t % TH) * P:(t % TH + 1) * P],
                               tbank(("wt", t))[:].rearrange("p (k r) -> p k r", k=KD), ACT.Copy).then_inc(wthi_done, 1)

            def product_hi(h):
                for part in range(2):
                    for j in range(2):
                        act.wait_ge(ysum, 4 * h + 2 * part + j + 1)
                        act.activation(Shi[:, h, 2 * part + j, :], SQ[:, 2 * j, :], ACT.Copy).then_inc(yhi_done, 1)

            def rstd_guess(n):
                act.wait_ge(var_ready, n + 1)
                act.activation(lnv[:], ve[:], ACT.Ln).then_inc(ln_log, 1)
                act.wait_ge(ln_log, n + 1)
                act.activation(y0[:], lnv[:], ACT.Exp, scale=-0.5).then_inc(ln_exp, 1)

            def rows_hi(t):
                h = t // TH
                act.wait_ge(x1_ps, t + 1)
                act.activation(Shi[:, h, :, (t % TH) * P:(t % TH + 1) * P],
                               tbank(("x1", t))[:].rearrange("p (k r) -> p k r", k=KD), ACT.Copy).then_inc(x1hi_done, 1)

            def keys_out(kind, h, m):
                act.wait_ge(acc_full, gidx[(kind, h, m)] + 1)
                part = 1 if kind == "kc" else 0
                act.activation(KC[:, part, m, h * HR:(h + 1) * HR], acc_bank((kind, h, m))[:], ACT.Copy).then_inc(acc_act, 1)

            def queries_out(s, m):
                act.wait_ge(acc_full, gidx[("q", s, m)] + 1)
                if s >= 2:
                    act.wait_ge(scored, 4 * (s - 1))
                act.activation(QC[:, s % 2, :, m, :], acc_bank(("q", s, m))[:].rearrange("p (b r) -> p b r", r=S),
                               ACT.Copy).then_inc(acc_act, 1)

            hi("fwd")
            x_hi(0)
            hi("wk")
            x_hi(1)
            spectrum_out(0)
            hi("cx0")
            for t in range(TH):
                even_copy(t)
                if t in (1, 2):
                    lag_exp(t - 1)
            spectrum_out(1)
            hi("wv")
            for m in range(CH):
                keys_out("kc", 0, m)
            for t in range(TH, NT):
                lag_exp(t - 2)
                even_copy(t)
            hi("inv")
            for t in range(TH):
                weights_hi(t)
            act.wait_ge(acc_full, gidx[("vc", 0, TH - 1)] + 1)
            hi("cx1")
            lag_exp(NT - 2)
            lag_exp(NT - 1)
            product_hi(0)
            for m in range(CH):
                keys_out("kc", 1, m)
            for t in range(TH, NT):
                weights_hi(t)
            rstd_guess(0)
            product_hi(1)
            act.wait_ge(prods, prods_count(1, 1))
            act.wait_ge(ylo_done, 8)
            act.wait_ge(dft_ps, 8)
            act.wait_ge(wdft_ps, 8)
            hi("wq0")
            for t in range(TH):
                rows_hi(t)
            rstd_guess(1)
            for m in range(CH):
                keys_out("kx", 0, m)
            for m in range(CH):
                queries_out(0, m)
            act.wait_ge(inv_ps, NT)
            act.wait_ge(acc_full, gidx[("vc", 1, TH - 1)] + 1)
            hi("wo0")
            for t in range(TH, NT):
                rows_hi(t)
            for m in range(CH):
                keys_out("kx", 1, m)

            def exp_scores(n):
                act.wait_ge(max_ready, n + 1)
                if n >= 2:
                    act.wait_ge(pt_ps, n - 1)
                for u in range(4):
                    ins = act.activation(PX[:, n % 2, u, :], sc[n % 2][:, u * P:(u + 1) * P], ACT.Exp,
                                         bias=nb[:, n % 2, u:u + 1], scale=SCALE, accum_out=sm[:, n % 2, u:u + 1])
                ins.then_inc(exped, 1)

            def output_out(n):
                s, i = divmod(n, 4)
                act.wait_ge(pv_ps, n + 1)
                if i == 0 and s >= 2:
                    act.wait_ge(otlo_done, s - 1)
                act.activation(OTF[0:HD, s % 2, :, 2 * i * S:(2 * i + 2) * S].rearrange("p g (b r) -> p b g r", r=S),
                               pv[n % 2][0:HD, :].rearrange("p (b g r) -> p b g r", g=G, r=S), ACT.Copy).then_inc(ot_read, 1)

            def output_hi(s):
                act.wait_ge(o_moved[s % 2], 48 * (s // 2 + 1))
                if s >= 2:
                    act.wait_ge(acc_full, gidx[("wo", s - 2, TH - 1)] + 1)
                act.activation(OThi[:, s % 2], OTF[:, s % 2, 0:CH], ACT.Copy).then_inc(othi_done, 1)

            for it in range(NQ + WOLAG):
                s, i = divmod(it, 4)
                if i == 0 and s % 2 == 1 and s // 2 + 1 < KV:
                    act.wait_ge(acc_full, gidx[("q", s, CH - 1)] + 1)
                    hi(f"wq{s // 2 + 1}")
                if it < NQ:
                    exp_scores(it)
                if i == 2 and s % 2 == 1 and 1 <= s // 2 < KV:
                    act.wait_ge(acc_full, gidx[("wo", s - 2, TH - 1)] + 1)
                    hi(f"wo{s // 2}")
                if i == 2 and 1 <= s <= NS:
                    output_hi(s - 1)
                if i >= 1 and s + 1 < NS:
                    queries_out(s + 1, i - 1)
                if 1 <= it <= NQ:
                    output_out(it - 1)
                if it == 31:
                    act.wait_ge(acc_full, gidx[("q", NS - 1, CH - 1)] + 1)
                    hi("w10")
                if it == 32:
                    hi("w11")
                if it == 33:
                    hi("a13")
                    hi("a2")
                    hi("b2")
                if it == 34:
                    hi("bb")
                if it == NQ + 3:
                    rstd_guess(2)

            def rows2_hi(t):
                act.wait_ge(x2_ps, t + 1)
                if t == TH:
                    act.wait_ge(ta_ps, 1)
                act.activation(X2hi[:, :, (t % TH) * P:(t % TH + 1) * P],
                               pv[t % 2][:].rearrange("p (k r) -> p k r", k=KD), ACT.Copy).then_inc(x2hi_done, 1)

            def fold_hi(t):
                act.wait_ge(xft_done, t + 1)
                if t == TH:
                    act.wait_ge(gu_ps, NF)
                act.activation(XFhi[:, (t % TH) * P:(t % TH + 1) * P], XFt[:, t % 2, :], ACT.Copy).then_inc(xfhi_done, 1)

            act.wait_ge(acc_full, len(groups))
            act.wait_ge(scored, NQ)
            hi("w2")
            for t in range(TH):
                rows2_hi(t)
                fold_hi(t)
            for h in range(2):
                act.wait_ge(ta_ps, h + 1)
                if h == 1:
                    act.wait_ge(gu_ps, NF)
                act.activation(TS[0:96, :], acc[0][0:96, :], ACT.Copy, scale=0.5).then_inc(tahi_done, 1)
                if h == 0:
                    rstd_guess(3)
                for n in range(NF + 1):
                    g = h * NF + n
                    if n < NF:
                        m = FW[n // 4]
                        act.wait_ge(gu_ps, g + 1)
                        if g >= 2:
                            act.wait_ge(h_done, g - 1)
                        act.activation(SG[0:m, g % 2, :], sc[g % 2][0:m, :], ACT.Silu).then_inc(silu_done, 1)
                    if n >= 1:
                        m = FW[(n - 1) // 4]
                        g -= 1
                        act.wait_ge(h_done, g + 1)
                        if g >= 2:
                            act.wait_ge(a2_ps, g - 1)
                        act.activation(HShi[0:m, g % 2, :], Hb[0:m, g % 4, :], ACT.Copy).then_inc(hhi_done, 1)
                    if n >= 4 and n % 4 == 0 or n == NF:
                        c = n // 4 - 1
                        act.wait_ge(fold_done, h * NF + n)
                        if h == 1:
                            act.wait_ge(w2_ps, TH)
                        act.activation(HFhi[0:FW[c], c, :], HF[0:FW[c], (h * FC + c) % 2, :], ACT.Copy).then_inc(hfhi_done, 1)
                if h == 0:
                    for t in range(TH, NT):
                        rows2_hi(t)
                        fold_hi(t)
                act.wait_ge(a2_ps, NF * (h + 1))
                if h == 1:
                    act.wait_ge(w2_ps, TH)
                act.activation(T2S[0:96, :], acc[1][0:96, :], ACT.Copy, scale=0.5).then_inc(t2hi_done, 1)
                if h == 1:
                    rstd_guess(4)
            rstd_guess(5)

        @block.gpsimd
        def _(_pool):
            pool = nc.gpsimd
            chain = [0]

            def link(ins):
                chain[0] += 1
                ins.then_inc(pch, 1)
                pool.wait_ge(pch, chain[0])

            def lo(kind):
                for n in range(count[kind]):
                    i = index[(kind, n)]
                    _, src, dhi, dlo = items[i]
                    pool.wait_ge(hi_done, i + 1)
                    if kind in ("b2", "bb", "w2"):
                        pool.wait_ge(lo_done, i)
                    raw = stg[:, i % 4, 0:src.shape[1]]
                    if dlo is not None:
                        pool.tensor_tensor(dlo, raw, dhi, ALU.subtract).then_inc(lo_done, 1)
                    elif kind in ("bb", "b2"):
                        full = BS if kind == "bb" else B2S
                        a = n * W if kind == "bb" else 0
                        w = src.shape[1]
                        pool.tensor_tensor(full[32:64, a:a + w], raw[32:64, :], full[32:64, a:a + w],
                                           ALU.subtract).then_inc(lo_done, 1)
                    else:
                        w = 4 if kind == "a13" else 2
                        d = dhi.rearrange("p (a c) -> p a c", c=32)[:, :, w:2 * w]
                        r = raw.rearrange("p (a c) -> p a c", c=32)[:, :, w:2 * w]
                        pool.tensor_tensor(d, r, d, ALU.subtract).then_inc(lo_done, 1)

            def x_lo(h):
                for k in range(4):
                    pool.wait_ge(xhi_done, 4 * h + k + 1)
                    pool.tensor_tensor(Slo[:, h, k, :], FOLD[:, k, :], Shi[:, h, k, :], ALU.subtract).then_inc(xlo_done, 1)

            def odd_power(h):
                pool.wait_ge(squared, 4 * (h + 1))
                pool.tensor_tensor(SQ[:, 2, :], SQ[:, 2, :], SQ[:, 3, :], ALU.add).then_inc(odd_sum, 1)

            def lag_weights(t):
                pool.wait_ge(lag_exps, 3 * t + 2)
                e = E1[:, t % 2, :]
                pool.tensor_tensor(e, e, E2[:], ALU.subtract).then_inc(lag_diff, 1)
                pool.wait_ge(lag_diff, t + 1)
                if t >= 4:
                    pool.wait_ge(wt_ps, t - 3)
                half = D // 2
                pool.tensor_tensor(WF[:, t % 4, 0:half], e[:, 0:half], e[:, half:D], ALU.add).then_inc(pch, 1)
                chain[0] += 1
                pool.wait_ge(pch, chain[0])
                pool.tensor_tensor(WF[:, t % 4, half:D], e[:, 0:half], e[:, half:D], ALU.subtract).then_inc(wf_done, 1)

            def product_sums(h):
                for part in range(2):
                    pool.wait_ge(prods, prods_count(h, part))
                    pool.tensor_tensor(SQ[:, 0, :], SQ[:, 0, :], SQ[:, 1, :], ALU.add).then_inc(ysum, 1)
                    pool.tensor_tensor(SQ[:, 2, :], SQ[:, 2, :], SQ[:, 3, :], ALU.subtract).then_inc(ysum, 1)
                    for j in range(2):
                        pool.wait_ge(yhi_done, 4 * h + 2 * part + j + 1)
                        pool.tensor_tensor(Slo[:, h, 2 * part + j, :], SQ[:, 2 * j, :], Shi[:, h, 2 * part + j, :],
                                           ALU.subtract).then_inc(ylo_done, 1)

            lo("fwd")
            x_lo(0)
            lo("wk")
            x_lo(1)
            odd_power(0)
            lo("cx0")
            pool.wait_ge(xlo_done, 8)
            lag_weights(0)
            lag_weights(1)
            odd_power(1)
            lo("wv")
            for t in range(2, TH + 1):
                lag_weights(t)
            lo("inv")
            pool.wait_ge(acc_full, gidx[("vc", 0, TH - 1)] + 1)
            lo("cx1")
            for t in range(TH + 1, NT):
                lag_weights(t)
            product_sums(0)
            product_sums(1)
            lo("wq0")
            lo("wo0")

            def normalise(n):
                pool.wait_ge(recips, n + 1)
                pool.tensor_tensor(PX[:, n % 2], PX[:, n % 2], rc[:, n % 2, :].unsqueeze(2).to_broadcast([P, 4, P]),
                                   ALU.mult).then_inc(p_normed, 1)

            for it in range(NQ + WOLAG):
                s, i = divmod(it, 4)
                if i == 0 and s % 2 == 1 and s // 2 + 1 < KV:
                    lo(f"wq{s // 2 + 1}")
                if it < NQ:
                    normalise(it)
                if i == 2 and s % 2 == 1 and 1 <= s // 2 < KV:
                    lo(f"wo{s // 2}")
                if it == 31:
                    lo("w10")
                if it == 32:
                    lo("w11")
                if it == 33:
                    lo("a13")
                    lo("a2")
                    lo("b2")
                if it == 34:
                    lo("bb")
            lo("w2")

            def fold_lo(t):
                pool.wait_ge(xfhi_done, t + 1)
                cols = slice((t % TH) * P, (t % TH + 1) * P)
                pool.tensor_tensor(XFlo[:, cols], XFt[:, t % 2, :], XFhi[:, cols], ALU.subtract).then_inc(xflo_done, 1)

            for t in range(TH):
                fold_lo(t)
            for h in range(2):
                for n in range(NF):
                    c, q = divmod(n, 4)
                    g = h * NF + n
                    m = FW[c]
                    pool.wait_ge(h_done, g + 1)
                    dst = HF[0:m, (h * FC + c) % 2, :]
                    if g >= 1:
                        pool.wait_ge(fold_done, g)
                    if q == 0:
                        if h * FC + c >= 2:
                            pool.wait_ge(hflo_done, h * FC + c - 1)
                        pool.tensor_copy(dst, Hb[0:m, g % 4, :]).then_inc(fold_done, 1)
                    else:
                        pool.tensor_tensor(dst, dst, Hb[0:m, g % 4, :], ALU.add).then_inc(fold_done, 1)
                if h == 0:
                    for t in range(TH, NT):
                        fold_lo(t)

        @block.vector
        def _(_dve):
            dve = nc.vector
            chain = [0]

            def link(ins):
                chain[0] += 1
                ins.then_inc(dch, 1)
                dve.wait_ge(dch, chain[0])

            def fold_x(h):
                dve.wait_ge(x_in[h], 16)
                for k in range(4):
                    if h == 1:
                        dve.wait_ge(xlo_done, k + 1)
                    j, op = k % 2, (ALU.add if k < 2 else ALU.subtract)
                    dve.tensor_tensor(FOLD[:, k, :], X[:, j, h, :], X[:, j + 2, h, :], op).then_inc(folded, 1)

            def build_corr(t):
                ps = tbank(("corr", t))
                dve.wait_ge(even_copied, t + 1)
                if t >= 2:
                    dve.wait_ge(lag_exps, 3 * (t - 1))
                c = CORR[:, t % 2, :]
                te = TE[:, t % 2, :]
                n = LAGS - 1
                link(dve.tensor_tensor(c[:, 0:LAGS], te[:, 0:LAGS], ps[:, 256:256 + LAGS], ALU.add))
                dve.tensor_tensor(c[:, 2 * n:n:-1], te[:, 0:n], ps[:, 256:256 + n], ALU.subtract).then_inc(corr_built, 1)
                dve.wait_ge(corr_built, t + 1)
                link(dve.tensor_copy(c[:, D - 1:2 * n:-1], c[:, 1:2 * n]))
                link(dve.max(T8[:, t % 2, :], c[:, 0:D]))
                link(dve.memset(T8[:, t % 2, TOPK:8], LOW))
                link(dve.tensor_scalar(ngm[:, t % 2, :], T8[:, t % 2, 0:1], -1.0, None, ALU.mult))
                dve.match_replace(REP[:, t % 2, 0:D + 2], T8[:, t % 2, :], c[:, 0:D + 2], LOW).then_inc(topped, 1)
                dve.wait_ge(topped, t + 1)

            def weights_lo(t):
                h = t // TH
                cols = slice((t % TH) * P, (t % TH + 1) * P)
                dve.wait_ge(wthi_done, t + 1)
                dve.tensor_tensor(Slo[:, h, :, cols], tbank(("wt", t))[:].rearrange("p (k r) -> p k r", k=KD),
                                  Shi[:, h, :, cols].bitcast(F32), ALU.subtract).then_inc(wtlo_done, 1)

            def products(h):
                for part in range(2):
                    re, im = dftb[2 * part], dftb[2 * part + 1]
                    xr, xi = X[:, 2 * part, h, :], X[:, 2 * part + 1, h, :]
                    dve.wait_ge(wdft_ps, 4 * h + 2 * part + 2)
                    if h == 0 and part == 0:
                        dve.wait_ge(corr_ps, NT)
                    else:
                        dve.wait_ge(ylo_done, 4 * h + 2 * part)
                    dve.tensor_tensor(SQ[:, 0, :], re[:], xr, ALU.mult).then_inc(prods, 1)
                    dve.tensor_tensor(SQ[:, 2, :], re[:], xi, ALU.mult).then_inc(prods, 1)
                    if part == 0:
                        dve.scalar_tensor_tensor(out=SQ[:, 1, :], in0=im[:], scalar=mask, in1=xi,
                                                 op0=ALU.mult, op1=ALU.mult).then_inc(prods, 1)
                        dve.scalar_tensor_tensor(out=SQ[:, 3, :], in0=im[:], scalar=mask, in1=xr,
                                                 op0=ALU.mult, op1=ALU.mult).then_inc(prods, 1)
                        dve.wait_ge(prods, 9 * h + 4)
                        dve.tensor_tensor(SQ[0:1, 2, :], im[0:1, :], xi[0:1, :], ALU.mult).then_inc(prods, 1)
                    else:
                        dve.tensor_tensor(SQ[:, 1, :], im[:], xi, ALU.mult).then_inc(prods, 1)
                        dve.tensor_tensor(SQ[:, 3, :], im[:], xr, ALU.mult).then_inc(prods, 1)

            def stats(t):
                link(dve.bn_stats(st6[:, t, :], rows[:, t, :]))
                link(dve.bn_aggr(mv[:, t, :], st6[:, t, :]))

            def combine(t):
                ps = tbank(("inv", t))
                dve.wait_ge(inv_ps, t + 1)
                dve.wait_ge(lag_exps, 3 * t + 3)
                link(dve.reciprocal(rsum[:, t:t + 1], ssum[:, t:t + 1]))
                link(dve.tensor_scalar(nrs[:, t:t + 1], rsum[:, t:t + 1], -1.0, None, ALU.mult))
                half = D // 2
                for j in range(2):
                    ins = dve.scalar_tensor_tensor(out=rows[:, t, j * half:(j + 1) * half], in0=ps[:, 0:half],
                                                   scalar=rsum[:, t:t + 1], in1=rows[:, t, j * half:(j + 1) * half],
                                                   op0=ALU.mult, op1=ALU.add)
                    link(ins)
                link(dve.scalar_tensor_tensor(out=rows[:, t, 0:half], in0=ps[:, half:D], scalar=rsum[:, t:t + 1],
                                              in1=rows[:, t, 0:half], op0=ALU.mult, op1=ALU.add))
                dve.scalar_tensor_tensor(out=rows[:, t, half:D], in0=ps[:, half:D], scalar=nrs[:, t:t + 1],
                                         in1=rows[:, t, half:D], op0=ALU.mult, op1=ALU.add).then_inc(combined, 1)
                dve.wait_ge(combined, t + 1)
                stats(t)

            def variance(n):
                t = (n % 2) * TH
                dve.tensor_scalar(ve[:], mv[:, t:t + TH, 1], EPS, None, ALU.add).then_inc(var_ready, 1)

            def layernorm(n):
                t0 = (n % 2) * TH
                dve.wait_ge(ln_exp, n + 1)
                link(dve.tensor_tensor(y1[:], y0[:], y0[:], ALU.mult))
                link(dve.tensor_tensor(y2[:], y1[:], ve[:], ALU.mult))
                link(dve.tensor_scalar(y1[:], y2[:], -0.5, 1.5, ALU.mult, ALU.add))
                link(dve.tensor_tensor(y2[:], y0[:], y1[:], ALU.mult))
                for j in range(TH):
                    t = t0 + j
                    dve.tensor_scalar(rows[:, t, :], rows[:, t, :], mv[:, t, 0:1], y2[:, j:j + 1],
                                      ALU.subtract, ALU.mult).then_inc(normed_rows, 1)

            def rows_lo(t):
                h = t // TH
                cols = slice((t % TH) * P, (t % TH + 1) * P)
                dve.wait_ge(x1hi_done, t + 1)
                dve.tensor_tensor(Slo[:, h, :, cols], tbank(("x1", t))[:].rearrange("p (k r) -> p k r", k=KD),
                                  Shi[:, h, :, cols].bitcast(F32), ALU.subtract).then_inc(x1lo_done, 1)

            def values_out(kind, h, t):
                dve.wait_ge(acc_full, gidx[(kind, h, t)] + 1)
                ps = acc_bank((kind, h, t))
                p0 = 64 if kind == "vc" else 0
                b = 2 * (h * TH + t)
                link(dve.tensor_copy(VB[p0:p0 + 64, b, :], ps[0:64, 0:KV * HD]))
                dve.tensor_copy(VB[p0:p0 + 64, b + 1, :], ps[64:128, 0:KV * HD]).then_inc(acc_dve, 1)

            for j in range(2):
                dve.memset(CORR[:, j, D:D + 2], LOW).then_inc(dch, 1)
            chain[0] += 2
            fold_x(0)
            fold_x(1)
            dve.wait_ge(dch, chain[0])
            for t in range(NT):
                if t == TH:
                    for j in range(TH):
                        pass
                build_corr(t)
                if t == NT - 1:
                    break
            for t in range(TH):
                values_out("vc", 0, t)
            for t in range(TH):
                weights_lo(t)
            dve.wait_ge(const_in, 16)
            dve.wait_ge(rows_in, 16)
            products(0)
            for t in range(TH):
                combine(t)
            variance(0)
            for t in range(TH, NT):
                weights_lo(t)
            layernorm(0)
            products(1)
            for t in range(TH):
                values_out("vc", 1, t)
            for t in range(TH, NT):
                combine(t)
            for t in range(TH):
                rows_lo(t)
            variance(1)
            layernorm(1)
            for t in range(TH):
                values_out("vx", 0, t)
            for t in range(TH, NT):
                rows_lo(t)
            for t in range(TH):
                values_out("vx", 1, t)

            def row_max(n):
                dve.wait_ge(scored, n + 1)
                if n >= 2:
                    dve.wait_ge(exped, n - 1)
                link(dve.tensor_reduce(mx[:, n % 2, :], sc[n % 2][:].rearrange("p (u k) -> p u k", u=4), AX.X, ALU.max))
                dve.tensor_scalar(nb[:, n % 2, :], mx[:, n % 2, :], -SCALE, None, ALU.mult).then_inc(max_ready, 1)

            def probs_out(n):
                dve.wait_ge(pt_ps, n + 1)
                if n >= 2:
                    dve.wait_ge(pv_ps, n - 1)
                dve.tensor_copy(PT[:, n % 2, :], pt[n % 2][:]).then_inc(pt_read, 1)

            def sum_recip(n):
                dve.wait_ge(exped, n + 1)
                if n >= 2:
                    dve.wait_ge(p_normed, n - 1)
                dve.reciprocal(rc[:, n % 2, :], sm[:, n % 2, :]).then_inc(recips, 1)

            def output_lo(s):
                dve.wait_ge(othi_done, s + 1)
                dve.tensor_tensor(OTlo[:, s % 2], OTF[:, s % 2, 0:CH], OThi[:, s % 2].bitcast(F32),
                                  ALU.subtract).then_inc(otlo_done, 1)

            def add_out(s, t):
                h = s % 2
                dve.wait_ge(acc_full, gidx[("wo", s, t)] + 1)
                r = rows[:, h * TH + t, :]
                dve.tensor_tensor(r, acc_bank(("wo", s, t))[:], r, ALU.add).then_inc(acc_dve, 1)
                if s >= NS - 2:
                    dve.wait_ge(acc_dve, evac_count(("wo", s, t)))
                    stats(h * TH + t)

            for it in range(NQ + WOLAG):
                s, i = divmod(it, 4)
                if it < NQ:
                    row_max(it)
                if 1 <= it <= NQ:
                    probs_out(it - 1)
                if it < NQ:
                    sum_recip(it)
                if i == 2 and 1 <= s <= NS:
                    output_lo(s - 1)
                if it >= WOLAG:
                    add_out(*divmod(it - WOLAG, 4))
                if it == NQ + 1:
                    variance(2)
                if it == NQ + 4:
                    layernorm(2)
            variance(3)

            def rows2_lo(t):
                cols = slice((t % TH) * P, (t % TH + 1) * P)
                dve.wait_ge(x2hi_done, t + 1)
                ps = pv[t % 2][:].rearrange("p (k r) -> p k r", k=KD)
                dve.tensor_tensor(X2lo[:, :, cols], ps, X2hi[:, :, cols].bitcast(F32), ALU.subtract).then_inc(x2lo_done, 1)
                if t >= 2:
                    dve.wait_ge(xflo_done, t - 1)
                dve.tensor_reduce(XFt[:, t % 2, :], pv[t % 2][:].rearrange("p (k r) -> p r k", k=KD),
                                  AX.X, ALU.add).then_inc(xft_done, 1)

            def add_down(t):
                dve.wait_ge(w2_ps, t + 1)
                r = rows[:, t, :]
                dve.tensor_tensor(r, pv[t % 2][:], r, ALU.add).then_inc(w2_read, 1)
                dve.wait_ge(w2_read, t + 1)
                stats(t)

            for t in range(TH):
                rows2_lo(t)
            for h in range(2):
                dve.wait_ge(tahi_done, h + 1)
                dve.scalar_tensor_tensor(out=TS[64:96, :], in0=acc[0][64:96, :], scalar=0.5,
                                         in1=TS[64:96, :].bitcast(F32), op0=ALU.mult, op1=ALU.subtract).then_inc(talo_done, 1)
                if h == 0:
                    layernorm(3)
                for n in range(NF + 1):
                    g = h * NF + n
                    if n < NF:
                        m = FW[n // 4]
                        dve.wait_ge(silu_done, g + 1)
                        if g >= 4:
                            dve.wait_ge(fold_done, g - 3)
                            dve.wait_ge(hlo_done, g - 3)
                        dve.tensor_tensor(Hb[0:m, g % 4, :], pt[g % 2][0:m, :], SG[0:m, g % 2, :], ALU.mult).then_inc(h_done, 1)
                    if n >= 1:
                        m = FW[(n - 1) // 4]
                        g -= 1
                        dve.wait_ge(hhi_done, g + 1)
                        dve.tensor_tensor(HSlo[0:m, g % 2, :], Hb[0:m, g % 4, :], HShi[0:m, g % 2, :].bitcast(F32),
                                          ALU.subtract).then_inc(hlo_done, 1)
                    if n >= 4 and n % 4 == 0:
                        c = n // 4 - 1
                        dve.wait_ge(hfhi_done, h * FC + c + 1)
                        dve.tensor_tensor(HFlo[0:FW[c], c, :], HF[0:FW[c], (h * FC + c) % 2, :],
                                          HFhi[0:FW[c], c, :].bitcast(F32), ALU.subtract).then_inc(hflo_done, 1)
                if h == 0:
                    for t in range(TH, NT):
                        rows2_lo(t)
                dve.wait_ge(t2hi_done, h + 1)
                dve.scalar_tensor_tensor(out=T2S[64:96, :], in0=acc[1][64:96, :], scalar=0.5,
                                         in1=T2S[64:96, :].bitcast(F32), op0=ALU.mult, op1=ALU.subtract).then_inc(t2lo_done, 1)
                if h == 1:
                    layernorm(4)
                for t in range(TH):
                    add_down(h * TH + t)
                variance(4 + h)
            layernorm(5)


def _kernel_inputs(np_, inp):
    def t3(a):
        return np_.ascontiguousarray(a.T.reshape(-1, P, a.shape[0]).transpose(1, 0, 2))

    x = np_.asarray(inp["x"]).reshape(ROWS, D)
    c = np_.asarray(inp["ctx_4096"]).reshape(ROWS, D)
    order = np_.concatenate([np_.concatenate([np_.arange(HD) + HD * m, 3 * HD + 32 * m + np_.arange(32)]) for m in range(CH)])
    wq = np_.asarray(inp["L0_xattn_Wq"]).reshape(KV, G * HD, D)[:, order]
    wk = np_.asarray(inp["L0_xattn_Wk"])[order]
    wv = np_.asarray(inp["L0_xattn_Wv"])
    wo = np_.asarray(inp["L0_xattn_Wo"]).T.reshape(KV, G * HD, D)[:, order]
    d = {
        "xT": t3(x), "xN": np_.ascontiguousarray(x.reshape(NT, P, D).transpose(1, 0, 2)), "ctxT": t3(c),
        "wqT": np_.stack([t3(wq[v]) for v in range(KV)]), "wkT": t3(wk), "wvT": t3(wv),
        "woT": np_.stack([np_.ascontiguousarray(wo[v].reshape(CH, P, D).transpose(1, 0, 2)) for v in range(KV)]),
    }

    def hidden(a):
        o = np_.zeros((a.shape[1], 4, FQP), a.dtype)
        o[:, :, :FQ] = a.T.reshape(-1, 4, FQ)
        return o.reshape(a.shape[1], 4 * FQP)

    d["w1T"] = hidden(np_.asarray(inp["L0_ffn_w1q"]))
    d["w3T"] = hidden(np_.asarray(inp["L0_ffn_w3q"]))
    w2 = np_.asarray(inp["L0_ffn_w2q"])
    w2p = np_.zeros((FC * P, D), w2.dtype)
    w2p[:FQ] = w2.T
    d["w2T"] = np_.ascontiguousarray(w2p.reshape(FC, P, D).transpose(1, 0, 2))
    a1, a3, a2 = (np_.asarray(inp["L0_ffn_" + n]) for n in ("a1", "a3", "a2"))
    ap = np_.zeros((P, KD, 96), a1.dtype)
    for j in range(3):
        for r in range(2):
            ap[:, :, 32 * j + 4 * r:32 * j + 4 * r + 2] = t3(a1)
            ap[:, :, 32 * j + 4 * r + 2:32 * j + 4 * r + 4] = t3(a3)
    d["a13"] = ap
    h2 = hidden(a2.T).reshape(2, 4, FQP)
    a2p = np_.zeros((P, NF, 96), a2.dtype)
    for n in range(NF):
        cc, q = divmod(n, 4)
        part = h2[:, q, cc * P:cc * P + FW[cc]].T
        for j in range(3):
            for r in range(2):
                a2p[:FW[cc], n, 32 * j + 2 * r:32 * j + 2 * r + 2] = part
    d["a2"] = a2p
    b1, b3, bd = (np_.asarray(inp["L0_ffn_" + n]) for n in ("b1", "b3", "b2"))
    bp = np_.zeros((96, 2, 4 * FQP), b1.dtype)
    b2p = np_.zeros((96, D), bd.dtype)
    for j in range(3):
        for r in range(2):
            bp[32 * j + 4 * r:32 * j + 4 * r + 2, 0] = hidden(b1)
            bp[32 * j + 4 * r + 2:32 * j + 4 * r + 4, 1] = hidden(b3)
            b2p[32 * j + 2 * r:32 * j + 2 * r + 2] = bd.T
    d["bb"] = bp.reshape(96, 2 * 4 * FQP)
    d["b2"] = b2p
    d["fwd"], d["inv"], d["ctab"] = dft_tables()
    consts = np_.ones((P, P + 1), np_.float32)
    consts[:, :P] = np_.eye(P, dtype=np_.float32)
    consts[0, P] = 0.0
    d["consts"] = consts
    return d


def kernel(**inputs):
    import concourse.bacc as _bacc
    from concourse.bass_utils import run_bass_kernel_spmd as _run

    nc = _bacc.Bacc("TRN2", target_bir_lowering=False, num_devices=1)
    arrays, args = {}, []
    for name, a in _kernel_inputs(np, inputs).items():
        a = np.ascontiguousarray(a)
        arrays[f"in_{name}"] = a
        args.append(nc.dram_tensor(f"in_{name}", a.shape, mybir.dt.from_np(a.dtype), kind="ExternalInput").ap())
    args.append(nc.dram_tensor("out_rows", (ROWS, D), F32, kind="ExternalOutput").ap())
    decoder_layer(nc, *args)
    r = _run(nc, [arrays], core_ids=[0])
    return r.results[0]["out_rows"].reshape(B, S, D)
```

```python
from contextlib import ExitStack

import numpy as np

import concourse.bass as bass
from concourse import mybir

F32 = mybir.dt.float32
F32R = mybir.dt.float32r
I32 = mybir.dt.int32
ALU = mybir.AluOpType
ACT = mybir.ActivationFunctionType
AX = mybir.AxisListType

P = 128
B, S, D = 16, 64, 512
ROWS = B * S
NT = ROWS // P
HR = ROWS // 2
TH = NT // 2
KD = D // P
H, KV, HD = 16, 4, 96
G = H // KV
CH = G * HD // P
F = 1376
FQ = F // 4
FC = 3
FW = [128, 128, 96]
FQP = sum(FW)
NF = 4 * FC
SCALE = float(np.float32(1.0) / np.sqrt(np.float32(HD)))
EPS = 1e-5
RSQRT_BITS = float(0x5F3759DF)
TOPK = 6
LOW = -3.0e38
LAGS = D // 4 + 1
W = 512


def dft_tables():
    g = np.arange(P)
    j = np.arange(D // 2)
    even = 2 * np.pi * np.outer(j, 2 * g) / D
    odd = 2 * np.pi * np.outer(j, 2 * g + 1) / D
    ere, eim, ore, oim = np.cos(even), -np.sin(even), np.cos(odd), -np.sin(odd)
    eim[:, 0] = (-1.0) ** j
    fwd = np.stack([np.concatenate([ere, eim], 1)[:P], np.concatenate([ere, eim], 1)[P:],
                    np.concatenate([ore, oim], 1)[:P], np.concatenate([ore, oim], 1)[P:]], 1)
    weight = np.full((P, 1), 2.0)
    weight[0] = 1.0
    inv = np.stack([ere.T * weight, eim.T * weight, ore.T * 2.0, oim.T * 2.0], 1) / D
    n = np.arange(LAGS)
    ce = np.cos(2 * np.pi * np.outer(2 * g, n) / D) * weight
    ci = np.cos(2 * np.pi * np.outer(2 * g, n) / D) * weight
    ci[0] = (-1.0) ** n
    co = np.cos(2 * np.pi * np.outer(2 * g + 1, n) / D) * 2.0
    co[:, LAGS - 1] = 0.0
    corr = np.stack([ce, ci, co], 1) / D
    return fwd.astype(np.float32), inv.astype(np.float32), corr.astype(np.float32)


def decoder_layer(nc, xT, xN, ctxT, wqT, wkT, wvT, woT, w1T, w3T, w2T, a13, a2, bb, b2, fwd, inv, ctab, consts, out):
    ctx = ExitStack()
    with ctx:
        arena = ctx.enter_context(nc.sbuf_tensor("arena", [P, 212800 // 4], F32))
        base = nc.sbuf_base - 212800

        def at(name, offset, shape, dt=F32):
            return nc.alloc_sbuf_tensor_at(name, [P] + shape, dt, offset=base + offset)

        oROW, oSTG, oKC, oVB, oS, oU = 0, 16384, 24576, 57344, 81920, 114688
        rows = at("rows", oROW, [NT, D])
        stg = at("stg", oSTG, [4, W])
        KC = at("KC", oKC, [2, KV, ROWS])
        VB = at("VB", oVB, [B, KV * HD])
        Shi = at("Shi", oS, [2, KD, HR], F32R)
        Slo = at("Slo", oS + 16384, [2, KD, HR], F32R)
        X = at("X", oU, [KD, 2, HR])
        SQ = at("SQ", oU + 16384, [KD, HR])
        DThi = at("DThi", oU + 24576, [KD, 256], F32R)
        DTlo = at("DTlo", oU + 28672, [KD, 256], F32R)
        IThi = at("IThi", oU + 32768, [KD, 256], F32R)
        ITlo = at("ITlo", oU + 36864, [KD, 256], F32R)
        CT = at("CT", oU + 40960, [3, LAGS])
        CXhi = at("CXhi", oU + 42560, [KD, HR], F32R)
        CXlo = at("CXlo", oU + 50752, [KD, HR], F32R)
        WKhi = at("WKhi", oU + 58944, [KD, KV * HD], F32R)
        WKlo = at("WKlo", oU + 65088, [KD, KV * HD], F32R)
        WVhi = at("WVhi", oU + 71232, [KD, KV * HD], F32R)
        WVlo = at("WVlo", oU + 77376, [KD, KV * HD], F32R)
        FOLD = at("FOLD", oU + 83520, [KD, HR])
        WF = at("WF", oU + 83520, [4, D])
        CORR = at("CORR", oKC, [2, D + 8])
        REP = at("REP", oKC + 4160, [2, D + 8])
        E1 = at("E1", oKC + 8320, [2, D])
        E2 = at("E2", oKC + 12416, [D])
        TE = at("TE", oKC + 14464, [2, LAGS + 7])
        QC = at("QC", oU, [2, 8, G, S])
        WQhi = at("WQhi", oU + 16384, [KD, G * HD], F32R)
        WQlo = at("WQlo", oU + 22528, [KD, G * HD], F32R)
        WOhi = at("WOhi", oU + 28672, [2, CH, D], F32R)
        WOlo = at("WOlo", oU + 40960, [2, CH, D], F32R)
        OTF = at("OTF", oU + 53248, [4, G, P])
        OThi = at("OThi", oU + 61440, [4, CH, P], F32R)
        OTlo = at("OTlo", oU + 67584, [4, CH, P], F32R)
        PX = at("PX", oU + 73728, [2, 4, P])
        PT = at("PT", oU + 77824, [2, W])
        W1hi = at("W1hi", oS, [2 * 4 * FQP], F32R)
        W1lo = at("W1lo", oS + 11264, [2 * 4 * FQP], F32R)
        A2S = at("A2S", oU + 81920, [NF, 96], F32R)
        A13S = at("A13S", oU + 86528, [KD, 96], F32R)
        B2S = at("B2S", oU + 88064, [D], F32R)
        BS = at("BS", oU + 16384, [2 * 4 * FQP], F32R)
        W2hi = at("W2hi", oU + 28672, [FC, D], F32R)
        W2lo = at("W2lo", oU + 40960, [FC, D], F32R)
        X2hi = at("X2hi", oKC, [KD, HR], F32R)
        X2lo = at("X2lo", oKC + 8192, [KD, HR], F32R)
        XFhi = at("XFhi", oKC + 16384, [2, HR], F32R)
        XFlo = at("XFlo", oKC + 20480, [2, HR], F32R)
        TS = at("TS", oKC + 24576, [2, HR], F32R)
        T2S = at("T2S", oKC + 28672, [2, HR], F32R)
        Hb = at("Hb", oVB, [4, HR])
        HShi = at("HShi", oVB + 8192, [2, HR], F32R)
        HSlo = at("HSlo", oVB + 12288, [2, HR], F32R)
        XFt = at("XFt", oVB + 16384, [2, P])
        HFhi = at("HFhi", oU, [2, FC, HR], F32R)
        HFlo = at("HFlo", oU + 53248, [2, FC, HR], F32R)
        SG = at("SG", oS + 22528, [2, HR])
        HF = at("HF", oS + 26624, [2, HR])
        oC = oU + 91712
        cst = at("cst", oC, [P + 1])
        T8 = at("T8", oC + 544, [2, 8])
        ngm = at("ngm", oC + 608, [2, 1])
        es6 = at("es6", oC + 640, [2, TOPK])
        ssum = at("ssum", oC + 704, [NT])
        rsum = at("rsum", oC + 736, [NT])
        nrs = at("nrs", oC + 768, [NT])
        st6 = at("st6", oC + 800, [NT, 6])
        mv = at("mv", oC + 992, [NT, 2])
        ve = at("ve", oC + 1056, [TH])
        y0 = at("y0", oC + 1088, [TH])
        y1 = at("y1", oC + 1120, [TH])
        y2 = at("y2", oC + 1152, [TH])
        mx = at("mx", oC + 1216, [2, 4])
        nb = at("nb", oC + 1248, [2, 4])
        sm = at("sm", oC + 1280, [2, 4])
        rc = at("rc", oC + 1312, [2, 4])
        ident = cst[:, 0:P]
        mask = cst[:, P:P + 1]

        def bank(name):
            return ctx.enter_context(nc.psum_tensor(name, [P, W], F32))

        acc = [bank("acc0"), bank("acc1")]
        sc = [bank("sc0"), bank("sc1")]
        pt = [bank("pt0"), bank("pt1")]
        pv = [bank("pv0"), bank("pv1")]
        dftb = [sc[0], sc[1], pt[0], pt[1]]

        def sem(name):
            return ctx.enter_context(nc.semaphore(name))

        stage_in = [sem(f"stage_in{i}") for i in range(4)]
        hi_done, lo_done = sem("hi_done"), sem("lo_done")
        x_in = [sem("x_in0"), sem("x_in1")]
        rows_in, const_in, ctab_in = sem("rows_in"), sem("const_in"), sem("ctab_in")
        folded, xhi_done, xlo_done = sem("folded"), sem("xhi_done"), sem("xlo_done")
        dft_ps, x_copied, squared, odd_sum = sem("dft_ps"), sem("x_copied"), sem("squared"), sem("odd_sum")
        corr_ps, even_copied, corr_built, topped = sem("corr_ps"), sem("even_copied"), sem("corr_built"), sem("topped")
        lag_exps, lag_diff, wf_done = sem("lag_exps"), sem("lag_diff"), sem("wf_done")
        wt_ps, wthi_done, wtlo_done = sem("wt_ps"), sem("wthi_done"), sem("wtlo_done")
        wdft_ps, prods, ysum, yhi_done, ylo_done = sem("wdft_ps"), sem("prods"), sem("ysum"), sem("yhi_done"), sem("ylo_done")
        inv_ps, combined, normed_rows = sem("inv_ps"), sem("combined"), sem("normed_rows")
        x1_ps, x1hi_done, x1lo_done = sem("x1_ps"), sem("x1hi_done"), sem("x1lo_done")
        acc_full, acc_act, acc_dve = sem("acc_full"), sem("acc_act"), sem("acc_dve")
        k_moved = sem("k_moved")
        q_moved = [sem("q_moved0"), sem("q_moved1")]
        o_moved = [sem(f"o_moved{i}") for i in range(4)]
        scored, max_ready, exped, recips, p_normed = (
            sem("scored"), sem("max_ready"), sem("exped"), sem("recips"), sem("p_normed"))
        pt_ps, pt_read, pv_ps, ot_read = sem("pt_ps"), sem("pt_read"), sem("pv_ps"), sem("ot_read")
        othi_done, otlo_done = sem("othi_done"), sem("otlo_done")
        x2_ps, x2hi_done, x2lo_done, xft_done, xfhi_done, xflo_done = (
            sem("x2_ps"), sem("x2hi_done"), sem("x2lo_done"), sem("xft_done"), sem("xfhi_done"), sem("xflo_done"))
        ta_ps, tahi_done, talo_done = sem("ta_ps"), sem("tahi_done"), sem("talo_done")
        gu_ps, silu_done, h_done, hhi_done, hlo_done = (
            sem("gu_ps"), sem("silu_done"), sem("h_done"), sem("hhi_done"), sem("hlo_done"))
        fold_done, hfhi_done, hflo_done, a2_ps = sem("fold_done"), sem("hfhi_done"), sem("hflo_done"), sem("a2_ps")
        t2_ps, t2hi_done, t2lo_done = sem("t2_ps"), sem("t2hi_done"), sem("t2lo_done")
        w2_ps, w2_read, stored = sem("w2_ps"), sem("w2_read"), sem("stored")
        dch, pch = sem("dve_chain"), sem("pool_chain")

        def flat(t):
            return t.rearrange("p a b -> p (a b)")

        items = []
        index = {}

        def add(kind, n, src, hi, lo):
            index[(kind, n)] = len(items)
            items.append((kind, src, hi, lo))

        def add_flat(kind, dram, hi, lo, width, step=W):
            for n in range((width + step - 1) // step):
                a, b = n * step, min(width, (n + 1) * step)
                add(kind, n, dram[:, a:b], hi[:, a:b], lo[:, a:b])

        add_flat("fwd", flat(fwd), flat(DThi[:]), flat(DTlo[:]), KD * 256)
        add_flat("wk", flat(wkT), flat(WKhi[:]), flat(WKlo[:]), KD * KV * HD)
        for c in range(KD):
            add("cx0", c, ctxT[:, c, 0:HR], CXhi[:, c, :], CXlo[:, c, :])
        add_flat("wv", flat(wvT), flat(WVhi[:]), flat(WVlo[:]), KD * KV * HD)
        add_flat("inv", flat(inv), flat(IThi[:]), flat(ITlo[:]), KD * 256)
        for c in range(KD):
            add("cx1", c, ctxT[:, c, HR:ROWS], CXhi[:, c, :], CXlo[:, c, :])
        add_flat("wq0", flat(wqT[0]), flat(WQhi[:]), flat(WQlo[:]), KD * G * HD)
        add_flat("wo0", flat(woT[0]), flat(WOhi[:, 0]), flat(WOlo[:, 0]), CH * D)
        for v in range(1, KV):
            add_flat(f"wq{v}", flat(wqT[v]), flat(WQhi[:]), flat(WQlo[:]), KD * G * HD)
            add_flat(f"wo{v}", flat(woT[v]), flat(WOhi[:, v % 2]), flat(WOlo[:, v % 2]), CH * D)
        NW1 = 4 * FQP
        add("a13", 0, flat(a13), flat(A13S[:]), None)
        for n in range(3):
            add("a2", n, flat(a2[:, 4 * n:4 * n + 4]), flat(A2S[:, 4 * n:4 * n + 4]), None)
        add_flat("w2", flat(w2T), flat(W2hi[:]), flat(W2lo[:]), FC * D)
        for w, dram in ((0, w1T), (1, w3T)):
            for n in range(3):
                a, b = n * W, min(NW1, (n + 1) * W)
                add(f"w1{w}", n, dram[:, a:b], W1hi[:, w * NW1 + a:w * NW1 + b], W1lo[:, w * NW1 + a:w * NW1 + b])
        add("b2", 0, b2, B2S[0:96], None)
        for n in range(6):
            a, b = n * W, min(2 * NW1, (n + 1) * W)
            add(f"bb{n // 4}", n % 4, bb[:, a:b], BS[0:96, a:b], None)
        TURN_AT = {2: 4, 4: 5, 6: 6, 8: 7}
        LORA_AT = 10
        DOWN_AT = {NF + 4: 0, NF + 6: 1, NF + 8: 2, NF + 10: 3}
        count = {}
        for kind, n in index:
            count[kind] = count.get(kind, 0) + 1

        PIECES_AT = {}
        for v in range(1, KV):
            PIECES_AT[8 * v - 4] = [f"wq{v}"]
            PIECES_AT[8 * v - 2] = [f"wo{v}"]
        FFN_AT = {24: ["a13", "a2"], 26: ["w2"], 28: ["w10"], 29: ["w11"], 30: ["b2"], 31: ["bb0"]}
        PIECES_AT.update(FFN_AT)
        LO_BY_DVE = ("b2", "bb0")

        def last_item(kind):
            return index[(kind, count[kind] - 1)] + 1

        groups = []
        groups += [("kc", 0, m) for m in range(CH)] + [("vc", 0, t) for t in range(TH)]
        groups += [("kc", 1, m) for m in range(CH)] + [("vc", 1, t) for t in range(TH)]
        groups += [("kx", 0, m) for m in range(CH)] + [("vx", 0, t) for t in range(TH)]
        groups += [("q", 0, m) for m in range(CH)]
        groups += [("kx", 1, m) for m in range(CH)] + [("vx", 1, t) for t in range(TH)]
        NS = 2 * KV
        NQ = NS * 4

        def projected(it):
            s, i = divmod(it, 4)
            quads = [[4 * s - 3, 4 * s - 2], [4 * s - 1], [], [4 * s]][i]
            return [n for n in quads if 0 <= n < NQ]

        for it in range(NQ + 2):
            s, i = divmod(it, 4)
            if i >= 1 and s + 1 < NS:
                groups.append(("q", s + 1, i - 1))
            groups += [("wo",) + divmod(n, 4) for n in projected(it)]
        gidx = {g: n for n, g in enumerate(groups)}
        by_act = {"kc", "kx", "q"}

        def evac_count(g):
            act = g[0] in by_act
            return sum((x[0] in by_act) == act for x in groups[:gidx[g] + 1])

        def acc_bank(g):
            return acc[gidx[g] % 2]

        tuses = [("corr", t) for t in range(NT)] + [("wt", t) for t in range(TH)] + [("inv", t) for t in range(TH)]
        tuses += [("wt", t) for t in range(TH, NT)] + [("inv", t) for t in range(TH, NT)]
        tuses += [("x1", t) for t in range(NT)]
        tidx = {u: n for n, u in enumerate(tuses)}

        def tbank(u):
            return pv[tidx[u] % 2]

        read_by = {"corr": corr_built, "wt": wtlo_done, "inv": combined, "x1": x1lo_done}

        def prods_count(h, part):
            return 9 * h + (5 if part == 0 else 9)

        block = ctx.enter_context(nc.Block())

        @block.sync
        def _(sp):
            loaded = [0]

            def load_to(end):
                for i in range(loaded[0], min(end, len(items))):
                    loaded[0] = i + 1
                    if i >= 4:
                        sp.wait_ge(lo_done, i - 3)
                    src = items[i][1]
                    sp.dma_start(stg[0:src.shape[0], i % 4, 0:src.shape[1]], src).then_inc(stage_in[i % 4], 16)

            def load(kind):
                load_to(last_item(kind))

            sp.dma_start(X[:, :, 0, :], xT[:, :, 0:HR]).then_inc(x_in[0], 16)
            load("fwd")
            sp.dma_start(X[:, :, 1, :], xT[:, :, HR:ROWS]).then_inc(x_in[1], 16)
            sp.dma_start(cst[:], consts).then_inc(const_in, 16)
            sp.dma_start(CT[:], ctab).then_inc(ctab_in, 16)
            load("wk")
            load("cx0")
            load("wv")
            sp.dma_start(rows[:], xN).then_inc(rows_in, 16)
            load("inv")
            load("cx1")

            def move_k(part, h):
                for m in range(CH):
                    kind = ("kx", "kc")[part]
                    sp.wait_ge(acc_act, evac_count((kind, h, m)))
                    sp.dma_start(KC[32 * m:32 * m + 32, part, 3, h * HR:(h + 1) * HR],
                                 KC[96:128, part, m, h * HR:(h + 1) * HR]).then_inc(k_moved, 16)

            def move_q(s, m):
                sp.wait_ge(acc_act, evac_count(("q", s, m)))
                sp.dma_start(QC[32 * m:32 * m + 32, s % 2, :, 3, :],
                             QC[96:128, s % 2, :, m, :]).then_inc(q_moved[s % 2], 16)

            move_k(1, 0)
            move_k(1, 1)
            load("wq0")
            move_k(0, 0)
            for m in range(CH):
                move_q(0, m)
            load("wo0")
            move_k(0, 1)
            taken = last_item("wo0")
            for it in range(NQ + 2):
                s, i = divmod(it, 4)
                for kind in PIECES_AT.get(it - 1, ()):
                    if it <= NQ - 1:
                        taken = last_item(kind)
                if it == NQ + 1:
                    taken = len(items)
                load_to(taken + 4)
                if i >= 1 and s + 1 < NS:
                    move_q(s + 1, i - 1)
                if 1 <= it <= NQ:
                    n = it - 1
                    sp.wait_ge(ot_read, n + 1)
                    for c in range(CH):
                        sp.dma_start(OTF[96:128, n % 4, c, :], OTF[32 * c:32 * c + 32, n % 4, 3, :]).then_inc(o_moved[n % 4], 16)
            for t in range(NT):
                sp.wait_ge(normed_rows, 2 * NT + t + 1)
                sp.dma_start(out[t * P:(t + 1) * P, :], rows[:, t, :]).then_inc(stored, 16)
            sp.wait_ge(stored, 16 * NT)

        @block.tensor
        def _(_pe):
            pe = nc.tensor

            def mm3(o, lhs, rhs, first, last):
                pe.matmul(o, lhs[0], rhs[0], start=first, stop=False)
                pe.matmul(o, lhs[0], rhs[1], start=False, stop=False)
                return pe.matmul(o, lhs[1], rhs[0], start=False, stop=last)

            def spectrum(h, done):
                for m in range(4):
                    part, im = divmod(m, 2)
                    for k in range(2):
                        kk = 2 * part + k
                        ins = mm3(dftb[m][:], (DThi[:, kk, im * P:(im + 1) * P], DTlo[:, kk, im * P:(im + 1) * P]),
                                  (Shi[:, h, kk, :], Slo[:, h, kk, :]), k == 0, k == 1)
                    ins.then_inc(done, 1)

            def begin_tbank(u):
                n = tidx[u]
                if n >= 2:
                    kind, t = tuses[n - 2]
                    pe.wait_ge(read_by[kind], t + 1)
                return pv[n % 2]

            def correlate(t):
                h = t // TH
                ps = begin_tbank(("corr", t))
                pe.wait_ge(odd_sum, h + 1)
                cols = slice((t % TH) * P, (t % TH + 1) * P)
                pe.matmul(ps[:, 0:LAGS], SQ[:, 0, cols], CT[:, 0, :], start=True, stop=False)
                pe.matmul(ps[:, 0:LAGS], SQ[:, 1, cols], CT[:, 1, :], start=False, stop=True)
                pe.matmul(ps[:, 256:256 + LAGS], SQ[:, 2, cols], CT[:, 2, :], start=True, stop=True).then_inc(corr_ps, 1)

            def turn_weights(t):
                ps = begin_tbank(("wt", t))
                pe.wait_ge(wf_done, t + 1)
                for k in range(KD):
                    ins = pe.transpose(ps[:, k * P:(k + 1) * P], WF[:, t % 4, k * P:(k + 1) * P], ident)
                ins.then_inc(wt_ps, 1)

            def weight_spectrum(h):
                pe.wait_ge(wtlo_done, TH * (h + 1))
                pe.wait_ge(squared, 8)
                pe.wait_ge(x_copied, 8)
                if h == 1:
                    pe.wait_ge(prods, prods_count(0, 1))
                spectrum(h, wdft_ps)

            def invert(t):
                h = t // TH
                ps = begin_tbank(("inv", t))
                pe.wait_ge(ylo_done, 4 * (h + 1))
                pe.wait_ge(lo_done, last_item("inv"))
                cols = slice((t % TH) * P, (t % TH + 1) * P)
                for part in range(2):
                    for k in range(2):
                        kk = 2 * part + k
                        ins = mm3(ps[:, part * 256:(part + 1) * 256], (Shi[:, h, kk, cols], Slo[:, h, kk, cols]),
                                  (IThi[:, kk, :], ITlo[:, kk, :]), k == 0, k == 1)
                ins.then_inc(inv_ps, 1)

            def turn_rows(t):
                ps = begin_tbank(("x1", t))
                pe.wait_ge(normed_rows, t + 1)
                for k in range(KD):
                    ins = pe.transpose(ps[:, k * P:(k + 1) * P], rows[:, t, k * P:(k + 1) * P], ident)
                ins.then_inc(x1_ps, 1)

            def begin_acc(g):
                n = gidx[g]
                if n >= 2:
                    prev = groups[n - 2]
                    pe.wait_ge(acc_act if prev[0] in by_act else acc_dve, evac_count(prev))
                return acc[n % 2]

            def keys(kind, h, m):
                ps = begin_acc((kind, h, m))
                ops = (CXhi, CXlo) if kind == "kc" else (Shi[:, h], Slo[:, h])
                for k in range(KD):
                    ins = mm3(ps[:], (WKhi[:, k, m * P:(m + 1) * P], WKlo[:, k, m * P:(m + 1) * P]),
                              (ops[0][:, k, :], ops[1][:, k, :]), k == 0, k == KD - 1)
                ins.then_inc(acc_full, 1)

            def values(kind, h, t):
                ps = begin_acc((kind, h, t))
                ops = (CXhi, CXlo) if kind == "vc" else (Shi[:, h], Slo[:, h])
                for k in range(KD):
                    ins = mm3(ps[:, 0:KV * HD], (ops[0][:, k, t * P:(t + 1) * P], ops[1][:, k, t * P:(t + 1) * P]),
                              (WVhi[:, k, :], WVlo[:, k, :]), k == 0, k == KD - 1)
                ins.then_inc(acc_full, 1)

            def queries(s, m):
                v, h = divmod(s, 2)
                ps = begin_acc(("q", s, m))
                pe.wait_ge(lo_done, last_item(f"wq{v}"))
                for k in range(KD):
                    ins = mm3(ps[:], (WQhi[:, k, m * P:(m + 1) * P], WQlo[:, k, m * P:(m + 1) * P]),
                              (Shi[:, h, k, :], Slo[:, h, k, :]), k == 0, k == KD - 1)
                ins.then_inc(acc_full, 1)

            def project_out(n):
                s, t = divmod(n, 4)
                v = s // 2
                ps = begin_acc(("wo", s, t))
                pe.wait_ge(lo_done, last_item(f"wo{v}"))
                pe.wait_ge(otlo_done, n + 1)
                for c in range(CH):
                    ins = mm3(ps[:], (OThi[:, n % 4, c, :], OTlo[:, n % 4, c, :]),
                              (WOhi[:, v % 2, c, :], WOlo[:, v % 2, c, :]), c == 0, c == CH - 1)
                ins.then_inc(acc_full, 1)

            pe.wait_ge(lo_done, last_item("fwd"))
            pe.wait_ge(xlo_done, 4)
            spectrum(0, dft_ps)
            pe.wait_ge(xlo_done, 8)
            pe.wait_ge(squared, 4)
            pe.wait_ge(x_copied, 4)
            spectrum(1, dft_ps)
            pe.wait_ge(ctab_in, 16)
            pe.wait_ge(const_in, 16)
            for t in range(TH):
                correlate(t)
            pe.wait_ge(lo_done, last_item("cx0"))
            for m in range(CH):
                keys("kc", 0, m)
            for t in range(TH, NT):
                correlate(t)
            pe.wait_ge(lo_done, last_item("wv"))
            for t in range(TH):
                values("vc", 0, t)
            for t in range(TH):
                turn_weights(t)
            weight_spectrum(0)
            pe.wait_ge(lo_done, last_item("cx1"))
            for m in range(CH):
                keys("kc", 1, m)
            for t in range(TH):
                invert(t)
            for t in range(TH, NT):
                turn_weights(t)
            weight_spectrum(1)
            for t in range(TH):
                values("vc", 1, t)
            for t in range(TH, NT):
                invert(t)
            for h in range(2):
                for t in range(TH):
                    turn_rows(h * TH + t)
                pe.wait_ge(x1lo_done, TH * (h + 1))
                for m in range(CH):
                    keys("kx", h, m)
                for t in range(TH):
                    values("vx", h, t)
                if h == 0:
                    for m in range(CH):
                        queries(0, m)

            def score(n):
                s, i = divmod(n, 4)
                v, h = divmod(s, 2)
                if i == 0:
                    pe.wait_ge(q_moved[s % 2], 48 * (s // 2 + 1))
                if n == 0:
                    pe.wait_ge(k_moved, 16 * 4 * CH)
                    pe.wait_ge(prods, prods_count(1, 1))
                if n >= 2:
                    pe.wait_ge(exped, n - 1)
                for u in range(4):
                    bl = 2 * i + u // 2
                    b = 8 * h + bl
                    q = QC[0:HD, s % 2, bl, 2 * (u % 2):2 * (u % 2) + 2, :].rearrange("p a b -> p (a b)")
                    ins = pe.matmul(sc[n % 2][:, u * P:(u + 1) * P], q, KC[0:HD, :, v, b * S:(b + 1) * S],
                                    start=True, stop=True)
                ins.then_inc(scored, 1)

            def turn_probs(n):
                pe.wait_ge(p_normed, n + 1)
                if n >= 2:
                    pe.wait_ge(pt_read, n - 1)
                for u in range(4):
                    ins = pe.transpose(pt[n % 2][:, u * P:(u + 1) * P], PX[:, n % 2, u, :], ident)
                ins.then_inc(pt_ps, 1)

            def attend(n):
                s, i = divmod(n, 4)
                v, h = divmod(s, 2)
                pe.wait_ge(pt_read, n + 1)
                if n == 0:
                    pe.wait_ge(x1lo_done, NT)
                    pe.wait_ge(acc_dve, evac_count(("vx", 1, TH - 1)))
                if n >= 2:
                    pe.wait_ge(ot_read, n - 1)
                for j in range(2):
                    b = 8 * h + 2 * i + j
                    ins = pe.matmul(pv[n % 2][0:HD, j * 256:(j + 1) * 256], VB[:, b, v * HD:(v + 1) * HD],
                                    PT[:, n % 2, j * 256:(j + 1) * 256], start=True, stop=True)
                ins.then_inc(pv_ps, 1)

            for it in range(NQ + 1):
                s, i = divmod(it, 4)
                wo = projected(it)
                queries_left = i >= 1 and s + 1 < NS
                if queries_left and i == CH:
                    queries(s + 1, i - 1)
                    queries_left = False
                if it < NQ:
                    score(it)
                if 1 <= it <= NQ:
                    turn_probs(it - 1)
                if queries_left:
                    queries(s + 1, i - 1)
                elif wo:
                    project_out(wo.pop(0))
                if 1 <= it <= NQ:
                    attend(it - 1)
                for n in wo:
                    if it < NQ:
                        project_out(n)

            def turn_rows2(t):
                if t >= 2:
                    pe.wait_ge(x2lo_done, t - 1)
                    pe.wait_ge(xft_done, t - 1)
                pe.wait_ge(normed_rows, NT + t + 1)
                for k in range(KD):
                    ins = pe.transpose(pv[t % 2][:, k * P:(k + 1) * P], rows[:, t, k * P:(k + 1) * P], ident)
                ins.then_inc(x2_ps, 1)

            def lora_down(h):
                if h == 0:
                    pe.wait_ge(acc_dve, evac_count(groups[-1]))
                    pe.wait_ge(acc_dve, evac_count(groups[-2]))
                pe.wait_ge(x2lo_done, TH * (h + 1))
                for k in range(KD):
                    pe.matmul(acc[0][0:96, :], A13S[:, k, :], X2hi[:, k, :], start=k == 0, stop=False)
                    ins = pe.matmul(acc[0][0:96, :], A13S[:, k, :], X2lo[:, k, :], start=False, stop=k == KD - 1)
                ins.then_inc(ta_ps, 1)

            def gate_up(g):
                h, n = divmod(g, NF)
                c, q = divmod(n, 4)
                m = FW[c]
                if n == 0:
                    pe.wait_ge(xflo_done, TH * (h + 1))
                if g >= 2:
                    pe.wait_ge(h_done, g - 1)
                for w, ps in ((0, sc[g % 2]), (1, pt[g % 2])):
                    o = w * NW1 + q * FQP + c * P
                    mm3(ps[0:m, :], (W1hi[:, o:o + m], W1lo[:, o:o + m]), (XFhi[:, h, :], XFlo[:, h, :]), True, False)
                    if n == 0 and w == 0:
                        pe.wait_ge(talo_done, h + 1)
                    ins = pe.matmul(ps[0:m, :], BS[0:96, o:o + m], TS[0:96, h, :], start=False, stop=True)
                ins.then_inc(gu_ps, 1)

            def lora2_down(g):
                h, n = divmod(g, NF)
                m = FW[n // 4]
                if h == 1 and n == 0:
                    pe.wait_ge(t2lo_done, 1)
                pe.wait_ge(hlo_done, g + 1)
                pe.matmul(acc[1][0:96, :], A2S[0:m, n, :], HShi[0:m, g % 2, :], start=n == 0, stop=False)
                ins = pe.matmul(acc[1][0:96, :], A2S[0:m, n, :], HSlo[0:m, g % 2, :], start=False, stop=n == NF - 1)
                ins.then_inc(a2_ps, 1)

            def down(t):
                h = t // TH
                if t % TH == 0:
                    pe.wait_ge(lo_done, last_item("w2"))
                    pe.wait_ge(hflo_done, FC * (h + 1))
                if t < 2:
                    pe.wait_ge(x2lo_done, NT)
                    pe.wait_ge(xft_done, NT)
                else:
                    pe.wait_ge(w2_read, t - 1)
                ps = pv[t % 2]
                cols = slice((t % TH) * P, (t % TH + 1) * P)
                for c in range(FC):
                    m = FW[c]
                    mm3(ps[:], (HFhi[0:m, h, c, cols], HFlo[0:m, h, c, cols]), (W2hi[0:m, c, :], W2lo[0:m, c, :]), c == 0, False)
                if t % TH == 0:
                    pe.wait_ge(t2lo_done, h + 1)
                pe.matmul(ps[:], T2S[0:96, h, cols], B2S[0:96, :], start=False, stop=True).then_inc(w2_ps, 1)

            pe.wait_ge(ot_read, NQ - 1)
            turn_rows2(0)
            project_out(NQ - 2)
            pe.wait_ge(ot_read, NQ)
            turn_rows2(1)
            turn_rows2(2)
            project_out(NQ - 1)
            turn_rows2(3)
            lora_down(0)
            pe.wait_ge(lo_done, last_item("bb1"))
            for g in range(2 * NF + 2):
                if g < 2 * NF:
                    gate_up(g)
                if g >= 2:
                    lora2_down(g - 2)
                if g in TURN_AT:
                    turn_rows2(TURN_AT[g])
                if g == LORA_AT:
                    lora_down(1)
                if g in DOWN_AT:
                    down(DOWN_AT[g])
            for t in range(TH, NT):
                down(t)

        @block.scalar
        def _(_act):
            act = nc.scalar

            def hi(kind, wait=None):
                for n in range(count[kind]):
                    i = index[(kind, n)]
                    _, src, dst, _ = items[i]
                    act.wait_ge(stage_in[i % 4], 16 * (i // 4 + 1))
                    act.activation(dst, stg[0:src.shape[0], i % 4, 0:src.shape[1]], ACT.Copy).then_inc(hi_done, 1)

            def x_hi(h):
                for k in range(4):
                    act.wait_ge(folded, 4 * h + k + 1)
                    act.activation(Shi[:, h, k, :], FOLD[:, k, :], ACT.Copy).then_inc(xhi_done, 1)

            def spectrum_out(h):
                act.wait_ge(folded, 4 * (h + 1))
                for m in range(4):
                    act.wait_ge(dft_ps, 4 * h + m + 1)
                    act.activation(X[:, m, h, :], dftb[m][:], ACT.Copy).then_inc(x_copied, 1)
                    if h == 1:
                        act.wait_ge(corr_ps, TH)
                    act.activation(SQ[:, m, :], dftb[m][:], ACT.Square).then_inc(squared, 1)

            def even_copy(t):
                act.wait_ge(corr_ps, t + 1)
                if t >= 2:
                    act.wait_ge(corr_built, t - 1)
                act.activation(TE[:, t % 2, 0:LAGS], tbank(("corr", t))[:, 0:LAGS], ACT.Copy).then_inc(even_copied, 1)

            def lag_exp(t):
                act.wait_ge(topped, t + 1)
                if t >= 1:
                    act.wait_ge(lag_diff, t)
                if t >= 2:
                    act.wait_ge(wf_done, t - 1)
                act.activation(E1[:, t % 2, :], CORR[:, t % 2, 0:D], ACT.Exp, bias=ngm[:, t % 2, :]).then_inc(lag_exps, 1)
                act.activation(E2[:], REP[:, t % 2, 0:D], ACT.Exp, bias=ngm[:, t % 2, :]).then_inc(lag_exps, 1)
                act.activation(es6[:, t % 2, :], T8[:, t % 2, 0:TOPK], ACT.Exp, bias=ngm[:, t % 2, :],
                               accum_out=ssum[:, t:t + 1]).then_inc(lag_exps, 1)

            def weights_hi(t):
                h = t // TH
                act.wait_ge(wt_ps, t + 1)
                act.activation(Shi[:, h, :, (t % TH) * P:(t % TH + 1) * P],
                               tbank(("wt", t))[:].rearrange("p (k r) -> p k r", k=KD), ACT.Copy).then_inc(wthi_done, 1)

            def product_hi(h):
                for part in range(2):
                    for j in range(2):
                        act.wait_ge(ysum, 4 * h + 2 * part + j + 1)
                        act.activation(Shi[:, h, 2 * part + j, :], SQ[:, 2 * j, :], ACT.Copy).then_inc(yhi_done, 1)

            def rows_hi(t):
                h = t // TH
                act.wait_ge(x1_ps, t + 1)
                act.activation(Shi[:, h, :, (t % TH) * P:(t % TH + 1) * P],
                               tbank(("x1", t))[:].rearrange("p (k r) -> p k r", k=KD), ACT.Copy).then_inc(x1hi_done, 1)

            def keys_out(kind, h, m):
                act.wait_ge(acc_full, gidx[(kind, h, m)] + 1)
                part = 1 if kind == "kc" else 0
                act.activation(KC[:, part, m, h * HR:(h + 1) * HR], acc_bank((kind, h, m))[:], ACT.Copy).then_inc(acc_act, 1)

            def queries_out(s, m):
                act.wait_ge(acc_full, gidx[("q", s, m)] + 1)
                if s >= 2:
                    act.wait_ge(scored, 4 * (s - 1))
                act.activation(QC[:, s % 2, :, m, :], acc_bank(("q", s, m))[:].rearrange("p (b r) -> p b r", r=S),
                               ACT.Copy).then_inc(acc_act, 1)

            hi("fwd")
            x_hi(0)
            hi("wk")
            x_hi(1)
            spectrum_out(0)
            hi("cx0")
            for t in range(TH):
                even_copy(t)
                if t in (1, 2):
                    lag_exp(t - 1)
            spectrum_out(1)
            hi("wv")
            for m in range(CH):
                keys_out("kc", 0, m)
            for t in range(TH, NT):
                lag_exp(t - 2)
                even_copy(t)
            hi("inv")
            for t in range(TH):
                weights_hi(t)
            act.wait_ge(acc_full, gidx[("vc", 0, TH - 1)] + 1)
            hi("cx1")
            lag_exp(NT - 2)
            lag_exp(NT - 1)
            product_hi(0)
            for m in range(CH):
                keys_out("kc", 1, m)
            for t in range(TH, NT):
                weights_hi(t)
            product_hi(1)
            act.wait_ge(prods, prods_count(1, 1))
            act.wait_ge(ylo_done, 8)
            act.wait_ge(dft_ps, 8)
            act.wait_ge(wdft_ps, 8)
            hi("wq0")
            for t in range(TH):
                rows_hi(t)
            for m in range(CH):
                keys_out("kx", 0, m)
            for m in range(CH):
                queries_out(0, m)
            act.wait_ge(inv_ps, NT)
            act.wait_ge(acc_full, gidx[("vc", 1, TH - 1)] + 1)
            hi("wo0")
            for t in range(TH, NT):
                rows_hi(t)
            for m in range(CH):
                keys_out("kx", 1, m)

            def exp_scores(n):
                act.wait_ge(max_ready, n + 1)
                if n >= 2:
                    act.wait_ge(pt_ps, n - 1)
                for u in range(4):
                    ins = act.activation(PX[:, n % 2, u, :], sc[n % 2][:, u * P:(u + 1) * P], ACT.Exp,
                                         bias=nb[:, n % 2, u:u + 1], scale=SCALE, accum_out=sm[:, n % 2, u:u + 1])
                ins.then_inc(exped, 1)

            def output_out(n):
                act.wait_ge(pv_ps, n + 1)
                if n >= 4:
                    act.wait_ge(otlo_done, n - 3)
                act.activation(OTF[0:HD, n % 4, :, :].rearrange("p g (b r) -> p b g r", r=S),
                               pv[n % 2][0:HD, :].rearrange("p (b g r) -> p b g r", g=G, r=S), ACT.Copy).then_inc(ot_read, 1)

            def output_hi(n):
                act.wait_ge(o_moved[n % 4], 48 * (n // 4 + 1))
                if n >= 4:
                    act.wait_ge(acc_full, gidx[("wo",) + divmod(n - 4, 4)] + 1)
                act.activation(OThi[:, n % 4], OTF[:, n % 4, 0:CH], ACT.Copy).then_inc(othi_done, 1)

            for it in range(NQ + 2):
                s, i = divmod(it, 4)
                if i == CH and s + 1 < NS:
                    queries_out(s + 1, i - 1)
                if it < NQ:
                    exp_scores(it)
                if it >= 2 and it != NQ + 1:
                    output_hi(it - 2)
                if i == 0 and s % 2 == 1 and s // 2 + 1 < KV:
                    act.wait_ge(acc_full, gidx[("q", s, CH - 1)] + 1)
                    hi(f"wq{s // 2 + 1}")
                if 1 <= i < CH and s + 1 < NS:
                    queries_out(s + 1, i - 1)
                if 1 <= it <= NQ:
                    output_out(it - 1)
                if i == 2 and s % 2 == 1 and s // 2 + 1 < KV:
                    v = s // 2 + 1
                    if v >= 2:
                        act.wait_ge(acc_full, gidx[("wo", 2 * (v - 2) + 1, TH - 1)] + 1)
                    hi(f"wo{v}")
                if it == 28:
                    act.wait_ge(acc_full, gidx[("q", NS - 1, CH - 1)] + 1)
                if it == 26:
                    act.wait_ge(acc_full, gidx[("wo", 2 * (KV - 2) + 1, TH - 1)] + 1)
                for kind in FFN_AT.get(it, ()):
                    hi(kind)

            def rows2_hi(t):
                act.wait_ge(x2_ps, t + 1)
                if t == TH:
                    act.wait_ge(ta_ps, 1)
                act.activation(X2hi[:, :, (t % TH) * P:(t % TH + 1) * P],
                               pv[t % 2][:].rearrange("p (k r) -> p k r", k=KD), ACT.Copy).then_inc(x2hi_done, 1)

            def fold_hi(t):
                act.wait_ge(xft_done, t + 1)
                act.activation(XFhi[:, t // TH, (t % TH) * P:(t % TH + 1) * P], XFt[:, t % 2, :], ACT.Copy).then_inc(xfhi_done, 1)

            def lora_out(h):
                act.wait_ge(ta_ps, h + 1)
                act.activation(TS[0:96, h, :], acc[0][0:96, :], ACT.Copy, scale=0.5).then_inc(tahi_done, 1)

            def lora2_out(h):
                act.wait_ge(a2_ps, NF * (h + 1))
                act.activation(T2S[0:96, h, :], acc[1][0:96, :], ACT.Copy, scale=0.5).then_inc(t2hi_done, 1)

            rows2_hi(0)
            rows2_hi(1)
            output_hi(NQ - 1)
            fold_hi(0)
            rows2_hi(2)
            fold_hi(1)
            rows2_hi(3)
            fold_hi(2)
            fold_hi(3)
            hi("bb1")
            lora_out(0)
            for g in range(2 * NF + 1):
                if g < 2 * NF:
                    m = FW[(g % NF) // 4]
                    act.wait_ge(gu_ps, g + 1)
                    if g >= 2:
                        act.wait_ge(h_done, g - 1)
                    act.activation(SG[0:m, g % 2, :], sc[g % 2][0:m, :], ACT.Silu).then_inc(silu_done, 1)
                if g >= 1:
                    p = g - 1
                    m = FW[(p % NF) // 4]
                    act.wait_ge(h_done, p + 1)
                    if p >= 2:
                        act.wait_ge(a2_ps, p - 1)
                    act.activation(HShi[0:m, p % 2, :], Hb[0:m, p % 4, :], ACT.Copy).then_inc(hhi_done, 1)
                if g >= 4 and g % 4 == 1 or g == 2 * NF:
                    j = (g - 1) // 4 - (g != 2 * NF)
                    m = FW[j % FC]
                    act.wait_ge(fold_done, 4 * (j + 1))
                    act.activation(HFhi[0:m, j // FC, j % FC, :], HF[0:m, j % 2, :], ACT.Copy).then_inc(hfhi_done, 1)
                if g in TURN_AT:
                    rows2_hi(TURN_AT[g])
                    fold_hi(TURN_AT[g])
                if g == LORA_AT:
                    lora_out(1)
                if g == NF + 1:
                    lora2_out(0)
            lora2_out(1)

        @block.gpsimd
        def _(_pool):
            pool = nc.gpsimd
            chain = [0]

            def link(ins):
                chain[0] += 1
                ins.then_inc(pch, 1)
                pool.wait_ge(pch, chain[0])

            def lo(kind):
                for n in range(count[kind]):
                    i = index[(kind, n)]
                    _, src, dhi, dlo = items[i]
                    pool.wait_ge(hi_done, i + 1)
                    raw = stg[:, i % 4, 0:src.shape[1]]
                    if dlo is not None:
                        pool.tensor_tensor(dlo, raw, dhi, ALU.subtract).then_inc(lo_done, 1)
                    else:
                        w = 4 if kind == "a13" else 2
                        d = dhi.rearrange("p (a c) -> p a c", c=32)[:, :, w:2 * w]
                        r = raw.rearrange("p (a c) -> p a c", c=32)[:, :, w:2 * w]
                        pool.tensor_tensor(d, r, d, ALU.subtract).then_inc(lo_done, 1)

            def x_lo(h):
                for k in range(4):
                    pool.wait_ge(xhi_done, 4 * h + k + 1)
                    pool.tensor_tensor(Slo[:, h, k, :], FOLD[:, k, :], Shi[:, h, k, :], ALU.subtract).then_inc(xlo_done, 1)

            def odd_power(h):
                pool.wait_ge(squared, 4 * (h + 1))
                pool.tensor_tensor(SQ[:, 2, :], SQ[:, 2, :], SQ[:, 3, :], ALU.add).then_inc(odd_sum, 1)

            def lag_weights(t):
                pool.wait_ge(lag_exps, 3 * t + 2)
                e = E1[:, t % 2, :]
                pool.tensor_tensor(e, e, E2[:], ALU.subtract).then_inc(lag_diff, 1)
                pool.wait_ge(lag_diff, t + 1)
                if t >= 4:
                    pool.wait_ge(wt_ps, t - 3)
                half = D // 2
                pool.tensor_tensor(WF[:, t % 4, 0:half], e[:, 0:half], e[:, half:D], ALU.add).then_inc(pch, 1)
                chain[0] += 1
                pool.wait_ge(pch, chain[0])
                pool.tensor_tensor(WF[:, t % 4, half:D], e[:, 0:half], e[:, half:D], ALU.subtract).then_inc(wf_done, 1)

            def product_sums(h):
                for part in range(2):
                    pool.wait_ge(prods, prods_count(h, part))
                    pool.tensor_tensor(SQ[:, 0, :], SQ[:, 0, :], SQ[:, 1, :], ALU.add).then_inc(ysum, 1)
                    pool.tensor_tensor(SQ[:, 2, :], SQ[:, 2, :], SQ[:, 3, :], ALU.subtract).then_inc(ysum, 1)
                    for j in range(2):
                        pool.wait_ge(yhi_done, 4 * h + 2 * part + j + 1)
                        pool.tensor_tensor(Slo[:, h, 2 * part + j, :], SQ[:, 2 * j, :], Shi[:, h, 2 * part + j, :],
                                           ALU.subtract).then_inc(ylo_done, 1)

            lo("fwd")
            x_lo(0)
            lo("wk")
            x_lo(1)
            odd_power(0)
            lo("cx0")
            pool.wait_ge(xlo_done, 8)
            lag_weights(0)
            lag_weights(1)
            odd_power(1)
            lo("wv")
            for t in range(2, TH + 1):
                lag_weights(t)
            lo("inv")
            pool.wait_ge(acc_full, gidx[("vc", 0, TH - 1)] + 1)
            lo("cx1")
            for t in range(TH + 1, NT):
                lag_weights(t)
            product_sums(0)
            product_sums(1)
            lo("wq0")
            lo("wo0")

            def normalise(n):
                pool.wait_ge(recips, n + 1)
                pool.tensor_tensor(PX[:, n % 2], PX[:, n % 2], rc[:, n % 2, :].unsqueeze(2).to_broadcast([P, 4, P]),
                                   ALU.mult).then_inc(p_normed, 1)

            for it in range(NQ + 2):
                s, i = divmod(it, 4)
                if it < NQ:
                    normalise(it)
                if i == 0 and s % 2 == 1 and s // 2 + 1 < KV:
                    lo(f"wq{s // 2 + 1}")
                if i == 2 and s % 2 == 1 and s // 2 + 1 < KV:
                    lo(f"wo{s // 2 + 1}")
                for kind in FFN_AT.get(it, ()):
                    if kind not in LO_BY_DVE:
                        lo(kind)

            def fold_lo(t):
                pool.wait_ge(xfhi_done, t + 1)
                h, cols = t // TH, slice((t % TH) * P, (t % TH + 1) * P)
                pool.tensor_tensor(XFlo[:, h, cols], XFt[:, t % 2, :], XFhi[:, h, cols], ALU.subtract).then_inc(xflo_done, 1)

            for t in range(TH):
                fold_lo(t)
            for g in range(2 * NF):
                j, q = divmod(g, 4)
                m = FW[j % FC]
                if q >= 1:
                    pool.wait_ge(h_done, g + 1)
                    dst = HF[0:m, j % 2, :]
                    if q == 1 and j >= 2:
                        pool.wait_ge(hflo_done, j - 1)
                    pool.wait_ge(fold_done, g if q > 1 else g - 1)
                    prev = dst if q > 1 else Hb[0:m, (g - 1) % 4, :]
                    pool.tensor_tensor(dst, prev, Hb[0:m, g % 4, :], ALU.add).then_inc(fold_done, 1 if q > 1 else 2)
                if g in TURN_AT:
                    fold_lo(TURN_AT[g])

        @block.vector
        def _(_dve):
            dve = nc.vector
            chain = [0]

            def link(ins):
                chain[0] += 1
                ins.then_inc(dch, 1)
                dve.wait_ge(dch, chain[0])

            def fold_x(h):
                dve.wait_ge(x_in[h], 16)
                for k in range(4):
                    if h == 1:
                        dve.wait_ge(xlo_done, k + 1)
                    j, op = k % 2, (ALU.add if k < 2 else ALU.subtract)
                    dve.tensor_tensor(FOLD[:, k, :], X[:, j, h, :], X[:, j + 2, h, :], op).then_inc(folded, 1)

            def build_corr(t):
                ps = tbank(("corr", t))
                dve.wait_ge(even_copied, t + 1)
                if t >= 2:
                    dve.wait_ge(lag_exps, 3 * (t - 1))
                c = CORR[:, t % 2, :]
                te = TE[:, t % 2, :]
                n = LAGS - 1
                link(dve.tensor_tensor(c[:, 0:LAGS], te[:, 0:LAGS], ps[:, 256:256 + LAGS], ALU.add))
                dve.tensor_tensor(c[:, 2 * n:n:-1], te[:, 0:n], ps[:, 256:256 + n], ALU.subtract).then_inc(corr_built, 1)
                dve.wait_ge(corr_built, t + 1)
                link(dve.tensor_copy(c[:, D - 1:2 * n:-1], c[:, 1:2 * n]))
                link(dve.max(T8[:, t % 2, :], c[:, 0:D]))
                link(dve.memset(T8[:, t % 2, TOPK:8], LOW))
                link(dve.tensor_scalar(ngm[:, t % 2, :], T8[:, t % 2, 0:1], -1.0, None, ALU.mult))
                dve.match_replace(REP[:, t % 2, 0:D + 2], T8[:, t % 2, :], c[:, 0:D + 2], LOW).then_inc(topped, 1)
                dve.wait_ge(topped, t + 1)

            def weights_lo(t):
                h = t // TH
                cols = slice((t % TH) * P, (t % TH + 1) * P)
                dve.wait_ge(wthi_done, t + 1)
                dve.tensor_tensor(Slo[:, h, :, cols], tbank(("wt", t))[:].rearrange("p (k r) -> p k r", k=KD),
                                  Shi[:, h, :, cols].bitcast(F32), ALU.subtract).then_inc(wtlo_done, 1)

            def products(h):
                for part in range(2):
                    re, im = dftb[2 * part], dftb[2 * part + 1]
                    xr, xi = X[:, 2 * part, h, :], X[:, 2 * part + 1, h, :]
                    dve.wait_ge(wdft_ps, 4 * h + 2 * part + 2)
                    if h == 0 and part == 0:
                        dve.wait_ge(corr_ps, NT)
                    else:
                        dve.wait_ge(ylo_done, 4 * h + 2 * part)
                    dve.tensor_tensor(SQ[:, 0, :], re[:], xr, ALU.mult).then_inc(prods, 1)
                    dve.tensor_tensor(SQ[:, 2, :], re[:], xi, ALU.mult).then_inc(prods, 1)
                    if part == 0:
                        dve.scalar_tensor_tensor(out=SQ[:, 1, :], in0=im[:], scalar=mask, in1=xi,
                                                 op0=ALU.mult, op1=ALU.mult).then_inc(prods, 1)
                        dve.scalar_tensor_tensor(out=SQ[:, 3, :], in0=im[:], scalar=mask, in1=xr,
                                                 op0=ALU.mult, op1=ALU.mult).then_inc(prods, 1)
                        dve.wait_ge(prods, 9 * h + 4)
                        dve.tensor_tensor(SQ[0:1, 2, :], im[0:1, :], xi[0:1, :], ALU.mult).then_inc(prods, 1)
                    else:
                        dve.tensor_tensor(SQ[:, 1, :], im[:], xi, ALU.mult).then_inc(prods, 1)
                        dve.tensor_tensor(SQ[:, 3, :], im[:], xr, ALU.mult).then_inc(prods, 1)

            def stats(t):
                link(dve.bn_stats(st6[:, t, :], rows[:, t, :]))
                link(dve.bn_aggr(mv[:, t, :], st6[:, t, :]))

            def combine(t):
                ps = tbank(("inv", t))
                dve.wait_ge(inv_ps, t + 1)
                dve.wait_ge(lag_exps, 3 * t + 3)
                link(dve.reciprocal(rsum[:, t:t + 1], ssum[:, t:t + 1]))
                link(dve.tensor_scalar(nrs[:, t:t + 1], rsum[:, t:t + 1], -1.0, None, ALU.mult))
                half = D // 2
                for j in range(2):
                    ins = dve.scalar_tensor_tensor(out=rows[:, t, j * half:(j + 1) * half], in0=ps[:, 0:half],
                                                   scalar=rsum[:, t:t + 1], in1=rows[:, t, j * half:(j + 1) * half],
                                                   op0=ALU.mult, op1=ALU.add)
                    link(ins)
                link(dve.scalar_tensor_tensor(out=rows[:, t, 0:half], in0=ps[:, half:D], scalar=rsum[:, t:t + 1],
                                              in1=rows[:, t, 0:half], op0=ALU.mult, op1=ALU.add))
                dve.scalar_tensor_tensor(out=rows[:, t, half:D], in0=ps[:, half:D], scalar=nrs[:, t:t + 1],
                                         in1=rows[:, t, half:D], op0=ALU.mult, op1=ALU.add).then_inc(combined, 1)
                dve.wait_ge(combined, t + 1)
                stats(t)

            def rstd(n):
                t0 = (n % 2) * TH
                link(dve.tensor_scalar(ve[:], mv[:, t0:t0 + TH, 1], EPS, None, ALU.add))
                link(dve.tensor_scalar(y0[:].bitcast(I32), ve[:].bitcast(I32), -0.5, RSQRT_BITS, ALU.mult, ALU.add))
                for _ in range(3):
                    link(dve.tensor_tensor(y1[:], y0[:], y0[:], ALU.mult))
                    link(dve.scalar_tensor_tensor(out=y2[:], in0=y1[:], scalar=-0.5, in1=ve[:], op0=ALU.mult, op1=ALU.mult))
                    link(dve.scalar_tensor_tensor(out=y0[:], in0=y2[:], scalar=1.5, in1=y0[:], op0=ALU.add, op1=ALU.mult))

            def normed(t):
                j = t % TH
                dve.tensor_scalar(rows[:, t, :], rows[:, t, :], mv[:, t, 0:1], y0[:, j:j + 1],
                                  ALU.subtract, ALU.mult).then_inc(normed_rows, 1)

            def layernorm(n):
                rstd(n)
                for j in range(TH):
                    normed((n % 2) * TH + j)

            def rows_lo(t):
                h = t // TH
                cols = slice((t % TH) * P, (t % TH + 1) * P)
                dve.wait_ge(x1hi_done, t + 1)
                dve.tensor_tensor(Slo[:, h, :, cols], tbank(("x1", t))[:].rearrange("p (k r) -> p k r", k=KD),
                                  Shi[:, h, :, cols].bitcast(F32), ALU.subtract).then_inc(x1lo_done, 1)

            def values_out(kind, h, t):
                dve.wait_ge(acc_full, gidx[(kind, h, t)] + 1)
                ps = acc_bank((kind, h, t))
                p0 = 64 if kind == "vc" else 0
                b = 2 * (h * TH + t)
                link(dve.tensor_copy(VB[p0:p0 + 64, b, :], ps[0:64, 0:KV * HD]))
                dve.tensor_copy(VB[p0:p0 + 64, b + 1, :], ps[64:128, 0:KV * HD]).then_inc(acc_dve, 1)

            for j in range(2):
                dve.memset(CORR[:, j, D:D + 2], LOW).then_inc(dch, 1)
            chain[0] += 2
            fold_x(0)
            fold_x(1)
            dve.wait_ge(dch, chain[0])
            for t in range(NT):
                if t == TH:
                    for j in range(TH):
                        pass
                build_corr(t)
                if t == NT - 1:
                    break
            for t in range(TH):
                values_out("vc", 0, t)
            for t in range(TH):
                weights_lo(t)
            dve.wait_ge(const_in, 16)
            dve.wait_ge(rows_in, 16)
            products(0)
            for t in range(TH):
                combine(t)
            for t in range(TH, NT):
                weights_lo(t)
            layernorm(0)
            products(1)
            for t in range(TH):
                values_out("vc", 1, t)
            for t in range(TH, NT):
                combine(t)
            for t in range(TH):
                rows_lo(t)
            layernorm(1)
            for t in range(TH):
                values_out("vx", 0, t)
            for t in range(TH, NT):
                rows_lo(t)
            for t in range(TH):
                values_out("vx", 1, t)

            def row_max(n):
                dve.wait_ge(scored, n + 1)
                if n >= 2:
                    dve.wait_ge(exped, n - 1)
                link(dve.tensor_reduce(mx[:, n % 2, :], sc[n % 2][:].rearrange("p (u k) -> p u k", u=4), AX.X, ALU.max))
                dve.tensor_scalar(nb[:, n % 2, :], mx[:, n % 2, :], -SCALE, None, ALU.mult).then_inc(max_ready, 1)

            def probs_out(n):
                dve.wait_ge(pt_ps, n + 1)
                if n >= 2:
                    dve.wait_ge(pv_ps, n - 1)
                dve.tensor_copy(PT[:, n % 2, :], pt[n % 2][:]).then_inc(pt_read, 1)

            def sum_recip(n):
                dve.wait_ge(exped, n + 1)
                if n >= 2:
                    dve.wait_ge(p_normed, n - 1)
                dve.reciprocal(rc[:, n % 2, :], sm[:, n % 2, :]).then_inc(recips, 1)

            def output_lo(n):
                dve.wait_ge(othi_done, n + 1)
                dve.tensor_tensor(OTlo[:, n % 4], OTF[:, n % 4, 0:CH], OThi[:, n % 4].bitcast(F32),
                                  ALU.subtract).then_inc(otlo_done, 1)

            def add_out(n):
                s, t = divmod(n, 4)
                h = s % 2
                dve.wait_ge(acc_full, gidx[("wo", s, t)] + 1)
                r = rows[:, h * TH + t, :]
                dve.tensor_tensor(r, acc_bank(("wo", s, t))[:], r, ALU.add).then_inc(acc_dve, 1)

            def measure(n):
                s, t = divmod(n, 4)
                dve.wait_ge(acc_dve, evac_count(("wo", s, t)))
                stats((s % 2) * TH + t)

            def lo(kind):
                for n in range(count[kind]):
                    i = index[(kind, n)]
                    src = items[i][1]
                    dve.wait_ge(hi_done, i + 1)
                    dve.wait_ge(lo_done, i)
                    part = items[i][2][32:64]
                    dve.tensor_tensor(part, stg[32:64, i % 4, 0:src.shape[1]], part.bitcast(F32), ALU.subtract).then_inc(lo_done, 1)

            unmeasured = []
            for it in range(NQ + 1):
                if it < NQ:
                    row_max(it)
                if 1 <= it:
                    probs_out(it - 1)
                for n in unmeasured:
                    measure(n)
                unmeasured = []
                if it < NQ:
                    sum_recip(it)
                if it >= 2:
                    output_lo(it - 2)
                for n in projected(it):
                    if n < NQ - 2:
                        add_out(n)
                        if n >= NQ - 8:
                            unmeasured.append(n)
                if it == NQ - 2:
                    rstd(2)
                if it == NQ - 1:
                    for t in range(TH):
                        normed(t)
                    lo("b2")
                if it == NQ:
                    lo("bb0")

            def rows2_lo(t):
                cols = slice((t % TH) * P, (t % TH + 1) * P)
                ps = pv[t % 2][:]
                dve.wait_ge(x2hi_done, t + 1)
                if t >= 2:
                    dve.wait_ge(xflo_done, t - 1)
                dve.tensor_reduce(XFt[:, t % 2, :], ps.rearrange("p (k r) -> p r k", k=KD), AX.X, ALU.add).then_inc(xft_done, 1)
                dve.tensor_tensor(X2lo[:, :, cols], ps.rearrange("p (k r) -> p k r", k=KD), X2hi[:, :, cols].bitcast(F32),
                                  ALU.subtract).then_inc(x2lo_done, 1)

            def add_down(t):
                dve.wait_ge(w2_ps, t + 1)
                r = rows[:, t, :]
                dve.tensor_tensor(r, pv[t % 2][:], r, ALU.add).then_inc(w2_read, 1)
                dve.wait_ge(w2_read, t + 1)
                stats(t)

            def lora_lo(h):
                dve.wait_ge(tahi_done, h + 1)
                dve.scalar_tensor_tensor(out=TS[64:96, h, :], in0=acc[0][64:96, :], scalar=0.5, in1=TS[64:96, h, :].bitcast(F32),
                                         op0=ALU.mult, op1=ALU.subtract).then_inc(talo_done, 1)

            def lora2_lo(h):
                dve.wait_ge(t2hi_done, h + 1)
                dve.scalar_tensor_tensor(out=T2S[64:96, h, :], in0=acc[1][64:96, :], scalar=0.5, in1=T2S[64:96, h, :].bitcast(F32),
                                         op0=ALU.mult, op1=ALU.subtract).then_inc(t2lo_done, 1)

            rows2_lo(0)
            add_out(NQ - 2)
            rows2_lo(1)
            output_lo(NQ - 1)
            rows2_lo(2)
            measure(NQ - 3)
            measure(NQ - 2)
            add_out(NQ - 1)
            rows2_lo(3)
            measure(NQ - 1)
            lo("bb1")
            rstd(3)
            lora_lo(0)
            for g in range(2 * NF + 1):
                if g < 2 * NF:
                    m = FW[(g % NF) // 4]
                    dve.wait_ge(silu_done, g + 1)
                    if g >= 4:
                        dve.wait_ge(fold_done, g - 3)
                        dve.wait_ge(hlo_done, g - 3)
                    dve.tensor_tensor(Hb[0:m, g % 4, :], pt[g % 2][0:m, :], SG[0:m, g % 2, :], ALU.mult).then_inc(h_done, 1)
                if g >= 1:
                    p = g - 1
                    m = FW[(p % NF) // 4]
                    dve.wait_ge(hhi_done, p + 1)
                    dve.tensor_tensor(HSlo[0:m, p % 2, :], Hb[0:m, p % 4, :], HShi[0:m, p % 2, :].bitcast(F32),
                                      ALU.subtract).then_inc(hlo_done, 1)
                if g >= 4 and g % 4 == 1 or g == 2 * NF:
                    j = (g - 1) // 4 - (g != 2 * NF)
                    m = FW[j % FC]
                    dve.wait_ge(hfhi_done, j + 1)
                    dve.tensor_tensor(HFlo[0:m, j // FC, j % FC, :], HF[0:m, j % 2, :],
                                      HFhi[0:m, j // FC, j % FC, :].bitcast(F32), ALU.subtract).then_inc(hflo_done, 1)
                if g in TURN_AT:
                    rows2_lo(TURN_AT[g])
                if g < TH:
                    normed(TH + g)
                if g == LORA_AT:
                    lora_lo(1)
                if g == NF + 1:
                    lora2_lo(0)
                if g in DOWN_AT:
                    add_down(DOWN_AT[g])
                if g == 2 * NF - 2:
                    rstd(4)
                if g >= 2 * NF - 1:
                    normed(0 if g < 2 * NF else 1)
            lora2_lo(1)
            normed(2)
            normed(3)
            for t in range(TH, NT):
                add_down(t)
            layernorm(5)


def _kernel_inputs(np_, inp):
    def t3(a):
        return np_.ascontiguousarray(a.T.reshape(-1, P, a.shape[0]).transpose(1, 0, 2))

    x = np_.asarray(inp["x"]).reshape(ROWS, D)
    c = np_.asarray(inp["ctx_4096"]).reshape(ROWS, D)
    order = np_.concatenate([np_.concatenate([np_.arange(HD) + HD * m, 3 * HD + 32 * m + np_.arange(32)]) for m in range(CH)])
    wq = np_.asarray(inp["L0_xattn_Wq"]).reshape(KV, G * HD, D)[:, order]
    wk = np_.asarray(inp["L0_xattn_Wk"])[order]
    wv = np_.asarray(inp["L0_xattn_Wv"])
    wo = np_.asarray(inp["L0_xattn_Wo"]).T.reshape(KV, G * HD, D)[:, order]
    d = {
        "xT": t3(x), "xN": np_.ascontiguousarray(x.reshape(NT, P, D).transpose(1, 0, 2)), "ctxT": t3(c),
        "wqT": np_.stack([t3(wq[v]) for v in range(KV)]), "wkT": t3(wk), "wvT": t3(wv),
        "woT": np_.stack([np_.ascontiguousarray(wo[v].reshape(CH, P, D).transpose(1, 0, 2)) for v in range(KV)]),
    }

    def hidden(a):
        o = np_.zeros((a.shape[1], 4, FQP), a.dtype)
        o[:, :, :FQ] = a.T.reshape(-1, 4, FQ)
        return o.reshape(a.shape[1], 4 * FQP)

    d["w1T"] = hidden(np_.asarray(inp["L0_ffn_w1q"]))
    d["w3T"] = hidden(np_.asarray(inp["L0_ffn_w3q"]))
    w2 = np_.asarray(inp["L0_ffn_w2q"])
    w2p = np_.zeros((FC * P, D), w2.dtype)
    w2p[:FQ] = w2.T
    d["w2T"] = np_.ascontiguousarray(w2p.reshape(FC, P, D).transpose(1, 0, 2))
    a1, a3, a2 = (np_.asarray(inp["L0_ffn_" + n]) for n in ("a1", "a3", "a2"))
    ap = np_.zeros((P, KD, 96), a1.dtype)
    for j in range(3):
        for r in range(2):
            ap[:, :, 32 * j + 4 * r:32 * j + 4 * r + 2] = t3(a1)
            ap[:, :, 32 * j + 4 * r + 2:32 * j + 4 * r + 4] = t3(a3)
    d["a13"] = ap
    h2 = hidden(a2.T).reshape(2, 4, FQP)
    a2p = np_.zeros((P, NF, 96), a2.dtype)
    for n in range(NF):
        cc, q = divmod(n, 4)
        part = h2[:, q, cc * P:cc * P + FW[cc]].T
        for j in range(3):
            for r in range(2):
                a2p[:FW[cc], n, 32 * j + 2 * r:32 * j + 2 * r + 2] = part
    d["a2"] = a2p
    b1, b3, bd = (np_.asarray(inp["L0_ffn_" + n]) for n in ("b1", "b3", "b2"))
    bp = np_.zeros((96, 2, 4 * FQP), b1.dtype)
    b2p = np_.zeros((96, D), bd.dtype)
    for j in range(3):
        for r in range(2):
            bp[32 * j + 4 * r:32 * j + 4 * r + 2, 0] = hidden(b1)
            bp[32 * j + 4 * r + 2:32 * j + 4 * r + 4, 1] = hidden(b3)
            b2p[32 * j + 2 * r:32 * j + 2 * r + 2] = bd.T
    d["bb"] = bp.reshape(96, 2 * 4 * FQP)
    d["b2"] = b2p
    d["fwd"], d["inv"], d["ctab"] = dft_tables()
    consts = np_.ones((P, P + 1), np_.float32)
    consts[:, :P] = np_.eye(P, dtype=np_.float32)
    consts[0, P] = 0.0
    d["consts"] = consts
    return d


def kernel(**inputs):
    import concourse.bacc as _bacc
    from concourse.bass_utils import run_bass_kernel_spmd as _run

    nc = _bacc.Bacc("TRN2", target_bir_lowering=False, num_devices=1)
    arrays, args = {}, []
    for name, a in _kernel_inputs(np, inputs).items():
        a = np.ascontiguousarray(a)
        arrays[f"in_{name}"] = a
        args.append(nc.dram_tensor(f"in_{name}", a.shape, mybir.dt.from_np(a.dtype), kind="ExternalInput").ap())
    args.append(nc.dram_tensor("out_rows", (ROWS, D), F32, kind="ExternalOutput").ap())
    decoder_layer(nc, *args)
    r = _run(nc, [arrays], core_ids=[0])
    return r.results[0]["out_rows"].reshape(B, S, D)
```

```python
from contextlib import ExitStack

import numpy as np

import concourse.bass as bass
from concourse import mybir

F32 = mybir.dt.float32
F32R = mybir.dt.float32r
I32 = mybir.dt.int32
ALU = mybir.AluOpType
ACT = mybir.ActivationFunctionType
AX = mybir.AxisListType

P = 128
B, S, D = 16, 64, 512
ROWS = B * S
NT = ROWS // P
HR = ROWS // 2
TH = NT // 2
KD = D // P
H, KV, HD = 16, 4, 96
G = H // KV
CH = G * HD // P
F = 1376
FQ = F // 4
FC = 3
FW = [128, 128, 96]
FQP = sum(FW)
NF = 4 * FC
SCALE = float(np.float32(1.0) / np.sqrt(np.float32(HD)))
EPS = 1e-5
RSQRT_BITS = float(0x5F3759DF)
TOPK = 6
LOW = -3.0e38
LAGS = D // 4 + 1
W = 512


def dft_tables():
    g = np.arange(P)
    j = np.arange(D // 2)
    even = 2 * np.pi * np.outer(j, 2 * g) / D
    odd = 2 * np.pi * np.outer(j, 2 * g + 1) / D
    ere, eim, ore, oim = np.cos(even), -np.sin(even), np.cos(odd), -np.sin(odd)
    eim[:, 0] = (-1.0) ** j
    fwd = np.stack([np.concatenate([ere, eim], 1)[:P], np.concatenate([ere, eim], 1)[P:],
                    np.concatenate([ore, oim], 1)[:P], np.concatenate([ore, oim], 1)[P:]], 1)
    weight = np.full((P, 1), 2.0)
    weight[0] = 1.0
    inv = np.stack([ere.T * weight, eim.T * weight, ore.T * 2.0, oim.T * 2.0], 1) / D
    n = np.arange(LAGS)
    ce = np.cos(2 * np.pi * np.outer(2 * g, n) / D) * weight
    ci = np.cos(2 * np.pi * np.outer(2 * g, n) / D) * weight
    ci[0] = (-1.0) ** n
    co = np.cos(2 * np.pi * np.outer(2 * g + 1, n) / D) * 2.0
    co[:, LAGS - 1] = 0.0
    corr = np.stack([ce, ci, co], 1) / D
    return fwd.astype(np.float32), inv.astype(np.float32), corr.astype(np.float32)


def decoder_layer(nc, xT, xN, ctxT, wqT, wkT, wvT, woT, w1T, w3T, w2T, a13, a2, bb, b2, fwd, inv, ctab, consts, out):
    ctx = ExitStack()
    with ctx:
        arena = ctx.enter_context(nc.sbuf_tensor("arena", [P, 212800 // 4], F32))
        base = nc.sbuf_base - 212800

        def at(name, offset, shape, dt=F32):
            return nc.alloc_sbuf_tensor_at(name, [P] + shape, dt, offset=base + offset)

        oROW, oSTG, oKC, oVB, oS, oU = 0, 16384, 24576, 57344, 81920, 114688
        rows = at("rows", oROW, [NT, D])
        stg = at("stg", oSTG, [4, W])
        KC = at("KC", oKC, [2, KV, ROWS])
        VB = at("VB", oVB, [B, KV * HD])
        Shi = at("Shi", oS, [2, KD, HR], F32R)
        Slo = at("Slo", oS + 16384, [2, KD, HR], F32R)
        X = at("X", oU, [KD, 2, HR])
        SQ = at("SQ", oU + 16384, [KD, HR])
        DThi = at("DThi", oU + 24576, [KD, 256], F32R)
        DTlo = at("DTlo", oU + 28672, [KD, 256], F32R)
        IThi = at("IThi", oU + 32768, [KD, 256], F32R)
        ITlo = at("ITlo", oU + 36864, [KD, 256], F32R)
        CT = at("CT", oU + 40960, [3, LAGS])
        CXhi = at("CXhi", oU + 42560, [KD, HR], F32R)
        CXlo = at("CXlo", oU + 50752, [KD, HR], F32R)
        WKhi = at("WKhi", oU + 58944, [KD, KV * HD], F32R)
        WKlo = at("WKlo", oU + 65088, [KD, KV * HD], F32R)
        WVhi = at("WVhi", oU + 71232, [KD, KV * HD], F32R)
        WVlo = at("WVlo", oU + 77376, [KD, KV * HD], F32R)
        FOLD = at("FOLD", oU + 83520, [KD, HR])
        WF = at("WF", oU + 83520, [4, D])
        CORR = at("CORR", oKC, [2, D + 8])
        REP = at("REP", oKC + 4160, [2, D + 8])
        E1 = at("E1", oKC + 8320, [2, D])
        E2 = at("E2", oKC + 12416, [D])
        TE = at("TE", oKC + 14464, [2, LAGS + 7])
        QC = at("QC", oU, [2, 8, G, S])
        WQhi = at("WQhi", oU + 16384, [KD, G * HD], F32R)
        WQlo = at("WQlo", oU + 22528, [KD, G * HD], F32R)
        WOhi = at("WOhi", oU + 28672, [2, CH, D], F32R)
        WOlo = at("WOlo", oU + 40960, [2, CH, D], F32R)
        OTF = at("OTF", oU + 53248, [4, G, P])
        OThi = at("OThi", oU + 61440, [4, CH, P], F32R)
        OTlo = at("OTlo", oU + 67584, [4, CH, P], F32R)
        PX = at("PX", oU + 83520, [2, 4, P])
        PT = at("PT", oU + 87616, [2, W])
        W1hi = at("W1hi", oS, [2 * 4 * FQP], F32R)
        W1lo = at("W1lo", oS + 11264, [2 * 4 * FQP], F32R)
        A2S = at("A2S", oU + 73728, [NF, 96], F32R)
        A13S = at("A13S", oU + 78336, [KD, 96], F32R)
        B2S = at("B2S", oU + 79872, [D], F32R)
        BS = at("BS", oU + 16384, [2 * 4 * FQP], F32R)
        W2hi = at("W2hi", oU + 28672, [FC, D], F32R)
        W2lo = at("W2lo", oU + 40960, [FC, D], F32R)
        X2hi = at("X2hi", oKC, [KD, HR], F32R)
        X2lo = at("X2lo", oKC + 8192, [KD, HR], F32R)
        XFhi = at("XFhi", oKC + 16384, [2, HR], F32R)
        XFlo = at("XFlo", oKC + 20480, [2, HR], F32R)
        TS = at("TS", oKC + 24576, [2, HR], F32R)
        T2S = at("T2S", oKC + 28672, [2, HR], F32R)
        Hb = at("Hb", oVB, [4, HR])
        HShi = at("HShi", oVB + 8192, [2, HR], F32R)
        HSlo = at("HSlo", oVB + 12288, [2, HR], F32R)
        XFt = at("XFt", oVB + 16384, [2, P])
        HFhi = at("HFhi", oU, [2, FC, HR], F32R)
        HFlo = at("HFlo", oU + 53248, [2, FC, HR], F32R)
        SG = at("SG", oS + 22528, [2, HR])
        HF = at("HF", oS + 26624, [2, HR])
        oC = oU + 91712
        cst = at("cst", oC, [P + 1])
        T8 = at("T8", oC + 544, [2, 8])
        ngm = at("ngm", oC + 608, [2, 1])
        es6 = at("es6", oC + 640, [2, TOPK])
        ssum = at("ssum", oC + 704, [NT])
        rsum = at("rsum", oC + 736, [NT])
        nrs = at("nrs", oC + 768, [NT])
        st6 = at("st6", oC + 800, [NT, 6])
        mv = at("mv", oC + 992, [NT, 2])
        ve = at("ve", oC + 1056, [TH])
        y0 = at("y0", oC + 1088, [TH])
        y1 = at("y1", oC + 1120, [TH])
        y2 = at("y2", oC + 1152, [TH])
        yo = at("yo", oC + 1184, [TH])
        shift = at("shift", oC + 1344, [2, TH])
        mx = at("mx", oC + 1216, [2, 4])
        nb = at("nb", oC + 1248, [2, 4])
        sm = at("sm", oC + 1280, [2, 4])
        rc = at("rc", oC + 1312, [2, 4])
        ident = cst[:, 0:P]
        mask = cst[:, P:P + 1]

        def bank(name):
            return ctx.enter_context(nc.psum_tensor(name, [P, W], F32))

        acc = [bank("acc0"), bank("acc1")]
        sc = [bank("sc0"), bank("sc1")]
        pt = [bank("pt0"), bank("pt1")]
        pv = [bank("pv0"), bank("pv1")]
        dftb = [sc[0], sc[1], pt[0], pt[1]]

        def sem(name):
            return ctx.enter_context(nc.semaphore(name))

        stage_in = [sem(f"stage_in{i}") for i in range(4)]
        hi_done, lo_done = sem("hi_done"), sem("lo_done")
        x_in = [[sem(f"x_in{h}{j}") for j in range(2)] for h in range(2)]
        rows_in, const_in, ctab_in = sem("rows_in"), sem("const_in"), sem("ctab_in")
        folded, xhi_done, xlo_done = sem("folded"), sem("xhi_done"), sem("xlo_done")
        dft_ps, x_copied, squared, odd_sum = sem("dft_ps"), sem("x_copied"), sem("squared"), sem("odd_sum")
        corr_ps, even_copied, corr_built, topped = sem("corr_ps"), sem("even_copied"), sem("corr_built"), sem("topped")
        lag_exps, lag_diff, wf_done = sem("lag_exps"), sem("lag_diff"), sem("wf_done")
        wt_ps, wthi_done, wtlo_done = sem("wt_ps"), sem("wthi_done"), sem("wtlo_done")
        wdft_ps, prods = sem("wdft_ps"), sem("prods")
        ysum, yhi_done, ylo_done = sem("ysum"), sem("yhi_done"), sem("ylo_done")
        ydiff, ylo2_done = sem("ydiff"), sem("ylo2_done")
        inv_ps, combined, normed_rows = sem("inv_ps"), sem("combined"), sem("normed_rows")
        x1_ps, x1hi_done, x1lo_done = sem("x1_ps"), sem("x1hi_done"), sem("x1lo_done")
        acc_full, acc_act, acc_dve = sem("acc_full"), sem("acc_act"), sem("acc_dve")
        k_moved, k_moved_last, val_half = sem("k_moved"), sem("k_moved_last"), sem("val_half")
        q_moved = [sem("q_moved0"), sem("q_moved1")]
        o_moved = [sem(f"o_moved{i}") for i in range(4)]
        scored, max_ready, exped, recips, p_normed = (
            sem("scored"), sem("max_ready"), sem("exped"), sem("recips"), sem("p_normed"))
        pt_ps, pt_read, pv_ps, ot_read = sem("pt_ps"), sem("pt_read"), sem("pv_ps"), sem("ot_read")
        othi_done, otlo_done = sem("othi_done"), sem("otlo_done")
        x2_ps, x2hi_done, x2lo_done, xft_done, xfhi_done, xflo_done = (
            sem("x2_ps"), sem("x2hi_done"), sem("x2lo_done"), sem("xft_done"), sem("xfhi_done"), sem("xflo_done"))
        ta_ps, tahi_done, talo_done = sem("ta_ps"), sem("tahi_done"), sem("talo_done")
        gu_ps, silu_done, h_done, hhi_done, hlo_done = (
            sem("gu_ps"), sem("silu_done"), sem("h_done"), sem("hhi_done"), sem("hlo_done"))
        fold_done, hfhi_done, hflo_done, a2_ps = sem("fold_done"), sem("hfhi_done"), sem("hflo_done"), sem("a2_ps")
        t2hi_done, t2lo_done = sem("t2hi_done"), sem("t2lo_done")
        w2_ps, w2_read, stored = sem("w2_ps"), sem("w2_read"), sem("stored")
        shifts, normed_act = sem("shifts"), sem("normed_act")
        dch, pch = sem("dve_chain"), sem("pool_chain")

        def flat(t):
            return t.rearrange("p a b -> p (a b)")

        items = []
        index = {}

        def add(kind, n, src, hi, lo):
            index[(kind, n)] = len(items)
            items.append((kind, src, hi, lo))

        def add_flat(kind, dram, hi, lo, width, step=W):
            for n in range((width + step - 1) // step):
                a, b = n * step, min(width, (n + 1) * step)
                add(kind, n, dram[:, a:b], hi[:, a:b], lo[:, a:b])

        add_flat("fwd", flat(fwd), flat(DThi[:]), flat(DTlo[:]), KD * 256)
        add_flat("wk", flat(wkT), flat(WKhi[:]), flat(WKlo[:]), KD * KV * HD)
        for c in range(KD):
            add("cx0", c, ctxT[:, c, 0:HR], CXhi[:, c, :], CXlo[:, c, :])
        add_flat("wv", flat(wvT), flat(WVhi[:]), flat(WVlo[:]), KD * KV * HD)
        add_flat("inv", flat(inv), flat(IThi[:]), flat(ITlo[:]), KD * 256)
        for c in range(KD):
            add("cx1", c, ctxT[:, c, HR:ROWS], CXhi[:, c, :], CXlo[:, c, :])
        add_flat("wq0", flat(wqT[0]), flat(WQhi[:]), flat(WQlo[:]), KD * G * HD)
        add_flat("wo0", flat(woT[0]), flat(WOhi[:, 0]), flat(WOlo[:, 0]), CH * D)
        for v in range(1, KV):
            add_flat(f"wq{v}", flat(wqT[v]), flat(WQhi[:]), flat(WQlo[:]), KD * G * HD)
            add_flat(f"wo{v}", flat(woT[v]), flat(WOhi[:, v % 2]), flat(WOlo[:, v % 2]), CH * D)
        NW1 = 4 * FQP
        add("a13", 0, flat(a13), flat(A13S[:]), None)
        for n in range(3):
            add("a2", n, flat(a2[:, 4 * n:4 * n + 4]), flat(A2S[:, 4 * n:4 * n + 4]), None)
        add_flat("w2", flat(w2T), flat(W2hi[:]), flat(W2lo[:]), FC * D)
        for w, dram in ((0, w1T), (1, w3T)):
            for n in range(3):
                a, b = n * W, min(NW1, (n + 1) * W)
                add(f"w1{w}", n, dram[:, a:b], W1hi[:, w * NW1 + a:w * NW1 + b], W1lo[:, w * NW1 + a:w * NW1 + b])
        add("b2", 0, b2, B2S[0:96], None)
        for n in range(6):
            a, b = n * W, min(2 * NW1, (n + 1) * W)
            add(f"bb{n // 4}", n % 4, bb[:, a:b], BS[0:96, a:b], None)
        TURN_AT = {2: 4, 4: 5, 6: 6, 8: 7}
        LORA_AT = 10
        DOWN_AT = {NF + 4: 0, NF + 6: 1, NF + 8: 2}
        count = {}
        for kind, n in index:
            count[kind] = count.get(kind, 0) + 1

        PIECES_AT = {}
        for v in range(1, KV):
            PIECES_AT[8 * v - 5] = [f"wq{v}"]
            PIECES_AT[8 * v - 2] = [f"wo{v}"]
        FFN_AT = {24: ["a13", "a2"], 26: ["w2"], 28: ["w10"], 29: ["w11"], 30: ["b2"]}
        PIECES_AT.update(FFN_AT)
        OUT_BY_ACT = [0, 1, 2, 3, 6, 7]
        STORE_ORDER = [0, 1, 2, 3, 4, 6, 5, 7]
        LO_BY_DVE = ("b2",)

        def last_item(kind):
            return index[(kind, count[kind] - 1)] + 1

        groups = []
        groups += [("kc", 0, m) for m in range(CH)] + [("vc", 0, t) for t in range(TH)]
        groups += [("kc", 1, m) for m in range(CH)] + [("vc", 1, t) for t in range(TH)]
        groups += [("kx", 0, m) for m in range(CH)] + [("vx", 0, t) for t in range(TH)]
        groups += [("q", 0, m) for m in range(CH)]
        groups += [("kx", 1, 0)]
        REST_AT = {0: [("kx", 1, 1), ("kx", 1, 2)], 1: [("vx", 1, 0), ("vx", 1, 1)], 2: [("vx", 1, 2), ("vx", 1, 3)]}
        NS = 2 * KV
        NQ = NS * 4

        def projected(it):
            if it < NQ:
                return [it - 3] if it >= 3 else []
            return [NQ - 3, NQ - 2] if it == NQ else [NQ - 1]

        for it in range(NQ + 2):
            s, i = divmod(it, 4)
            if i >= 1 and s + 1 < NS:
                groups.append(("q", s + 1, i - 1))
            groups += REST_AT.get(it, [])
            groups += [("wo",) + divmod(n, 4) for n in projected(it)]
        gidx = {g: n for n, g in enumerate(groups)}
        by_act = {"kc", "kx", "q", "vc", "vx"}

        def evac_count(g):
            act = g[0] in by_act
            return sum((x[0] in by_act) == act for x in groups[:gidx[g] + 1])

        def acc_bank(g):
            return acc[gidx[g] % 2]

        tuses = [("corr", t) for t in range(TH)]
        for t in range(TH):
            tuses += [("wt", t), ("corr", TH + t)]
        tuses += [("wt", t) for t in range(TH, NT - 1)] + [("inv", t) for t in range(TH - 1)]
        tuses += [("wt", NT - 1), ("inv", TH - 1)]
        tuses += [("x1", t) for t in range(TH)] + [("inv", t) for t in range(TH, NT)] + [("x1", t) for t in range(TH, NT)]
        tidx = {u: n for n, u in enumerate(tuses)}

        def tbank(u):
            return pv[tidx[u] % 2]

        read_by = {"corr": corr_built, "wt": wtlo_done, "inv": combined, "x1": x1lo_done}

        def down_bank(t):
            return (pv + sc)[t - TH] if t >= TH else pv[t % 2]

        def prods_count(h, part):
            return 9 * h + (5 if part == 0 else 9)

        block = ctx.enter_context(nc.Block())

        @block.sync
        def _(sp):
            loaded = [0]

            def load_to(end):
                for i in range(loaded[0], min(end, len(items))):
                    loaded[0] = i + 1
                    if i >= 4:
                        sp.wait_ge(lo_done, i - 3)
                    src = items[i][1]
                    sp.dma_start(stg[0:src.shape[0], i % 4, 0:src.shape[1]], src).then_inc(stage_in[i % 4], 16)

            def load(kind):
                load_to(last_item(kind))

            def load_x(h, j):
                sp.dma_start(X[:, j::2, h, :], xT[:, j::2, h * HR:(h + 1) * HR]).then_inc(x_in[h][j], 16)

            load_x(0, 0)
            load_to(1)
            load_x(0, 1)
            load_to(4)
            load_x(1, 0)
            load_x(1, 1)
            load("wk")
            sp.dma_start(CT[:], ctab).then_inc(ctab_in, 16)
            sp.dma_start(cst[:], consts).then_inc(const_in, 16)
            load("cx0")
            load("wv")
            sp.dma_start(rows[:], xN).then_inc(rows_in, 16)
            load("inv")
            load("cx1")

            def move_k(part, h, done):
                for m in range(CH):
                    kind = ("kx", "kc")[part]
                    sp.wait_ge(acc_act, evac_count((kind, h, m)))
                    sp.dma_start(KC[32 * m:32 * m + 32, part, 3, h * HR:(h + 1) * HR],
                                 KC[96:128, part, m, h * HR:(h + 1) * HR]).then_inc(done, 16)

            def move_q(s, m):
                sp.wait_ge(acc_act, evac_count(("q", s, m)))
                sp.dma_start(QC[32 * m:32 * m + 32, s % 2, :, 3, :],
                             QC[96:128, s % 2, :, m, :]).then_inc(q_moved[s % 2], 16)

            move_k(1, 0, k_moved)
            move_k(1, 1, k_moved)
            load("wq0")
            move_k(0, 0, k_moved)
            for m in range(CH):
                move_q(0, m)
            load("wo0")
            move_k(0, 1, k_moved_last)
            taken = last_item("wo0")
            for it in range(NQ + 2):
                s, i = divmod(it, 4)
                if i >= 1 and s + 1 < NS:
                    move_q(s + 1, i - 1)
                for kind in PIECES_AT.get(it - 1, ()):
                    taken = last_item(kind)
                if it == NQ + 1:
                    taken = len(items)
                load_to(taken + 4)
                if 1 <= it <= NQ:
                    n = it - 1
                    sp.wait_ge(ot_read, n + 1)
                    for c in range(CH):
                        sp.dma_start(OTF[96:128, n % 4, c, :], OTF[32 * c:32 * c + 32, n % 4, 3, :]).then_inc(o_moved[n % 4], 16)
            for t in STORE_ORDER:
                if t in OUT_BY_ACT:
                    sp.wait_ge(normed_act, OUT_BY_ACT.index(t) + 1)
                else:
                    sp.wait_ge(normed_rows, 2 * NT + t - TH + 1)
                sp.dma_start(out[t * P:(t + 1) * P, :], rows[:, t, :]).then_inc(stored, 16)
            sp.wait_ge(stored, 16 * NT)

        @block.tensor
        def _(_pe):
            pe = nc.tensor

            def mm3(o, lhs, rhs, first, last):
                pe.matmul(o, lhs[0], rhs[0], start=first, stop=False)
                pe.matmul(o, lhs[0], rhs[1], start=False, stop=False)
                return pe.matmul(o, lhs[1], rhs[0], start=False, stop=last)

            def spectrum(h, done, ready, read):
                for m in range(4):
                    part, im = divmod(m, 2)
                    read(m)
                    for k in range(2):
                        kk = 2 * part + k
                        ready(kk)
                        ins = mm3(dftb[m][:], (DThi[:, kk, im * P:(im + 1) * P], DTlo[:, kk, im * P:(im + 1) * P]),
                                  (Shi[:, h, kk, :], Slo[:, h, kk, :]), k == 0, k == 1)
                    ins.then_inc(done, 1)

            def row_spectrum(h):
                def ready(kk):
                    if h == 0:
                        pe.wait_ge(lo_done, index[("fwd", kk // 2)] + 1)
                    pe.wait_ge(xlo_done, 4 * h + kk + 1)

                def read(m):
                    if h == 1:
                        pe.wait_ge(squared, m + 1)
                        pe.wait_ge(x_copied, m + 1)

                spectrum(h, dft_ps, ready, read)

            def begin_tbank(u):
                n = tidx[u]
                if n >= 2:
                    kind, t = tuses[n - 2]
                    pe.wait_ge(read_by[kind], t + 1)
                return pv[n % 2]

            def correlate(t):
                h = t // TH
                ps = begin_tbank(("corr", t))
                pe.wait_ge(odd_sum, h + 1)
                cols = slice((t % TH) * P, (t % TH + 1) * P)
                pe.matmul(ps[:, 0:LAGS], SQ[:, 0, cols], CT[:, 0, :], start=True, stop=False)
                pe.matmul(ps[:, 0:LAGS], SQ[:, 1, cols], CT[:, 1, :], start=False, stop=True)
                pe.matmul(ps[:, 256:256 + LAGS], SQ[:, 2, cols], CT[:, 2, :], start=True, stop=True).then_inc(corr_ps, 1)

            def turn_weights(t):
                ps = begin_tbank(("wt", t))
                pe.wait_ge(wf_done, t + 1)
                for k in range(KD):
                    ins = pe.transpose(ps[:, k * P:(k + 1) * P], WF[:, t % 4, k * P:(k + 1) * P], ident)
                ins.then_inc(wt_ps, 1)

            def weight_spectrum(h):
                def ready(kk):
                    pe.wait_ge(wtlo_done, TH * (h + 1))

                def read(m):
                    if h == 0:
                        pe.wait_ge(squared, 8)
                        pe.wait_ge(x_copied, 8)
                    else:
                        pe.wait_ge(prods, prods_count(0, m // 2))

                spectrum(h, wdft_ps, ready, read)

            def invert(t):
                h = t // TH
                ps = begin_tbank(("inv", t))
                pe.wait_ge(ylo_done, 2 * (h + 1))
                pe.wait_ge(ylo2_done, 2 * (h + 1))
                pe.wait_ge(lo_done, last_item("inv"))
                cols = slice((t % TH) * P, (t % TH + 1) * P)
                for part in range(2):
                    for k in range(2):
                        kk = 2 * part + k
                        ins = mm3(ps[:, part * 256:(part + 1) * 256], (Shi[:, h, kk, cols], Slo[:, h, kk, cols]),
                                  (IThi[:, kk, :], ITlo[:, kk, :]), k == 0, k == 1)
                ins.then_inc(inv_ps, 1)

            def turn_rows(t):
                ps = begin_tbank(("x1", t))
                pe.wait_ge(normed_rows, t + 1)
                for k in range(KD):
                    ins = pe.transpose(ps[:, k * P:(k + 1) * P], rows[:, t, k * P:(k + 1) * P], ident)
                ins.then_inc(x1_ps, 1)

            def begin_acc(g):
                n = gidx[g]
                if n >= 2:
                    prev = groups[n - 2]
                    pe.wait_ge(acc_act if prev[0] in by_act else acc_dve, evac_count(prev))
                return acc[n % 2]

            def keys(kind, h, m):
                ps = begin_acc((kind, h, m))
                ops = (CXhi, CXlo) if kind == "kc" else (Shi[:, h], Slo[:, h])
                for k in range(KD):
                    ins = mm3(ps[:], (WKhi[:, k, m * P:(m + 1) * P], WKlo[:, k, m * P:(m + 1) * P]),
                              (ops[0][:, k, :], ops[1][:, k, :]), k == 0, k == KD - 1)
                ins.then_inc(acc_full, 1)

            def values(kind, h, t):
                ps = begin_acc((kind, h, t))
                ops = (CXhi, CXlo) if kind == "vc" else (Shi[:, h], Slo[:, h])
                for k in range(KD):
                    ins = mm3(ps[:, 0:KV * HD], (ops[0][:, k, t * P:(t + 1) * P], ops[1][:, k, t * P:(t + 1) * P]),
                              (WVhi[:, k, :], WVlo[:, k, :]), k == 0, k == KD - 1)
                ins.then_inc(acc_full, 1)

            def queries(s, m):
                v, h = divmod(s, 2)
                ps = begin_acc(("q", s, m))
                pe.wait_ge(lo_done, last_item(f"wq{v}"))
                for k in range(KD):
                    ins = mm3(ps[:], (WQhi[:, k, m * P:(m + 1) * P], WQlo[:, k, m * P:(m + 1) * P]),
                              (Shi[:, h, k, :], Slo[:, h, k, :]), k == 0, k == KD - 1)
                ins.then_inc(acc_full, 1)

            def project_out(n):
                s, t = divmod(n, 4)
                v = s // 2
                ps = begin_acc(("wo", s, t))
                pe.wait_ge(lo_done, last_item(f"wo{v}"))
                pe.wait_ge(otlo_done, n + 1)
                for c in range(CH):
                    ins = mm3(ps[:], (OThi[:, n % 4, c, :], OTlo[:, n % 4, c, :]),
                              (WOhi[:, v % 2, c, :], WOlo[:, v % 2, c, :]), c == 0, c == CH - 1)
                ins.then_inc(acc_full, 1)

            row_spectrum(0)
            pe.wait_ge(ctab_in, 16)
            pe.wait_ge(const_in, 16)
            correlate(0)
            correlate(1)
            row_spectrum(1)
            correlate(2)
            pe.wait_ge(lo_done, last_item("cx0"))
            keys("kc", 0, 0)
            correlate(3)
            keys("kc", 0, 1)
            turn_weights(0)
            correlate(4)
            keys("kc", 0, 2)
            turn_weights(1)
            correlate(5)
            pe.wait_ge(lo_done, last_item("wv"))
            values("vc", 0, 0)
            turn_weights(2)
            correlate(6)
            values("vc", 0, 1)
            turn_weights(3)
            correlate(7)
            values("vc", 0, 2)
            weight_spectrum(0)
            turn_weights(4)
            values("vc", 0, 3)
            turn_weights(5)
            turn_weights(6)
            invert(0)
            invert(1)
            invert(2)
            pe.wait_ge(lo_done, last_item("cx1"))
            keys("kc", 1, 0)
            turn_weights(7)
            invert(3)
            weight_spectrum(1)
            for t in range(TH):
                turn_rows(t)
            keys("kc", 1, 1)
            keys("kc", 1, 2)
            for t in range(TH):
                values("vc", 1, t)
            pe.wait_ge(x1lo_done, TH)
            keys("kx", 0, 0)
            invert(4)
            invert(5)
            keys("kx", 0, 1)
            invert(6)
            keys("kx", 0, 2)
            invert(7)
            for t in range(TH):
                values("vx", 0, t)
            queries(0, 0)
            turn_rows(4)
            turn_rows(5)
            queries(0, 1)
            turn_rows(6)
            turn_rows(7)
            queries(0, 2)
            pe.wait_ge(x1lo_done, NT)
            keys("kx", 1, 0)

            def score(n):
                s, i = divmod(n, 4)
                v, h = divmod(s, 2)
                if i == 0:
                    pe.wait_ge(q_moved[s % 2], 48 * (s // 2 + 1))
                if n == 0:
                    pe.wait_ge(k_moved, 16 * 3 * CH)
                    pe.wait_ge(prods, prods_count(1, 1))
                if n == 4:
                    pe.wait_ge(k_moved_last, 16 * CH)
                if n >= 2:
                    pe.wait_ge(exped, n - 1)
                for u in range(4):
                    bl = 2 * i + u // 2
                    b = 8 * h + bl
                    q = QC[0:HD, s % 2, bl, 2 * (u % 2):2 * (u % 2) + 2, :].rearrange("p a b -> p (a b)")
                    ins = pe.matmul(sc[n % 2][:, u * P:(u + 1) * P], q, KC[0:HD, :, v, b * S:(b + 1) * S],
                                    start=True, stop=True)
                ins.then_inc(scored, 1)

            def turn_probs(n):
                pe.wait_ge(p_normed, n + 1)
                if n >= 2:
                    pe.wait_ge(pt_read, n - 1)
                for u in range(4):
                    ins = pe.transpose(pt[n % 2][:, u * P:(u + 1) * P], PX[:, n % 2, u, :], ident)
                ins.then_inc(pt_ps, 1)

            def attend(n):
                s, i = divmod(n, 4)
                v, h = divmod(s, 2)
                pe.wait_ge(pt_read, n + 1)
                if n == 0:
                    pe.wait_ge(x1lo_done, NT)
                if n == 4:
                    pe.wait_ge(acc_act, evac_count(("vx", 1, TH - 1)))
                if n >= 2:
                    pe.wait_ge(ot_read, n - 1)
                for j in range(2):
                    b = 8 * h + 2 * i + j
                    ins = pe.matmul(pv[n % 2][0:HD, j * 256:(j + 1) * 256], VB[:, b, v * HD:(v + 1) * HD],
                                    PT[:, n % 2, j * 256:(j + 1) * 256], start=True, stop=True)
                ins.then_inc(pv_ps, 1)

            for it in range(NQ + 1):
                s, i = divmod(it, 4)
                wo = projected(it)
                queries_left = i >= 1 and s + 1 < NS
                if queries_left and i == CH:
                    queries(s + 1, i - 1)
                    queries_left = False
                if it < NQ:
                    score(it)
                if 1 <= it <= NQ:
                    turn_probs(it - 1)
                for kind, h, m in REST_AT.get(it, []):
                    if queries_left:
                        queries(s + 1, i - 1)
                        queries_left = False
                    (keys if kind == "kx" else values)(kind, h, m)
                if queries_left:
                    queries(s + 1, i - 1)
                elif wo:
                    project_out(wo.pop(0))
                if 1 <= it <= NQ:
                    attend(it - 1)
                for n in wo:
                    if it < NQ:
                        project_out(n)

            def turn_rows2(t):
                if t >= 2:
                    pe.wait_ge(x2lo_done, t - 1)
                    pe.wait_ge(xft_done, t - 1)
                pe.wait_ge(normed_rows, NT + t + 1)
                for k in range(KD):
                    ins = pe.transpose(pv[t % 2][:, k * P:(k + 1) * P], rows[:, t, k * P:(k + 1) * P], ident)
                ins.then_inc(x2_ps, 1)

            def lora_down(h):
                if h == 0:
                    pe.wait_ge(acc_dve, evac_count(("wo",) + divmod(NQ - 2, 4)))
                pe.wait_ge(x2lo_done, TH * (h + 1))
                for k in range(KD):
                    pe.matmul(acc[0][0:96, :], A13S[:, k, :], X2hi[:, k, :], start=k == 0, stop=False)
                    ins = pe.matmul(acc[0][0:96, :], A13S[:, k, :], X2lo[:, k, :], start=False, stop=k == KD - 1)
                ins.then_inc(ta_ps, 1)

            def gate_up(g):
                h, n = divmod(g, NF)
                c, q = divmod(n, 4)
                m = FW[c]
                if n == 0:
                    pe.wait_ge(xflo_done, TH * (h + 1))
                if g >= 2:
                    pe.wait_ge(h_done, g - 1)
                both = [(w * NW1 + q * FQP + c * P, ps) for w, ps in ((0, sc[g % 2]), (1, pt[g % 2]))]
                for o, ps in both:
                    mm3(ps[0:m, :], (W1hi[:, o:o + m], W1lo[:, o:o + m]), (XFhi[:, h, :], XFlo[:, h, :]), True, False)
                for o, ps in both:
                    if n == 0:
                        pe.wait_ge(talo_done, h + 1)
                    if h == 0:
                        pe.wait_ge(lo_done, index[("bb0", 0)] + 1 + (o + m - 1) // W)
                    ins = pe.matmul(ps[0:m, :], BS[0:96, o:o + m], TS[0:96, h, :], start=False, stop=True)
                ins.then_inc(gu_ps, 1)

            def lora2_down(g):
                h, n = divmod(g, NF)
                m = FW[n // 4]
                if g == 0:
                    pe.wait_ge(acc_dve, evac_count(("wo",) + divmod(NQ - 1, 4)))
                pe.wait_ge(hlo_done, g + 1)
                pe.matmul(acc[1 - h][0:96, :], A2S[0:m, n, :], HShi[0:m, g % 2, :], start=n == 0, stop=False)
                ins = pe.matmul(acc[1 - h][0:96, :], A2S[0:m, n, :], HSlo[0:m, g % 2, :], start=False, stop=n == NF - 1)
                ins.then_inc(a2_ps, 1)

            def down_chunks(t, chunks):
                h = t // TH
                cols = slice((t % TH) * P, (t % TH + 1) * P)
                for c in chunks:
                    if t % TH == 0:
                        pe.wait_ge(hflo_done, FC * h + c + 1)
                    m = FW[c]
                    mm3(down_bank(t)[:], (HFhi[0:m, h, c, cols], HFlo[0:m, h, c, cols]), (W2hi[0:m, c, :], W2lo[0:m, c, :]),
                        c == 0, False)

            def begin_down(t):
                if t % TH == 0:
                    pe.wait_ge(lo_done, last_item("w2"))
                if t < 2:
                    pe.wait_ge(x2lo_done, NT)
                    pe.wait_ge(xft_done, NT)
                elif t < TH + 2:
                    pe.wait_ge(w2_read, t - 1)
                else:
                    pe.wait_ge(silu_done, 2 * NF)
                down_chunks(t, range(FC - 1))

            def finish_down(t):
                h = t // TH
                cols = slice((t % TH) * P, (t % TH + 1) * P)
                down_chunks(t, [FC - 1])
                if t % TH == 0:
                    pe.wait_ge(t2lo_done, h + 1)
                pe.matmul(down_bank(t)[:], T2S[0:96, h, cols], B2S[0:96, :], start=False, stop=True).then_inc(w2_ps, 1)

            def down(t):
                begin_down(t)
                finish_down(t)

            pe.wait_ge(ot_read, NQ - 1)
            turn_rows2(0)
            pe.wait_ge(ot_read, NQ)
            turn_rows2(1)
            project_out(NQ - 2)
            turn_rows2(2)
            turn_rows2(3)
            project_out(NQ - 1)
            lora_down(0)
            for g in range(2 * NF + 2):
                if g < 2 * NF:
                    gate_up(g)
                if g == 2 * NF:
                    down(TH - 1)
                if g == 2 * NF + 1:
                    begin_down(TH)
                if g >= 2:
                    lora2_down(g - 2)
                if g in TURN_AT:
                    turn_rows2(TURN_AT[g])
                if g == LORA_AT:
                    lora_down(1)
                if g in DOWN_AT:
                    down(DOWN_AT[g])
            begin_down(TH + 1)
            finish_down(TH)
            finish_down(TH + 1)
            for t in range(TH + 2, NT):
                down(t)

        @block.scalar
        def _(_act):
            act = nc.scalar

            def hi(kind, first=0, end=None):
                for n in range(first, count[kind] if end is None else end):
                    i = index[(kind, n)]
                    _, src, dst, _ = items[i]
                    act.wait_ge(stage_in[i % 4], 16 * (i // 4 + 1))
                    act.activation(dst, stg[0:src.shape[0], i % 4, 0:src.shape[1]], ACT.Copy).then_inc(hi_done, 1)

            def x_hi(h, k):
                act.wait_ge(folded, 4 * h + k + 1)
                act.activation(Shi[:, h, k, :], FOLD[:, k, :], ACT.Copy).then_inc(xhi_done, 1)

            def copy_spectrum(h, m):
                act.wait_ge(dft_ps, 4 * h + m + 1)
                act.activation(X[:, m, h, :], dftb[m][:], ACT.Copy).then_inc(x_copied, 1)

            def square(h, m):
                act.wait_ge(dft_ps, 4 * h + m + 1)
                if h == 1:
                    act.wait_ge(corr_ps, TH)
                act.activation(SQ[:, m, :], dftb[m][:], ACT.Square).then_inc(squared, 1)

            def even_copy(t):
                act.wait_ge(corr_ps, t + 1)
                if t >= 2:
                    act.wait_ge(corr_built, t - 1)
                act.activation(TE[:, t % 2, 0:LAGS], tbank(("corr", t))[:, 0:LAGS], ACT.Copy).then_inc(even_copied, 1)

            def lag_exp(t):
                act.wait_ge(topped, t + 1)
                if t >= 1:
                    act.wait_ge(lag_diff, t)
                if t >= 2:
                    act.wait_ge(wf_done, t - 1)
                act.activation(E1[:, t % 2, :], CORR[:, t % 2, 0:D], ACT.Exp, bias=ngm[:, t % 2, :]).then_inc(lag_exps, 1)
                act.activation(E2[:], REP[:, t % 2, 0:D], ACT.Exp, bias=ngm[:, t % 2, :]).then_inc(lag_exps, 1)
                act.activation(es6[:, t % 2, :], T8[:, t % 2, 0:TOPK], ACT.Exp, bias=ngm[:, t % 2, :],
                               accum_out=ssum[:, t:t + 1]).then_inc(lag_exps, 1)

            def weights_hi(t):
                h = t // TH
                act.wait_ge(wt_ps, t + 1)
                act.activation(Shi[:, h, :, (t % TH) * P:(t % TH + 1) * P],
                               tbank(("wt", t))[:].rearrange("p (k r) -> p k r", k=KD), ACT.Copy).then_inc(wthi_done, 1)

            def product_hi(h, part):
                n = 2 * h + part + 1
                for j, done in ((1, ydiff), (0, ysum)):
                    act.wait_ge(done, n)
                    act.activation(Shi[:, h, 2 * part + j, :], SQ[:, 2 * j, :], ACT.Copy).then_inc(yhi_done, 1)

            def rows_hi(t):
                h = t // TH
                act.wait_ge(x1_ps, t + 1)
                act.activation(Shi[:, h, :, (t % TH) * P:(t % TH + 1) * P],
                               tbank(("x1", t))[:].rearrange("p (k r) -> p k r", k=KD), ACT.Copy).then_inc(x1hi_done, 1)

            def keys_out(kind, h, m):
                act.wait_ge(acc_full, gidx[(kind, h, m)] + 1)
                part = 1 if kind == "kc" else 0
                act.activation(KC[:, part, m, h * HR:(h + 1) * HR], acc_bank((kind, h, m))[:], ACT.Copy).then_inc(acc_act, 1)

            def values_out(kind, h, t):
                act.wait_ge(acc_full, gidx[(kind, h, t)] + 1)
                ps = acc_bank((kind, h, t))
                p0 = 64 if kind == "vc" else 0
                b = 2 * (h * TH + t)
                act.activation(VB[p0:p0 + 64, b, :], ps[0:64, 0:KV * HD], ACT.Copy).then_inc(val_half, 1)
                act.activation(VB[p0:p0 + 64, b + 1, :], ps[64:128, 0:KV * HD], ACT.Copy).then_inc(acc_act, 1)

            def queries_out(s, m):
                act.wait_ge(acc_full, gidx[("q", s, m)] + 1)
                if s >= 2:
                    act.wait_ge(scored, 4 * (s - 1))
                act.activation(QC[:, s % 2, :, m, :], acc_bank(("q", s, m))[:].rearrange("p (b r) -> p b r", r=S),
                               ACT.Copy).then_inc(acc_act, 1)

            x_hi(0, 0)
            hi("fwd", 0, 1)
            x_hi(0, 1)
            hi("fwd", 1)
            hi("wk", 0, 1)
            x_hi(0, 2)
            x_hi(0, 3)
            hi("wk", 1)
            square(0, 0)
            x_hi(1, 0)
            square(0, 1)
            x_hi(1, 1)
            square(0, 2)
            square(0, 3)
            copy_spectrum(0, 0)
            copy_spectrum(0, 1)
            copy_spectrum(0, 2)
            x_hi(1, 2)
            copy_spectrum(0, 3)
            x_hi(1, 3)
            hi("cx0")
            even_copy(0)
            even_copy(1)
            hi("wv")
            lag_exp(0)
            even_copy(2)
            for m in range(4):
                square(1, m)
            even_copy(3)
            lag_exp(1)
            keys_out("kc", 0, 0)
            lag_exp(2)
            weights_hi(0)
            even_copy(4)
            keys_out("kc", 0, 1)
            lag_exp(3)
            weights_hi(1)
            even_copy(5)
            keys_out("kc", 0, 2)
            lag_exp(4)
            values_out("vc", 0, 0)
            weights_hi(2)
            even_copy(6)
            lag_exp(5)
            copy_spectrum(1, 0)
            copy_spectrum(1, 1)
            values_out("vc", 0, 1)
            weights_hi(3)
            even_copy(7)
            copy_spectrum(1, 2)
            copy_spectrum(1, 3)
            hi("inv")
            values_out("vc", 0, 2)
            lag_exp(6)
            weights_hi(4)
            product_hi(0, 0)
            values_out("vc", 0, 3)
            weights_hi(5)
            hi("cx1")
            product_hi(0, 1)
            weights_hi(6)
            lag_exp(7)
            keys_out("kc", 1, 0)
            weights_hi(7)
            for t in range(TH):
                rows_hi(t)
            keys_out("kc", 1, 1)
            product_hi(1, 0)
            keys_out("kc", 1, 2)
            values_out("vc", 1, 0)
            product_hi(1, 1)
            for t in range(1, TH):
                values_out("vc", 1, t)
            act.wait_ge(prods, prods_count(1, 1))
            act.wait_ge(ylo_done, 4)
            act.wait_ge(ylo2_done, 4)
            act.wait_ge(wdft_ps, 8)
            hi("wq0")
            for m in range(CH):
                keys_out("kx", 0, m)
            for t in range(TH):
                values_out("vx", 0, t)
            queries_out(0, 0)
            rows_hi(4)
            rows_hi(5)
            queries_out(0, 1)
            rows_hi(6)
            rows_hi(7)
            queries_out(0, 2)
            keys_out("kx", 1, 0)
            hi("wo0")

            def exp_scores(n):
                act.wait_ge(max_ready, n + 1)
                if n >= 2:
                    act.wait_ge(pt_ps, n - 1)
                for u in range(4):
                    ins = act.activation(PX[:, n % 2, u, :], sc[n % 2][:, u * P:(u + 1) * P], ACT.Exp,
                                         bias=nb[:, n % 2, u:u + 1], scale=SCALE, accum_out=sm[:, n % 2, u:u + 1])
                ins.then_inc(exped, 1)

            def output_out(n):
                act.wait_ge(pv_ps, n + 1)
                if n >= 4:
                    act.wait_ge(otlo_done, n - 3)
                act.activation(OTF[0:HD, n % 4, :, :].rearrange("p g (b r) -> p b g r", r=S),
                               pv[n % 2][0:HD, :].rearrange("p (b g r) -> p b g r", g=G, r=S), ACT.Copy).then_inc(ot_read, 1)

            def output_hi(n):
                act.wait_ge(o_moved[n % 4], 48 * (n // 4 + 1))
                if n >= 4:
                    act.wait_ge(acc_full, gidx[("wo",) + divmod(n - 4, 4)] + 1)
                act.activation(OThi[:, n % 4], OTF[:, n % 4, 0:CH], ACT.Copy).then_inc(othi_done, 1)

            for it in range(NQ + 2):
                s, i = divmod(it, 4)
                if i == CH and s + 1 < NS:
                    queries_out(s + 1, i - 1)
                if it < NQ:
                    exp_scores(it)
                if it >= 2 and it != NQ + 1:
                    output_hi(it - 2)
                if 1 <= i < CH and s + 1 < NS:
                    queries_out(s + 1, i - 1)
                for kind, h, m in REST_AT.get(it, []):
                    (keys_out if kind == "kx" else values_out)(kind, h, m)
                if 1 <= it <= NQ:
                    output_out(it - 1)
                if i == 3 and s % 2 == 0 and s // 2 + 1 < KV:
                    act.wait_ge(acc_full, gidx[("q", s + 1, CH - 1)] + 1)
                    hi(f"wq{s // 2 + 1}")
                if i == 2 and s % 2 == 1 and s // 2 + 1 < KV:
                    v = s // 2 + 1
                    if v >= 2:
                        act.wait_ge(acc_full, gidx[("wo", 2 * (v - 2) + 1, TH - 1)] + 1)
                    hi(f"wo{v}")
                if it == 28:
                    act.wait_ge(acc_full, gidx[("q", NS - 1, CH - 1)] + 1)
                if it == 26:
                    act.wait_ge(acc_full, gidx[("wo", 2 * (KV - 2) + 1, TH - 1)] + 1)
                for kind in FFN_AT.get(it, ()):
                    hi(kind)
                if it == NQ - 1:
                    hi("bb0")

            def rows2_hi(t):
                act.wait_ge(x2_ps, t + 1)
                if t == TH:
                    act.wait_ge(ta_ps, 1)
                act.activation(X2hi[:, :, (t % TH) * P:(t % TH + 1) * P],
                               pv[t % 2][:].rearrange("p (k r) -> p k r", k=KD), ACT.Copy).then_inc(x2hi_done, 1)

            def fold_hi(t):
                act.wait_ge(xft_done, t + 1)
                act.activation(XFhi[:, t // TH, (t % TH) * P:(t % TH + 1) * P], XFt[:, t % 2, :], ACT.Copy).then_inc(xfhi_done, 1)

            def lora_out(h):
                act.wait_ge(ta_ps, h + 1)
                act.activation(TS[0:96, h, :], acc[0][0:96, :], ACT.Copy, scale=0.5).then_inc(tahi_done, 1)

            def lora2_out(h):
                act.wait_ge(a2_ps, NF * (h + 1))
                act.activation(T2S[0:96, h, :], acc[1 - h][0:96, :], ACT.Copy, scale=0.5).then_inc(t2hi_done, 1)

            rows2_hi(0)
            rows2_hi(1)
            output_hi(NQ - 1)
            fold_hi(0)
            rows2_hi(2)
            fold_hi(1)
            rows2_hi(3)
            fold_hi(2)
            fold_hi(3)
            hi("bb1")
            lora_out(0)
            for g in range(2 * NF + 1):
                if g < 2 * NF:
                    m = FW[(g % NF) // 4]
                    act.wait_ge(gu_ps, g + 1)
                    if g >= 2:
                        act.wait_ge(h_done, g - 1)
                    act.activation(SG[0:m, g % 2, :], sc[g % 2][0:m, :], ACT.Silu).then_inc(silu_done, 1)
                if g >= 1:
                    p = g - 1
                    m = FW[(p % NF) // 4]
                    act.wait_ge(h_done, p + 1)
                    if p >= 2:
                        act.wait_ge(a2_ps, p - 1)
                    act.activation(HShi[0:m, p % 2, :], Hb[0:m, p % 4, :], ACT.Copy).then_inc(hhi_done, 1)
                if g >= 4 and g % 4 == 1 or g == 2 * NF:
                    j = (g - 1) // 4 - (g != 2 * NF)
                    m = FW[j % FC]
                    act.wait_ge(fold_done, 4 * (j + 1))
                    act.activation(HFhi[0:m, j // FC, j % FC, :], HF[0:m, j % 2, :], ACT.Copy).then_inc(hfhi_done, 1)
                if g in TURN_AT:
                    rows2_hi(TURN_AT[g])
                    fold_hi(TURN_AT[g])
                if g == LORA_AT:
                    lora_out(1)
                if g == NF + 1:
                    lora2_out(0)
            lora2_out(1)
            for t in OUT_BY_ACT:
                h, j = divmod(t, TH)
                act.wait_ge(shifts, h + 1)
                act.activation(rows[:, t, :], rows[:, t, :], ACT.Identity, bias=shift[:, h, j:j + 1],
                               scale=(yo, y0)[h][:, j:j + 1]).then_inc(normed_act, 1)

        @block.gpsimd
        def _(_pool):
            pool = nc.gpsimd
            chain = [0]

            def link(ins):
                chain[0] += 1
                ins.then_inc(pch, 1)
                pool.wait_ge(pch, chain[0])

            def lo(kind, first=0, end=None):
                for n in range(first, count[kind] if end is None else end):
                    i = index[(kind, n)]
                    _, src, dhi, dlo = items[i]
                    pool.wait_ge(hi_done, i + 1)
                    raw = stg[:, i % 4, 0:src.shape[1]]
                    if dlo is not None:
                        pool.tensor_tensor(dlo, raw, dhi, ALU.subtract).then_inc(lo_done, 1)
                    elif kind in ("bb0", "bb1"):
                        pool.tensor_tensor(dhi[32:64], raw[32:64, :], dhi[32:64], ALU.subtract).then_inc(lo_done, 1)
                    else:
                        w = 4 if kind == "a13" else 2
                        d = dhi.rearrange("p (a c) -> p a c", c=32)[:, :, w:2 * w]
                        r = raw.rearrange("p (a c) -> p a c", c=32)[:, :, w:2 * w]
                        pool.tensor_tensor(d, r, d, ALU.subtract).then_inc(lo_done, 1)

            def lag_weights(t):
                pool.wait_ge(lag_exps, 3 * t + 2)
                e = E1[:, t % 2, :]
                pool.tensor_tensor(e, e, E2[:], ALU.subtract).then_inc(lag_diff, 1)
                pool.wait_ge(lag_diff, t + 1)
                if t >= 4:
                    pool.wait_ge(wt_ps, t - 3)
                half = D // 2
                pool.tensor_tensor(WF[:, t % 4, 0:half], e[:, 0:half], e[:, half:D], ALU.add).then_inc(pch, 1)
                chain[0] += 1
                pool.wait_ge(pch, chain[0])
                pool.tensor_tensor(WF[:, t % 4, half:D], e[:, 0:half], e[:, half:D], ALU.subtract).then_inc(wf_done, 1)

            def product_diff(h, part):
                n = 2 * h + part + 1
                pool.wait_ge(prods, prods_count(h, part) - 2)
                pool.tensor_tensor(SQ[:, 2, :], SQ[:, 2, :], SQ[:, 3, :], ALU.subtract).then_inc(ydiff, 1)
                pool.wait_ge(yhi_done, 2 * n - 1)
                pool.tensor_tensor(Slo[:, h, 2 * part + 1, :], SQ[:, 2, :], Shi[:, h, 2 * part + 1, :],
                                   ALU.subtract).then_inc(ylo2_done, 1)

            lo("fwd")
            lo("wk")
            pool.wait_ge(lo_done, last_item("cx0"))
            lo("wv")
            lag_weights(0)
            pool.wait_ge(xlo_done, 8)
            lag_weights(1)
            lag_weights(2)
            lag_weights(3)
            lag_weights(4)
            lag_weights(5)
            lo("inv")
            lag_weights(6)
            product_diff(0, 0)
            product_diff(0, 1)
            lo("cx1")
            lag_weights(7)
            product_diff(1, 0)
            product_diff(1, 1)
            lo("wq0")
            lo("wo0")

            def normalise(n):
                pool.wait_ge(recips, n + 1)
                pool.tensor_tensor(PX[:, n % 2], PX[:, n % 2], rc[:, n % 2, :].unsqueeze(2).to_broadcast([P, 4, P]),
                                   ALU.mult).then_inc(p_normed, 1)

            for it in range(NQ + 2):
                s, i = divmod(it, 4)
                if it < NQ:
                    normalise(it)
                if i == 3 and s % 2 == 0 and s // 2 + 1 < KV:
                    lo(f"wq{s // 2 + 1}", 0, 2)
                if i == 0 and s % 2 == 1 and s // 2 + 1 < KV:
                    lo(f"wq{s // 2 + 1}", 2)
                if i == 2 and s % 2 == 1 and s // 2 + 1 < KV:
                    lo(f"wo{s // 2 + 1}")
                for kind in FFN_AT.get(it, ()):
                    if kind not in LO_BY_DVE:
                        lo(kind)

            def fold_lo(t):
                pool.wait_ge(xfhi_done, t + 1)
                h, cols = t // TH, slice((t % TH) * P, (t % TH + 1) * P)
                pool.tensor_tensor(XFlo[:, h, cols], XFt[:, t % 2, :], XFhi[:, h, cols], ALU.subtract).then_inc(xflo_done, 1)

            pool.wait_ge(p_normed, NQ)
            pool.wait_ge(lo_done, last_item("b2"))
            lo("bb0")
            pool.wait_ge(lo_done, last_item("bb0"))
            for t in range(TH):
                fold_lo(t)
            pool.wait_ge(xflo_done, TH)
            lo("bb1")
            pool.wait_ge(lo_done, last_item("bb1"))
            for g in range(2 * NF):
                j, q = divmod(g, 4)
                m = FW[j % FC]
                if q >= 1:
                    pool.wait_ge(h_done, g + 1)
                    dst = HF[0:m, j % 2, :]
                    if q == 1 and j >= 2:
                        pool.wait_ge(hflo_done, j - 1)
                    pool.wait_ge(fold_done, g if q > 1 else g - 1)
                    prev = dst if q > 1 else Hb[0:m, (g - 1) % 4, :]
                    pool.tensor_tensor(dst, prev, Hb[0:m, g % 4, :], ALU.add).then_inc(fold_done, 1 if q > 1 else 2)
                if g in TURN_AT:
                    fold_lo(TURN_AT[g])

        @block.vector
        def _(_dve):
            dve = nc.vector
            chain = [0]

            def link(ins):
                chain[0] += 1
                ins.then_inc(dch, 1)
                dve.wait_ge(dch, chain[0])

            def mark(ins):
                chain[0] += 1
                ins.then_inc(dch, 1)

            def settle():
                dve.wait_ge(dch, chain[0])

            def lo(kind):
                for n in range(count[kind]):
                    i = index[(kind, n)]
                    _, src, dhi, dlo = items[i]
                    dve.wait_ge(hi_done, i + 1)
                    dve.wait_ge(lo_done, i)
                    if dlo is None:
                        dhi, dlo = dhi[32:64], dhi[32:64]
                        raw = stg[32:64, i % 4, 0:src.shape[1]]
                    else:
                        raw = stg[:, i % 4, 0:src.shape[1]]
                    dve.tensor_tensor(dlo, raw, dhi.bitcast(F32), ALU.subtract).then_inc(lo_done, 1)

            def fold_x(h, part):
                for j in range(2):
                    k = 2 * part + j
                    dve.wait_ge(x_in[h][j], 16)
                    if h == 1:
                        dve.wait_ge(xlo_done, k + 1)
                    dve.tensor_tensor(FOLD[:, k, :], X[:, j, h, :], X[:, j + 2, h, :],
                                      (ALU.add, ALU.subtract)[part]).then_inc(folded, 1)
                for j in range(2):
                    k = 2 * part + j
                    dve.wait_ge(xhi_done, 4 * h + k + 1)
                    dve.tensor_tensor(Slo[:, h, k, :], FOLD[:, k, :], Shi[:, h, k, :].bitcast(F32),
                                      ALU.subtract).then_inc(xlo_done, 1)

            def odd_power(h):
                dve.wait_ge(squared, 4 * (h + 1))
                dve.tensor_tensor(SQ[:, 2, :], SQ[:, 2, :], SQ[:, 3, :], ALU.add).then_inc(odd_sum, 1)

            def build_corr(t):
                ps = tbank(("corr", t))
                dve.wait_ge(even_copied, t + 1)
                if t >= 2:
                    dve.wait_ge(lag_exps, 3 * (t - 1))
                c = CORR[:, t % 2, :]
                te = TE[:, t % 2, :]
                n = LAGS - 1
                mark(dve.tensor_tensor(c[:, 0:LAGS], te[:, 0:LAGS], ps[:, 256:256 + LAGS], ALU.add))
                dve.tensor_tensor(c[:, 2 * n:n:-1], te[:, 0:n], ps[:, 256:256 + n], ALU.subtract).then_inc(corr_built, 1)
                dve.wait_ge(corr_built, t + 1)
                settle()
                link(dve.tensor_copy(c[:, D - 1:2 * n:-1], c[:, 1:2 * n]))
                link(dve.max(T8[:, t % 2, :], c[:, 0:D]))
                mark(dve.memset(T8[:, t % 2, TOPK:8], LOW))
                mark(dve.tensor_scalar(ngm[:, t % 2, :], T8[:, t % 2, 0:1], -1.0, None, ALU.mult))
                settle()
                dve.match_replace(REP[:, t % 2, 0:D + 2], T8[:, t % 2, :], c[:, 0:D + 2], LOW).then_inc(topped, 1)

            def weights_lo(t):
                h = t // TH
                cols = slice((t % TH) * P, (t % TH + 1) * P)
                dve.wait_ge(wthi_done, t + 1)
                dve.tensor_tensor(Slo[:, h, :, cols], tbank(("wt", t))[:].rearrange("p (k r) -> p k r", k=KD),
                                  Shi[:, h, :, cols].bitcast(F32), ALU.subtract).then_inc(wtlo_done, 1)

            def products(h, part):
                n = 2 * h + part
                re, im = dftb[2 * part], dftb[2 * part + 1]
                xr, xi = X[:, 2 * part, h, :], X[:, 2 * part + 1, h, :]
                dve.wait_ge(wdft_ps, 4 * h + 2 * part + 2)
                if n == 0:
                    dve.wait_ge(corr_ps, NT)
                    dve.wait_ge(const_in, 16)
                else:
                    dve.wait_ge(ylo2_done, n)
                dve.tensor_tensor(SQ[:, 2, :], re[:], xi, ALU.mult).then_inc(prods, 1)
                if part == 0:
                    dve.scalar_tensor_tensor(out=SQ[:, 3, :], in0=im[:], scalar=mask, in1=xr,
                                             op0=ALU.mult, op1=ALU.mult).then_inc(prods, 1)
                    dve.wait_ge(prods, 9 * h + 2)
                    dve.tensor_tensor(SQ[0:1, 2, :], im[0:1, :], xi[0:1, :], ALU.mult).then_inc(prods, 1)
                else:
                    dve.tensor_tensor(SQ[:, 3, :], im[:], xr, ALU.mult).then_inc(prods, 1)
                if n:
                    dve.wait_ge(ylo_done, n)
                dve.tensor_tensor(SQ[:, 0, :], re[:], xr, ALU.mult).then_inc(prods, 1)
                if part == 0:
                    dve.scalar_tensor_tensor(out=SQ[:, 1, :], in0=im[:], scalar=mask, in1=xi,
                                             op0=ALU.mult, op1=ALU.mult).then_inc(prods, 1)
                else:
                    dve.tensor_tensor(SQ[:, 1, :], im[:], xi, ALU.mult).then_inc(prods, 1)
                dve.wait_ge(prods, prods_count(h, part))
                dve.tensor_tensor(SQ[:, 0, :], SQ[:, 0, :], SQ[:, 1, :], ALU.add).then_inc(ysum, 1)

            def real_lo(h, part):
                n = 2 * h + part
                dve.wait_ge(yhi_done, 2 * n + 2)
                dve.tensor_tensor(Slo[:, h, 2 * part, :], SQ[:, 0, :], Shi[:, h, 2 * part, :].bitcast(F32),
                                  ALU.subtract).then_inc(ylo_done, 1)

            def stats(t):
                link(dve.bn_stats(st6[:, t, :], rows[:, t, :]))
                mark(dve.bn_aggr(mv[:, t, :], st6[:, t, :]))

            def combine(t):
                ps = tbank(("inv", t))
                half = D // 2
                dve.wait_ge(lag_exps, 3 * t + 3)
                link(dve.reciprocal(rsum[:, t:t + 1], ssum[:, t:t + 1]))
                mark(dve.tensor_scalar(nrs[:, t:t + 1], rsum[:, t:t + 1], -1.0, None, ALU.mult))
                dve.wait_ge(inv_ps, t + 1)
                both = rows[:, t, :].rearrange("p (a n) -> p a n", a=2)
                link(dve.scalar_tensor_tensor(out=both, in0=ps[:, 0:half].unsqueeze(1).to_broadcast([P, 2, half]),
                                              scalar=rsum[:, t:t + 1], in1=both, op0=ALU.mult, op1=ALU.add))
                mark(dve.scalar_tensor_tensor(out=rows[:, t, 0:half], in0=ps[:, half:D], scalar=rsum[:, t:t + 1],
                                              in1=rows[:, t, 0:half], op0=ALU.mult, op1=ALU.add))
                dve.scalar_tensor_tensor(out=rows[:, t, half:D], in0=ps[:, half:D], scalar=nrs[:, t:t + 1],
                                         in1=rows[:, t, half:D], op0=ALU.mult, op1=ALU.add).then_inc(combined, 1)
                dve.wait_ge(combined, t + 1)
                settle()
                stats(t)

            def rstd(n, y=y0):
                t0 = (n % 2) * TH
                settle()
                link(dve.tensor_scalar(ve[:], mv[:, t0:t0 + TH, 1], EPS, None, ALU.add))
                link(dve.tensor_scalar(y[:].bitcast(I32), ve[:].bitcast(I32), -0.5, RSQRT_BITS, ALU.mult, ALU.add))
                for _ in range(3):
                    link(dve.tensor_tensor(y1[:], y[:], y[:], ALU.mult))
                    link(dve.scalar_tensor_tensor(out=y2[:], in0=y1[:], scalar=-0.5, in1=ve[:], op0=ALU.mult, op1=ALU.mult))
                    link(dve.scalar_tensor_tensor(out=y[:], in0=y2[:], scalar=1.5, in1=y[:], op0=ALU.add, op1=ALU.mult))

            def out_shift(h, y):
                dve.scalar_tensor_tensor(out=shift[:, h, :], in0=mv[:, h * TH:(h + 1) * TH, 0], scalar=-1.0, in1=y[:],
                                         op0=ALU.mult, op1=ALU.mult).then_inc(shifts, 1)

            def normed(t):
                j = t % TH
                dve.tensor_scalar(rows[:, t, :], rows[:, t, :], mv[:, t, 0:1], y0[:, j:j + 1],
                                  ALU.subtract, ALU.mult).then_inc(normed_rows, 1)

            def layernorm(n):
                rstd(n)
                for j in range(TH):
                    normed((n % 2) * TH + j)

            def rows_lo(t):
                h = t // TH
                cols = slice((t % TH) * P, (t % TH + 1) * P)
                dve.wait_ge(x1hi_done, t + 1)
                dve.tensor_tensor(Slo[:, h, :, cols], tbank(("x1", t))[:].rearrange("p (k r) -> p k r", k=KD),
                                  Shi[:, h, :, cols].bitcast(F32), ALU.subtract).then_inc(x1lo_done, 1)

            for j in range(2):
                mark(dve.memset(CORR[:, j, D:D + 2], LOW))
            fold_x(0, 0)
            fold_x(0, 1)
            fold_x(1, 0)
            odd_power(0)
            fold_x(1, 1)
            lo("cx0")
            settle()
            for t in range(TH - 1):
                build_corr(t)
            odd_power(1)
            build_corr(TH - 1)
            weights_lo(0)
            build_corr(4)
            weights_lo(1)
            build_corr(5)
            weights_lo(2)
            build_corr(6)
            weights_lo(3)
            build_corr(7)
            products(0, 0)
            weights_lo(4)
            real_lo(0, 0)
            products(0, 1)
            weights_lo(5)
            real_lo(0, 1)
            dve.wait_ge(rows_in, 16)
            weights_lo(6)
            combine(0)
            combine(1)
            combine(2)
            weights_lo(7)
            combine(3)
            layernorm(0)
            for t in range(TH):
                rows_lo(t)
            products(1, 0)
            real_lo(1, 0)
            products(1, 1)
            real_lo(1, 1)
            for t in range(TH, NT):
                combine(t)
            layernorm(1)
            for t in range(TH, NT):
                rows_lo(t)

            def row_max(n):
                dve.wait_ge(scored, n + 1)
                if n >= 2:
                    dve.wait_ge(exped, n - 1)
                link(dve.tensor_reduce(mx[:, n % 2, :], sc[n % 2][:].rearrange("p (u k) -> p u k", u=4), AX.X, ALU.max))
                dve.tensor_scalar(nb[:, n % 2, :], mx[:, n % 2, :], -SCALE, None, ALU.mult).then_inc(max_ready, 1)

            def probs_out(n):
                dve.wait_ge(pt_ps, n + 1)
                if n >= 2:
                    dve.wait_ge(pv_ps, n - 1)
                dve.tensor_copy(PT[:, n % 2, :], pt[n % 2][:]).then_inc(pt_read, 1)

            def sum_recip(n):
                dve.wait_ge(exped, n + 1)
                if n >= 2:
                    dve.wait_ge(p_normed, n - 1)
                dve.reciprocal(rc[:, n % 2, :], sm[:, n % 2, :]).then_inc(recips, 1)

            def output_lo(n):
                dve.wait_ge(othi_done, n + 1)
                dve.tensor_tensor(OTlo[:, n % 4], OTF[:, n % 4, 0:CH], OThi[:, n % 4].bitcast(F32),
                                  ALU.subtract).then_inc(otlo_done, 1)

            def add_out(n):
                s, t = divmod(n, 4)
                h = s % 2
                dve.wait_ge(acc_full, gidx[("wo", s, t)] + 1)
                r = rows[:, h * TH + t, :]
                dve.tensor_tensor(r, acc_bank(("wo", s, t))[:], r, ALU.add).then_inc(acc_dve, 1)

            def measure(n):
                s, t = divmod(n, 4)
                dve.wait_ge(acc_dve, evac_count(("wo", s, t)))
                stats((s % 2) * TH + t)

            unmeasured = []
            for it in range(NQ):
                row_max(it)
                if 1 <= it:
                    probs_out(it - 1)
                for n in unmeasured:
                    measure(n)
                unmeasured = []
                sum_recip(it)
                if it >= 2:
                    output_lo(it - 2)
                for n in projected(it):
                    add_out(n)
                    if NQ - 8 <= n < NQ - 4:
                        unmeasured.append(n)
                if it == NQ - 2:
                    for n in unmeasured:
                        measure(n)
                    unmeasured = []
                    lo("b2")

            def rows2_lo(t):
                cols = slice((t % TH) * P, (t % TH + 1) * P)
                ps = pv[t % 2][:]
                dve.wait_ge(x2hi_done, t + 1)
                if t >= 2:
                    dve.wait_ge(xflo_done, t - 1)
                dve.tensor_reduce(XFt[:, t % 2, :], ps.rearrange("p (k r) -> p r k", k=KD), AX.X, ALU.add).then_inc(xft_done, 1)
                dve.tensor_tensor(X2lo[:, :, cols], ps.rearrange("p (k r) -> p k r", k=KD), X2hi[:, :, cols].bitcast(F32),
                                  ALU.subtract).then_inc(x2lo_done, 1)

            def add_down_rows(t):
                dve.wait_ge(w2_ps, t + 1)
                r = rows[:, t, :]
                dve.tensor_tensor(r, down_bank(t)[:], r, ALU.add).then_inc(w2_read, 1)

            def measure_down(t):
                dve.wait_ge(w2_read, t + 1)
                stats(t)

            def add_down(t):
                add_down_rows(t)
                measure_down(t)

            def lora_lo(h):
                dve.wait_ge(tahi_done, h + 1)
                dve.scalar_tensor_tensor(out=TS[64:96, h, :], in0=acc[0][64:96, :], scalar=0.5,
                                         in1=TS[64:96, h, :].bitcast(F32),
                                         op0=ALU.mult, op1=ALU.subtract).then_inc(talo_done, 1)

            def lora2_lo(h):
                dve.wait_ge(t2hi_done, h + 1)
                dve.scalar_tensor_tensor(out=T2S[64:96, h, :], in0=acc[1 - h][64:96, :], scalar=0.5,
                                         in1=T2S[64:96, h, :].bitcast(F32),
                                         op0=ALU.mult, op1=ALU.subtract).then_inc(t2lo_done, 1)

            probs_out(NQ - 1)
            rstd(2)
            normed(0)
            output_lo(NQ - 2)
            normed(1)
            normed(2)
            rows2_lo(0)
            rows2_lo(1)
            normed(3)
            add_out(NQ - 3)
            output_lo(NQ - 1)
            rows2_lo(2)
            add_out(NQ - 2)
            rows2_lo(3)
            for n in range(NQ - 4, NQ - 1):
                measure(n)
            add_out(NQ - 1)
            measure(NQ - 1)
            lora_lo(0)
            rstd(3)
            for g in range(2 * NF + 1):
                if g < 2 * NF:
                    m = FW[(g % NF) // 4]
                    dve.wait_ge(silu_done, g + 1)
                    if g >= 4:
                        dve.wait_ge(fold_done, g - 3)
                        dve.wait_ge(hlo_done, g - 3)
                    dve.tensor_tensor(Hb[0:m, g % 4, :], pt[g % 2][0:m, :], SG[0:m, g % 2, :], ALU.mult).then_inc(h_done, 1)
                if g >= 1:
                    p = g - 1
                    m = FW[(p % NF) // 4]
                    dve.wait_ge(hhi_done, p + 1)
                    dve.tensor_tensor(HSlo[0:m, p % 2, :], Hb[0:m, p % 4, :], HShi[0:m, p % 2, :].bitcast(F32),
                                      ALU.subtract).then_inc(hlo_done, 1)
                if g >= 4 and g % 4 == 1 or g == 2 * NF:
                    j = (g - 1) // 4 - (g != 2 * NF)
                    m = FW[j % FC]
                    if g == 2 * NF:
                        add_down_rows(TH - 1)
                    dve.wait_ge(hfhi_done, j + 1)
                    dve.tensor_tensor(HFlo[0:m, j // FC, j % FC, :], HF[0:m, j % 2, :],
                                      HFhi[0:m, j // FC, j % FC, :].bitcast(F32), ALU.subtract).then_inc(hflo_done, 1)
                if g in TURN_AT:
                    rows2_lo(TURN_AT[g])
                if g < TH:
                    normed(TH + g)
                if g == LORA_AT:
                    lora_lo(1)
                if g == NF + 1:
                    lora2_lo(0)
                if g in DOWN_AT:
                    add_down(DOWN_AT[g])
            measure_down(TH - 1)
            lora2_lo(1)
            rstd(4, yo)
            out_shift(0, yo)
            for t in range(TH, NT):
                add_down(t)
            rstd(5)
            out_shift(1, y0)
            for t in range(TH, NT):
                if t not in OUT_BY_ACT:
                    normed(t)


def _kernel_inputs(np_, inp):
    def t3(a):
        return np_.ascontiguousarray(a.T.reshape(-1, P, a.shape[0]).transpose(1, 0, 2))

    x = np_.asarray(inp["x"]).reshape(ROWS, D)
    c = np_.asarray(inp["ctx_4096"]).reshape(ROWS, D)
    order = np_.concatenate([np_.concatenate([np_.arange(HD) + HD * m, 3 * HD + 32 * m + np_.arange(32)]) for m in range(CH)])
    wq = np_.asarray(inp["L0_xattn_Wq"]).reshape(KV, G * HD, D)[:, order]
    wk = np_.asarray(inp["L0_xattn_Wk"])[order]
    wv = np_.asarray(inp["L0_xattn_Wv"])
    wo = np_.asarray(inp["L0_xattn_Wo"]).T.reshape(KV, G * HD, D)[:, order]
    d = {
        "xT": t3(x), "xN": np_.ascontiguousarray(x.reshape(NT, P, D).transpose(1, 0, 2)), "ctxT": t3(c),
        "wqT": np_.stack([t3(wq[v]) for v in range(KV)]), "wkT": t3(wk), "wvT": t3(wv),
        "woT": np_.stack([np_.ascontiguousarray(wo[v].reshape(CH, P, D).transpose(1, 0, 2)) for v in range(KV)]),
    }

    def hidden(a):
        o = np_.zeros((a.shape[1], 4, FQP), a.dtype)
        o[:, :, :FQ] = a.T.reshape(-1, 4, FQ)
        return o.reshape(a.shape[1], 4 * FQP)

    d["w1T"] = hidden(np_.asarray(inp["L0_ffn_w1q"]))
    d["w3T"] = hidden(np_.asarray(inp["L0_ffn_w3q"]))
    w2 = np_.asarray(inp["L0_ffn_w2q"])
    w2p = np_.zeros((FC * P, D), w2.dtype)
    w2p[:FQ] = w2.T
    d["w2T"] = np_.ascontiguousarray(w2p.reshape(FC, P, D).transpose(1, 0, 2))
    a1, a3, a2 = (np_.asarray(inp["L0_ffn_" + n]) for n in ("a1", "a3", "a2"))
    ap = np_.zeros((P, KD, 96), a1.dtype)
    for j in range(3):
        for r in range(2):
            ap[:, :, 32 * j + 4 * r:32 * j + 4 * r + 2] = t3(a1)
            ap[:, :, 32 * j + 4 * r + 2:32 * j + 4 * r + 4] = t3(a3)
    d["a13"] = ap
    h2 = hidden(a2.T).reshape(2, 4, FQP)
    a2p = np_.zeros((P, NF, 96), a2.dtype)
    for n in range(NF):
        cc, q = divmod(n, 4)
        part = h2[:, q, cc * P:cc * P + FW[cc]].T
        for j in range(3):
            for r in range(2):
                a2p[:FW[cc], n, 32 * j + 2 * r:32 * j + 2 * r + 2] = part
    d["a2"] = a2p
    b1, b3, bd = (np_.asarray(inp["L0_ffn_" + n]) for n in ("b1", "b3", "b2"))
    bp = np_.zeros((96, 2, 4 * FQP), b1.dtype)
    b2p = np_.zeros((96, D), bd.dtype)
    for j in range(3):
        for r in range(2):
            bp[32 * j + 4 * r:32 * j + 4 * r + 2, 0] = hidden(b1)
            bp[32 * j + 4 * r + 2:32 * j + 4 * r + 4, 1] = hidden(b3)
            b2p[32 * j + 2 * r:32 * j + 2 * r + 2] = bd.T
    d["bb"] = bp.reshape(96, 2 * 4 * FQP)
    d["b2"] = b2p
    d["fwd"], d["inv"], d["ctab"] = dft_tables()
    consts = np_.ones((P, P + 1), np_.float32)
    consts[:, :P] = np_.eye(P, dtype=np_.float32)
    consts[0, P] = 0.0
    d["consts"] = consts
    return d


def kernel(**inputs):
    import concourse.bacc as _bacc
    from concourse.bass_utils import run_bass_kernel_spmd as _run

    nc = _bacc.Bacc("TRN2", target_bir_lowering=False, num_devices=1)
    arrays, args = {}, []
    for name, a in _kernel_inputs(np, inputs).items():
        a = np.ascontiguousarray(a)
        arrays[f"in_{name}"] = a
        args.append(nc.dram_tensor(f"in_{name}", a.shape, mybir.dt.from_np(a.dtype), kind="ExternalInput").ap())
    args.append(nc.dram_tensor("out_rows", (ROWS, D), F32, kind="ExternalOutput").ap())
    decoder_layer(nc, *args)
    r = _run(nc, [arrays], core_ids=[0])
    return r.results[0]["out_rows"].reshape(B, S, D)
```
